# Optimizing a Trainium2 kernel written in Bass

```python
import numpy as np
import jax
import jax.numpy as jnp

def _softmax(x, axis=-1):
    return jax.nn.softmax(x, axis=axis)

def _gelu(x):
    return jax.nn.gelu(x, approximate=True)

def _silu(x):
    return jax.nn.silu(x)

def _sigmoid(x):
    return jax.nn.sigmoid(x)

def _layernorm(x, axis=-1, eps=1e-05):
    m = jnp.mean(x, axis=axis, keepdims=True)
    v = jnp.var(x, axis=axis, keepdims=True)
    return (x - m) / jnp.sqrt(v + eps)

def _scatter_add(tgt, idx, src, axis=0):
    return tgt.at[idx].add(src)

def _segment_sum(src, seg, n):
    return jax.ops.segment_sum(src, seg, n)
kernel_name = 'mk_adaln_d1_jaxref_r4_91c680'

def setup_inputs(seed: int=0):
    np.random.seed(seed)
    _w = jnp.asarray

    def _L0_attn_setup():
        import jax, jax.numpy as jnp
        import numpy as np
        B, T = (4, 512)
        D_MODEL = 256
        N_HEADS = 8
        HEAD_DIM = 64
        KV_LRANK = 64

        def _orthogonalize_per_head(w):
            chunks = w.reshape(N_HEADS, HEAD_DIM, D_MODEL)

            def ns(m):
                A = m @ m.T
                Bm = 1.5 * jnp.eye(HEAD_DIM, dtype=m.dtype) - 0.5 * A
                return Bm @ m
            return jax.vmap(ns)(chunks).reshape(w.shape)
        key = jax.random.key(seed)
        ks = jax.random.split(key, 6)

        def lin(k, out_dim, in_dim):
            bound = 1.0 / np.sqrt(in_dim)
            return jax.random.uniform(k, (out_dim, in_dim), jnp.float32, -bound, bound)
        Wq = _orthogonalize_per_head(lin(ks[0], N_HEADS * HEAD_DIM, D_MODEL))
        return {'x': jax.random.normal(ks[1], (B, T, D_MODEL), jnp.float32), 'Wq': Wq, 'Wkv_down': lin(ks[2], KV_LRANK, D_MODEL), 'Wk_up': lin(ks[3], N_HEADS * HEAD_DIM, KV_LRANK), 'Wv_up': lin(ks[4], N_HEADS * HEAD_DIM, KV_LRANK), 'Wo': lin(ks[5], D_MODEL, N_HEADS * HEAD_DIM)}
    _L0_attn_in = _L0_attn_setup()

    def _L0_ffn_setup():
        import math
        import jax, jax.numpy as jnp
        import numpy as np
        E = 8
        TOPK = 2
        CF = 1.25
        EPS = 1e-05
        NEG = -1e+30

        def _layer_norm(x, gamma, beta):
            mu = jnp.mean(x, axis=-1, keepdims=True)
            var = jnp.mean((x - mu) ** 2, axis=-1, keepdims=True)
            return (x - mu) * jax.lax.rsqrt(var + EPS) * gamma + beta
        key = jax.random.key(seed)
        ks = jax.random.split(key, 8)
        B, S, H, F = (4, 512, 256, 1024)
        hidden_states = jax.random.normal(ks[0], (B, S, H), jnp.float32)
        token_mask = jnp.ones((B, S), jnp.int32)
        Wr = jax.random.normal(ks[1], (H, E), jnp.float32) * 0.001
        br = jnp.zeros((E,), jnp.float32)
        W1 = jax.random.normal(ks[2], (E, H, F), jnp.float32) * (1.0 / np.sqrt(H))
        b1 = jax.random.normal(ks[3], (E, F), jnp.float32) * 0.01
        W2 = jax.random.normal(ks[4], (E, F, H), jnp.float32) * (1.0 / np.sqrt(F))
        b2 = jax.random.normal(ks[5], (E, H), jnp.float32) * 0.01
        gamma = jnp.ones((H,), jnp.float32)
        beta = jnp.zeros((H,), jnp.float32)
        return {'hidden_states': hidden_states, 'Wr': Wr, 'br': br, 'W1': W1, 'b1': b1, 'W2': W2, 'b2': b2, 'gamma': gamma, 'beta': beta, 'token_mask': token_mask}
    _L0_ffn_in = _L0_ffn_setup()
    _L0_c = _w((lambda *s: np.random.randn(*s).astype(np.float32) * 0.05)(16, 256))
    _L0_wmod = _w((lambda *s: np.random.randn(*s).astype(np.float32) * 0.05)(256, 6 * 256) * 256 ** (-0.5))
    _d = {'L0_attn_x': _L0_attn_in['x'], 'L0_attn_Wq': _L0_attn_in['Wq'], 'L0_attn_Wkv_down': _L0_attn_in['Wkv_down'], 'L0_attn_Wk_up': _L0_attn_in['Wk_up'], 'L0_attn_Wv_up': _L0_attn_in['Wv_up'], 'L0_attn_Wo': _L0_attn_in['Wo'], 'L0_ffn_Wr': _L0_ffn_in['Wr'], 'L0_ffn_br': _L0_ffn_in['br'], 'L0_ffn_W1': _L0_ffn_in['W1'], 'L0_ffn_b1': _L0_ffn_in['b1'], 'L0_ffn_W2': _L0_ffn_in['W2'], 'L0_ffn_b2': _L0_ffn_in['b2'], 'L0_ffn_gamma': _L0_ffn_in['gamma'], 'L0_ffn_beta': _L0_ffn_in['beta'], 'L0_ffn_token_mask': _L0_ffn_in['token_mask'], 'L0_c': _L0_c, 'L0_wmod': _L0_wmod}
    _x0 = _d['L0_attn_x']
    _d['L0_attn_x'] = jax.random.normal(jax.random.fold_in(jax.random.key(seed), 1), (16, 512, 256), dtype=_x0.dtype)
    del _x0
    return _d

def reference(L0_attn_x, L0_attn_Wq, L0_attn_Wkv_down, L0_attn_Wk_up, L0_attn_Wv_up, L0_attn_Wo, L0_ffn_Wr, L0_ffn_br, L0_ffn_W1, L0_ffn_b1, L0_ffn_W2, L0_ffn_b2, L0_ffn_gamma, L0_ffn_beta, L0_ffn_token_mask, L0_c, L0_wmod):

    def _L0_attn_ref(x, Wq, Wkv_down, Wk_up, Wv_up, Wo):
        import jax, jax.numpy as jnp
        import numpy as np
        B, T = (4, 512)
        D_MODEL = 256
        N_HEADS = 8
        HEAD_DIM = 64
        KV_LRANK = 64

        def _orthogonalize_per_head(w):
            chunks = w.reshape(N_HEADS, HEAD_DIM, D_MODEL)

            def ns(m):
                A = m @ m.T
                Bm = 1.5 * jnp.eye(HEAD_DIM, dtype=m.dtype) - 0.5 * A
                return Bm @ m
            return jax.vmap(ns)(chunks).reshape(w.shape)
        b, t, _ = x.shape
        q = (x @ Wq.T).reshape(b, t, N_HEADS, HEAD_DIM)
        kv_latent = x @ Wkv_down.T
        k = (kv_latent @ Wk_up.T).reshape(b, t, N_HEADS, HEAD_DIM)
        v = (kv_latent @ Wv_up.T).reshape(b, t, N_HEADS, HEAD_DIM)
        scale = HEAD_DIM ** (-0.5)
        scores = jnp.einsum('bqhd,bkhd->bhqk', q, k) * scale
        attn = jax.nn.softmax(scores, axis=-1)
        out = jnp.einsum('bhqk,bkhd->bqhd', attn, v)
        out = out.reshape(b, t, N_HEADS * HEAD_DIM)
        return out @ Wo.T

    def _L0_ffn_ref(hidden_states, Wr, br, W1, b1, W2, b2, gamma, beta, token_mask):
        import math
        import jax, jax.numpy as jnp
        import numpy as np
        E = 8
        TOPK = 2
        CF = 1.25
        EPS = 1e-05
        NEG = -1e+30

        def _layer_norm(x, gamma, beta):
            mu = jnp.mean(x, axis=-1, keepdims=True)
            var = jnp.mean((x - mu) ** 2, axis=-1, keepdims=True)
            return (x - mu) * jax.lax.rsqrt(var + EPS) * gamma + beta
        B, S, H = hidden_states.shape
        x = hidden_states.reshape(-1, H)
        N = x.shape[0]
        logits = x @ Wr + br
        top_vals, top_idx = jax.lax.top_k(logits, TOPK)
        w = jax.nn.softmax(top_vals, axis=-1)
        flat_idx = top_idx.reshape(-1)
        flat_tok = jnp.repeat(jnp.arange(N), TOPK)
        w_flat = w.reshape(-1)
        cap = max(int(math.ceil(N / E * CF)), 1)
        key_mat = jnp.where(flat_idx[None, :] == jnp.arange(E)[:, None], w_flat[None, :], NEG)
        kv, ki = jax.lax.top_k(key_mat, cap)
        valid = kv > NEG / 2
        tok = flat_tok[ki]
        gate = jnp.where(valid, w_flat[ki], 0.0)
        xe = x[tok]
        h1 = jnp.einsum('ech,ehf->ecf', xe, W1) + b1[:, None, :]
        h1 = jax.nn.gelu(h1, approximate=False)
        y = jnp.einsum('ecf,efh->ech', h1, W2) + b2[:, None, :]
        out = jnp.zeros_like(x).at[tok.reshape(-1)].add((y * gate[..., None]).reshape(-1, H))
        out = out.reshape(B, S, H) + hidden_states
        return _layer_norm(out, gamma, beta)
    x = L0_attn_x
    mod = (_silu(L0_c) @ L0_wmod).reshape(L0_c.shape[0], 6, 1, -1)
    sa, ca, ga, sb, cb, gb = (mod[:, 0], mod[:, 1], mod[:, 2], mod[:, 3], mod[:, 4], mod[:, 5])
    ga = (2 * (ga >= 0) - 1) * jnp.maximum(jnp.abs(ga), 0.25)
    gb = (2 * (gb >= 0) - 1) * jnp.maximum(jnp.abs(gb), 0.25)
    h = _layernorm(x, axis=-1) * (1 + ca) + sa
    x = x + ga * _L0_attn_ref(h, L0_attn_Wq, L0_attn_Wkv_down, L0_attn_Wk_up, L0_attn_Wv_up, L0_attn_Wo)
    h = _layernorm(x, axis=-1) * (1 + cb) + sb
    x = x + gb * _L0_ffn_ref(h, L0_ffn_Wr, L0_ffn_br, L0_ffn_W1, L0_ffn_b1, L0_ffn_W2, L0_ffn_b2, L0_ffn_gamma, L0_ffn_beta, L0_ffn_token_mask)
    return x

_drawn_inputs = setup_inputs


def setup_inputs(seed=0):
    import zlib

    import numpy as np

    out = dict(_drawn_inputs(seed))
    spreads = {'L0_ffn_br': (0.0, 0.1), 'L0_ffn_gamma': (1.0, 0.2), 'L0_ffn_beta': (0.0, 0.1)}
    factors = {}
    for name, (base, spread) in spreads.items():
        noise = np.random.default_rng([zlib.crc32(name.encode()), seed]).standard_normal(out[name].shape)
        drawn = base * np.exp(spread * noise) if base else spread * noise
        out[name] = jnp.asarray(drawn.astype(out[name].dtype))
    for name, factor in factors.items():
        out[name] = (out[name] * factor).astype(out[name].dtype)
    return out
```

```python
from contextlib import ExitStack

import concourse.bass as bass
from concourse import mybir

F32, F32R = mybir.dt.float32, mybir.dt.float32r
U32, I32 = mybir.dt.uint32, mybir.dt.int32
ALU, ACT, AX = mybir.AluOpType, mybir.ActivationFunctionType, mybir.AxisListType

P = 128
NB, T, D = 16, 512, 256
H, R = 8, 64
KC = D // P
TC = T // P
NT = NB * T
NCH = NT // P
E, F = 8, 1024
CAP = -(-NT * 5 // (E * 4))
BLK = 256
EPS = 1e-5
UNITS = H * TC
RSQRT_SEED = 0x5F3759DF


class Stream:

    def __init__(self, sem, per, step=1):
        self.sem, self.per, self.step = sem, per, step

    def done(self, ins):
        ins.then_inc(self.sem, self.step)

    def value(self, b, k):
        value = b * (self.per * self.step) + (k + 1) * self.step
        return max(value, 0) if isinstance(value, int) else value

    def wait(self, eng, b, k):
        value = self.value(b, k)
        if not isinstance(value, int) or value > 0:
            eng.wait_ge(self.sem, value)


def snap(eng, x):
    return x if isinstance(x, int) else eng.snap(x)


class PairStream:

    def __init__(self, sem, parity):
        self.sem, self.parity = sem, parity

    def done(self, ins):
        ins.then_inc(self.sem, 16)

    def wait(self, eng, b):
        eng.wait_ge(self.sem, b * 8 + (16 - 8 * self.parity))


class Chain:

    def __init__(self, eng, sem):
        self.eng, self.sem, self.n = eng, sem, 0

    def __call__(self, ins):
        ins.then_inc(self.sem, 1)
        self.n += 1
        self.eng.wait_ge(self.sem, self.n)


def hi_lo_matmul(eng, out, lhs, rhs, first=True, last=True):
    eng.matmul(out, lhs[0], rhs[0], start=first, stop=False)
    eng.matmul(out, lhs[0], rhs[1], start=False, stop=False)
    return eng.matmul(out, lhs[1], rhs[0], start=False, stop=last)


def rsqrt_and_shift(dve, link, mv, v, y, t, nmr):
    link(dve.tensor_scalar(v, mv[:, :, 1], EPS, None, ALU.add))
    link(dve.tensor_scalar(t.bitcast(U32), v.bitcast(U32), 1, None, ALU.logical_shift_right))
    link(dve.tensor_scalar(y.bitcast(U32), t.bitcast(U32), -1.0, float(RSQRT_SEED), ALU.mult, ALU.add))
    for _ in range(3):
        link(dve.tensor_tensor(t, y, y, ALU.mult))
        link(dve.scalar_tensor_tensor(out=t, in0=t, scalar=-0.5, in1=v, op0=ALU.mult, op1=ALU.mult))
        link(dve.scalar_tensor_tensor(out=y, in0=t, scalar=1.5, in1=y, op0=ALU.add, op1=ALU.mult))
    link(dve.scalar_tensor_tensor(out=nmr, in0=mv[:, :, 0], scalar=-1.0, in1=y, op0=ALU.mult, op1=ALU.mult))


def build_program(nc, ap, out):
    top = ExitStack()
    with top:
        def sb(name, shape, dt=F32, ctx=top):
            return ctx.enter_context(nc.sbuf_tensor(name, shape, dt))

        def sem(name, ctx=top):
            return ctx.enter_context(nc.semaphore(name))

        PS = top.enter_context(nc.psum_tensor("PS", [P, 8, 512], F32))
        h2_dram = nc.dram_tensor("h2_rows", [NT + P, D], F32).ap()
        acc_dram = nc.dram_tensor("acc_rows", [NT + P, D], F32).ap()
        mod_dram = nc.dram_tensor("mod_rows", [NB, 5, D], F32).ap()
        ktab_dram = nc.dram_tensor("key_rows", [NT + P, E], F32).ap()
        m = dict(ktab_dram=ktab_dram, PS=PS, h2_dram=h2_dram, acc_dram=acc_dram, mod_dram=mod_dram)
        m["X1"] = sb("X1", [P, NCH, D])
        m["IDENT"] = sb("IDENT", [P, P])
        m["LOGITS"] = sb("LOGITS", [P, NCH, E])
        with ExitStack() as attn:
            def sba(name, shape, dt=F32):
                return sb(name, shape, dt, attn)
            for k, shape, dt in (
                    ("AH", [P, KC, H * R], F32R), ("AL", [P, KC, H * R], F32R),
                    ("DH", [P, KC, 2 * R], F32R), ("DL", [P, KC, 2 * R], F32R),
                    ("GH", [P, H // 2, D], F32R), ("GL", [P, H // 2, D], F32R),
                    ("WR", [P, KC, E], F32), ("BR", [P, E], F32),
                    ("SA", [P, KC, NB], F32), ("CA1", [P, KC, NB], F32)):
                m[k] = sba(k, shape, dt)
            setup(nc, ap, m, sem)
            attention(nc, ap, m, sem, sba)
        m["IDX"] = sb("IDX", [P, E * CAP // P], U32)
        m["INFO"] = sb("INFO", [1, 4 * E], I32)
        for phase in (route, experts):
            with ExitStack() as tiles:
                phase(nc, ap, m, sem, lambda name, shape, dt=F32: sb(name, shape, dt, tiles))
        with ExitStack() as tiles:
            last_norm(nc, out, m, sem, lambda name, shape, dt=F32: sb(name, shape, dt, tiles))


def setup(nc, ap, m, sem):
    PS, IDENT = m["PS"], m["IDENT"]
    with ExitStack() as ctx:
        def sb(name, shape, dt=F32):
            return ctx.enter_context(nc.sbuf_tensor(name, shape, dt))

        C = sb("C", [NB, D]); SG = sb("SG", [NB, D]); ST = sb("STc", [P, KC, NB])
        WM = sb("WM", [P, KC, 6 * D])
        WQ = sb("WQ", [R, H, D]); WK = sb("WK", [R, H, R]); WV = sb("WV", [R, H, R])
        WO = sb("WO", [P, KC, H * R]); WOT = sb("WOT", [R, H, D]); WD = sb("WD", [R, D])
        GB = sb("GBs", [NB, 2, D])
        MR = sb("MR", [NB, 5, D])
        MA = sb("MA", [NB, 2, D]); ZERO = sb("ZERO", [P, D])
        s_in, s_w, s_id, s_out = (sem(x) for x in ("s_in", "s_w", "s_id", "s_setout"))
        s_pe, s_act, s_dve, s_mr = (sem(x) for x in ("s_setpe", "s_setact", "s_setdve", "s_mr"))
        MODS_DONE, AL_DONE = 13, 17
        PE_SILU_T, PE_MODT, PE_WDT, PE_A, PE_WOT, PE_G = 1, 3, 4, 5, 6, 7
        silu_ps = PS[:, 0, 0:KC * NB].rearrange("p (k b) -> p k b", k=KC)
        modt_ps = PS[:, 1, 0:4 * NB].rearrange("p (j b) -> p j b", j=4)
        wdt_ps = PS[:, 2, 0:KC * R].rearrange("p (k r) -> p k r", k=KC)
        with nc.Block() as block:
            @block.sync
            def _(sp):
                sp.dma_start(C[:, :], ap["L0_c"]).then_inc(s_in, 16)
                sp.dma_start(WM[:, :, :], ap["L0_wmod"].rearrange("(k p) n -> p k n", p=P)).then_inc(s_in, 16)
                for j, name in enumerate(("L0_ffn_gamma", "L0_ffn_beta")):
                    sp.dma_start(GB[:, j, :], ap[name].partition_broadcast(NB)).then_inc(s_in, 16)
                sp.dma_start(WD[:, :], ap["L0_attn_Wkv_down"]).then_inc(s_w, 16)
                sp.dma_start(WQ[:, :, :], ap["L0_attn_Wq"].rearrange("(h d) n -> d h n", h=H)).then_inc(s_w, 16)
                sp.dma_start(WK[:, :, :], ap["L0_attn_Wk_up"].rearrange("(h d) n -> d h n", h=H)).then_inc(s_w, 16)
                sp.dma_start(WV[:, :, :], ap["L0_attn_Wv_up"].rearrange("(h d) n -> d h n", h=H)).then_inc(s_w, 16)
                sp.dma_start(WO[:, :, :], ap["L0_attn_Wo"].rearrange("(k p) n -> p k n", p=P)).then_inc(s_w, 16)
                sp.dma_start(m["WR"][:, :, :], ap["L0_ffn_Wr"].rearrange("(k p) n -> p k n", p=P)).then_inc(s_w, 16)
                sp.dma_start(m["BR"][:, :], ap["L0_ffn_br"].partition_broadcast(P)).then_inc(s_w, 16)
                sp.wait_ge(s_mr, 1)
                sp.dma_start(m["mod_dram"], MR[:, :, :]).then_inc(s_out, 16)
                sp.wait_ge(s_id, 3)
                sp.dma_start(m["h2_dram"][NT:NT + P, :], ZERO[:, :]).then_inc(s_out, 16)
                sp.dma_start(m["acc_dram"][NT:NT + P, :], ZERO[:, :]).then_inc(s_out, 16)
                sp.wait_ge(s_out, 48)
                sp.wait_ge(s_w, 16 * 7)

            @block.gpsimd
            def _(pool):
                pool.memset(IDENT[:, :], 0.0).then_inc(s_id, 1)
                pool.wait_ge(s_id, 1)
                pool.affine_select(out=IDENT[:, :], in_=IDENT[:, :], compare_op=ALU.not_equal, fill=1.0, base=0,
                                   pattern=[[-1, P]], channel_multiplier=1).then_inc(s_id, 1)
                pool.memset(ZERO[:, :], 0.0).then_inc(s_id, 1)

            @block.scalar
            def _(act):
                act.wait_ge(s_in, 64)
                act.activation(SG[:, :], C[:, :], ACT.Silu).then_inc(s_act, 1)
                act.wait_ge(s_pe, PE_WDT)
                for j in range(2):
                    act.activation(m["DH"][:, :, j * R:(j + 1) * R], wdt_ps, ACT.Copy).then_inc(s_act, 1)
                act.wait_ge(s_pe, PE_A)
                for k in range(KC):
                    act.activation(m["AH"][:, k, :], PS[:, 3 + k, :], ACT.Copy, scale=float(R) ** -0.5).then_inc(s_act, 1)
                act.wait_ge(s_pe, PE_WOT)
                for j in range(4):
                    act.activation(WOT[:, 2 * j:2 * j + 2, :], PS[0:R, 4 + j, :].rearrange("p (h n) -> p h n", h=2),
                                   ACT.Copy).then_inc(s_act, 1)
                act.wait_ge(s_pe, PE_G)
                for j in range(4):
                    for odd in range(2):
                        act.activation(m["GH"][odd * R:(odd + 1) * R, j, :], PS[0:R, j, odd * D:(odd + 1) * D],
                                       ACT.Copy).then_inc(s_act, 1)
            SILU, DH_DONE, AH_DONE, WOT_DONE, GH_DONE = 1, 3, 5, 9, 17

            @block.tensor
            def _(pe):
                pe.wait_ge(s_id, 2)
                pe.wait_ge(s_act, SILU)
                for k in range(KC):
                    last = pe.transpose(silu_ps[:, k, :], SG[:, k * P:(k + 1) * P], IDENT[0:NB, 0:NB])
                last.then_inc(s_pe, 1)
                pe.wait_ge(s_dve, 1)
                for j in range(3):
                    for k in range(KC):
                        last = pe.matmul(PS[0:NB, 5 + j, :], ST[:, k, :], WM[:, k, j * 512:(j + 1) * 512],
                                         start=(k == 0), stop=(k == KC - 1))
                last.then_inc(s_pe, 1)
                for j in range(4):
                    for k in range(KC):
                        last = pe.matmul(modt_ps[:, j, :], WM[:, k, j * P:(j + 1) * P], ST[:, k, :],
                                         start=(k == 0), stop=(k == KC - 1))
                last.then_inc(s_pe, 1)
                pe.wait_ge(s_w, 16 * 7)
                for k in range(KC):
                    last = pe.transpose(wdt_ps[:, k, :], WD[:, k * P:(k + 1) * P], IDENT[0:R, 0:R])
                last.then_inc(s_pe, 1)
                for k in range(KC):
                    for h in range(H):
                        last = pe.matmul(PS[:, 3 + k, h * R:(h + 1) * R], WQ[:, h, k * P:(k + 1) * P], WK[:, h, :],
                                         start=True, stop=True)
                last.then_inc(s_pe, 1)
                pe.wait_ge(s_dve, MODS_DONE)
                pe.wait_ge(s_act, AH_DONE)
                pe.wait_ge(s_dve, AL_DONE)
                for h in range(H):
                    for k in range(KC):
                        last = pe.transpose(PS[0:R, 4 + h // 2, (h % 2) * D + k * P:(h % 2) * D + (k + 1) * P],
                                            WO[:, k, h * R:(h + 1) * R], IDENT[:, :])
                last.then_inc(s_pe, 1)
                pe.wait_ge(s_act, WOT_DONE)
                for h in range(H):
                    last = pe.matmul(PS[0:R, h // 2, (h % 2) * D:(h % 2 + 1) * D], WV[:, h, :], WOT[:, h, :],
                                     start=True, stop=True)
                last.then_inc(s_pe, 1)
            @block.vector
            def _(dve):
                chain = Chain(dve, s_dve)
                dve.wait_ge(s_pe, PE_SILU_T)
                chain(dve.tensor_copy(ST[:, :, :], silu_ps))
                dve.wait_ge(s_pe, PE_MODT)
                chain(dve.tensor_copy(m["SA"][:, :, :], modt_ps[:, 0:2, :]))
                chain(dve.tensor_scalar(m["CA1"][:, :, :], modt_ps[:, 2:4, :], 1.0, None, ALU.add))
                for j, src in enumerate((PS[0:NB, 6, 0:D], PS[0:NB, 7, D:2 * D])):
                    sign, g = MA[:, j, :], MR[:, 4 * j, :]
                    chain(dve.tensor_scalar(sign, src, 0.0, 2.0, ALU.is_ge, ALU.mult))
                    chain(dve.tensor_scalar(sign, sign, -1.0, None, ALU.add))
                    chain(dve.tensor_tensor(g, src, sign, ALU.mult))
                    chain(dve.scalar_tensor_tensor(out=g, in0=g, scalar=0.25, in1=sign, op0=ALU.max, op1=ALU.mult))
                chain(dve.tensor_scalar(MR[:, 1, :], PS[0:NB, 7, 0:D], 1.0, None, ALU.add))
                chain(dve.tensor_copy(MR[:, 2, :], PS[0:NB, 6, D:2 * D]))
                dve.wait_ge(s_act, DH_DONE)
                for j in range(2):
                    chain(dve.tensor_tensor(m["DL"][:, :, j * R:(j + 1) * R], wdt_ps,
                                            m["DH"][:, :, j * R:(j + 1) * R].bitcast(F32), ALU.subtract))
                dve.wait_ge(s_act, AH_DONE)
                for k in range(KC):
                    chain(dve.scalar_tensor_tensor(out=m["AL"][:, k, :], in0=PS[:, 3 + k, :], scalar=float(R) ** -0.5,
                                                   in1=m["AH"][:, k, :].bitcast(F32), op0=ALU.mult,
                                                   op1=ALU.subtract))
                chain(dve.tensor_tensor(MR[:, 3, :], MR[:, 4, :], GB[:, 1, :], ALU.mult))
                dve.tensor_tensor(MR[:, 4, :], MR[:, 4, :], GB[:, 0, :], ALU.mult).then_inc(s_mr, 1)
                dve.wait_ge(s_act, GH_DONE)
                for j in range(4):
                    for odd in range(2):
                        chain(dve.tensor_tensor(m["GL"][odd * R:(odd + 1) * R, j, :], PS[0:R, j, odd * D:(odd + 1) * D],
                                                m["GH"][odd * R:(odd + 1) * R, j, :].bitcast(F32), ALU.subtract))


def attention(nc, ap, m, sem, sb):
    PS, IDENT, X1, LOGITS = m["PS"], m["IDENT"], m["X1"], m["LOGITS"]
    AH, AL, DH, DL, GH, GL, WR, BR = (m[k] for k in ("AH", "AL", "DH", "DL", "GH", "GL", "WR", "BR"))
    x_rows = ap["L0_attn_x"].rearrange("b (c p) n -> p (b c) n", p=P)
    NHI, NLO = sb("NHI", [P, 2, KC, T], F32R), sb("NLO", [P, 2, KC, T], F32R)
    K1, K2 = sb("K1", [P, 2, T], F32R), sb("K2", [P, 2, T], F32R)
    V1, V2 = sb("V1", [P, 2, TC, 2 * R], F32R), sb("V2", [P, 2, TC, 2 * R], F32R)
    MODB = sb("MODB", [P, 2, 4, D])
    Q1, Q2 = sb("Q1", [P, 4, T], F32R), sb("Q2", [P, 4, T], F32R)
    NMAX, MROW = sb("NMAX", [P, 2, TC]), sb("MROW", [TC, 2, P], F32R)
    PF, PH, PL = sb("PF", [P, 2, T]), sb("PH", [P, 4, T], F32R), sb("PL", [P, 4, T], F32R)
    DENT, RDEN, RECT = sb("DENT", [R, T]), sb("RDEN", [R, T // 32]), sb("RECT", [R, T])
    XF = sb("XF", [P, 2, T])
    XH, XL = sb("XH", [P, H // 2, T], F32R), sb("XL", [P, H // 2, T], F32R)
    XN1, NF, LTF = sb("XN1", [P, TC, D]), sb("NF", [P, KC, T]), sb("LTF", [P, T])
    H2, H2T = sb("H2", [P, TC, D]), sb("H2T", [P, TC, KC, P])
    YT, GATE = sb("YT", [P, 2, D]), sb("GATE", [P, 16])
    norm = [dict(s6=sb(f"s6_{j}", [P, TC, 6]), mv=sb(f"mv_{j}", [P, TC, 2]), v=sb(f"v_{j}", [P, TC]),
                 y=sb(f"y_{j}", [P, TC]), t=sb(f"t_{j}", [P, TC]), nmr=sb(f"nmr_{j}", [P, TC])) for j in range(2)]

    def S(name, per, step=1):
        return Stream(sem(name), per, step)

    s_st, s_mx, s_pv = S("st", UNITS), S("mx", UNITS), S("pv", UNITS)
    s_mt, s_q, s_proj, s_n1t, s_lat, s_vt, s_h2t, s_lg = (
        S("mt", H), S("q", 4), S("proj", TC), S("n1t", KC), S("lat", 1), S("vt", 1), S("h2t", TC), S("lg", 2))
    s_exp, s_qhi, s_latc, s_vhi, s_nf = S("exp", 2 * UNITS), S("qhi", 16), S("latc", 3), S("vhi", 1), S("nf", KC)
    s_xn1, s_xn2, s_h2c, s_xhi = S("xn1", TC), S("xn2", TC), S("h2c", TC), S("xhi", H // 2)
    s_mred, s_mrow, s_x, s_qlo, s_nhl, s_klo, s_vlo = (
        S("mred", UNITS), S("mrow", H), S("x", 4 * H), S("qlo", 8), S("nhl", 2 * KC), S("klo", 1), S("vlo", 1))
    s_y, s_x1, s_lgc, s_xlo = S("y", TC), S("x1", TC), S("lgc", 2), S("xlo", H // 2)
    NORM_OPS = 2 * TC + 13
    s_norm = [S("norm1", NORM_OPS), S("norm2", NORM_OPS)]
    s_plo, s_hmul, s_hadd, s_gbb = S("plo", UNITS), S("hmul", TC), S("hadd", TC), S("gbb", TC)
    s_xin = [PairStream(sem(f"xin{j}"), j) for j in range(2)]
    s_modin = [PairStream(sem(f"modin{j}"), j) for j in range(2)]
    s_mdma, s_h2out = S("mdma", H, 16), S("h2out", 2, 16)
    s_const = sem("s_attn_const")

    def st_bank(n):
        return PS[:, n % 2, :]

    def mx_bank(n):
        return PS[:, 2 + n % 2, :]

    def pv_bank(h):
        return PS[:, 4 + h % 2, :]

    JOBS = {1: [("mrow", 1, 0)], 5: [("mrow", 2, 0), ("proj", 1, -1)], 9: [("mrow", 3, 0)],
            13: [("mrow", 4, 0), ("lat", 0, 1)], 17: [("mrow", 5, 0), ("h2t", 1, -1)],
            21: [("mrow", 6, 0), ("h2t", 3, -1)], 25: [("mrow", 7, 0)], 29: [("mrow", 0, 1)],
            4: [("proj", 0, -1)], 7: [("proj", 2, -1)], 8: [("proj", 3, -1)],
            6: [("q", 2, 0)], 14: [("q", 3, 0)], 22: [("q", 0, 1)], 30: [("q", 1, 1)],
            10: [("n1t", 0, 1)], 11: [("n1t", 1, 1)], 16: [("vt", 0, 1)],
            15: [("h2t", 0, -1)], 19: [("h2t", 2, -1)], 23: [("lg", 0, -1)], 24: [("lg", 1, -1)]}
    ORDER = [j for n in range(UNITS) for j in JOBS.get(n, [])]
    assert len(ORDER) % 2 == 0
    FREED = {"mrow": (s_mrow, 1), "proj": (s_y, 1), "q": (s_qlo, 2), "n1t": (s_nf, 1), "lat": (s_klo, 1),
             "vt": (s_vlo, 1), "h2t": (s_h2c, 1), "lg": (s_lgc, 1)}

    def exists(b):
        return not isinstance(b, int) or 0 <= b < NB

    def job_bank(job):
        return PS[:, 6 + ORDER.index(job) % 2, :]

    def wait_job_bank(eng, b, job):
        at = ORDER.index(job) - 2
        while True:
            kind, idx, off = ORDER[at % len(ORDER)]
            bb = b + at // len(ORDER) + off
            if isinstance(bb, int) and bb < 0 and at < -len(ORDER):
                return
            if exists(bb):
                stream, each = FREED[kind]
                stream.wait(eng, bb, idx * each + each - 1)
                return
            at -= 2

    def unit(b, n):
        return b + n // UNITS, n % UNITS

    def batches(eng, body, looped=NB - 2):
        for b in (-1, 0):
            body(b, b % 2)
        with eng.Fori(0, looped // 2) as i:
            for j in range(2):
                body(i * 2 + (1 + j), (1 + j) % 2)
        for b in range(1 + looped, NB + 1):
            body(b, b % 2)

    with nc.Block() as block:
        @block.sync
        def _(sp):
            def load_x(b, par, row):
                sp.dma_start(X1[:, bass.ds(row, TC), :], x_rows[:, bass.ds(row, TC), :]
                             ).then_inc(s_xin[par].sem, 16)

            def body(b, par):
                if isinstance(b, int) and b == -1:
                    sp.wait_ge(s_const, 5)
                    load_x(0, 0, 0)
                    load_x(1, 1, TC)
                if exists(b):
                    if not (isinstance(b, int) and b >= NB - 2):
                        row = snap(sp, (b + 2) * TC)
                        s_norm[0].wait(sp, b, NORM_OPS - 1)
                        load_x(b + 2, par, row)
                    row = snap(sp, b + 0)
                    s_gbb.wait(sp, b - 2, TC - 1)
                    sp.dma_start(MODB[:, par, :, :], m["mod_dram"][bass.ds(row, 1), 0:4, :].rearrange("a j n -> (a j) n").partition_broadcast(P)
                                 ).then_inc(s_modin[par].sem, 16)
                for n in range(UNITS):
                    if n % 4 == 2:
                        tb, h = unit(b, n + 2)
                        h = h // TC
                        if exists(tb):
                            s_mrow.wait(sp, tb, h)
                            s_mdma.done(sp.dma_start(Q2[R:R + 1, h % 4, :].bitcast(F32), MROW[:, h % 2, :].bitcast(F32)))
                    if n == 20 and exists(b - 1):
                        row = snap(sp, (b - 1) * T)
                        s_hadd.wait(sp, b - 1, TC - 1)
                        for dram in (m["h2_dram"], m["acc_dram"]):
                            rows = dram[bass.ds(row, T), :].rearrange("(c p) n -> p c n", p=P)
                            s_h2out.done(sp.dma_start(rows, H2[:, :, :]))

            batches(sp, body, looped=NB - 4)
            s_h2out.wait(sp, NB - 1, 1)

        @block.gpsimd
        def _(pool):
            for i, (part, value) in enumerate(((K2[R:P, :, :], 0.0), (K2[R:R + 1, :, :], 1.0), (Q2[R:P, :, :], 0.0),
                                               (V1[:, :, :, R:2 * R], 1.0), (V2[:, :, :, R:2 * R], 0.0))):
                pool.memset(part.bitcast(F32), value).then_inc(s_const, 1)
                pool.wait_ge(s_const, i + 1)

            def body(b, par):
                for n in range(UNITS):
                    tb, u = unit(b, n + 1)
                    if exists(tb):
                        s_exp.wait(pool, tb, 2 * u + 1)
                        s_pv.wait(pool, tb, u - 4)
                        s_plo.done(pool.tensor_tensor(PL[:, u % 4, :], PF[:, u % 2, :], PH[:, u % 4, :].bitcast(F32),
                                                      ALU.subtract))
                    pb, pp = b - 1, 1 - par
                    if exists(pb):
                        if 12 <= n < 20:
                            c = (n - 12) // 2
                            if n % 2 == 0:
                                s_xn2.wait(pool, pb, c)
                                s_hmul.done(pool.tensor_tensor(H2[:, c, :], H2[:, c, :], MODB[:, pp, 1, :], ALU.mult))
                            else:
                                s_hmul.wait(pool, pb, c)
                                s_hadd.done(pool.tensor_tensor(H2[:, c, :], H2[:, c, :], MODB[:, pp, 2, :], ALU.add))
                        if 20 <= n < 24:
                            c = n - 20
                            x = X1[:, bass.ds(pb * TC + c, 1), :].rearrange("p c n -> p (c n)")
                            s_gbb.done(pool.tensor_tensor(x, x, MODB[:, pp, 3, :], ALU.add))

            batches(pool, body)

        @block.scalar
        def _(act):
            def body(b, par):
                for n in range(UNITS):
                    tb, u = unit(b, n + 1)
                    if exists(tb):
                        s_st.wait(act, tb, u)
                        s_pv.wait(act, tb, u - 4)
                        s_exp.done(act.activation(PH[:, u % 4, :], st_bank(u), ACT.Exp))
                        s_plo.wait(act, tb, u - 2)
                        s_exp.done(act.activation(PF[:, u % 2, :], st_bank(u), ACT.Exp))
                    for job in JOBS.get(n, []):
                        kind, idx, off = job
                        jb = b + off
                        if not exists(jb):
                            continue
                        bank = job_bank(job)
                        jp = (par + off) % 2
                        if kind == "q":
                            s_q.wait(act, jb, idx)
                            s_st.wait(act, jb, 8 * idx - 9)
                            for odd in range(2):
                                for half in range(2):
                                    s_qhi.done(act.activation(Q1[half * R:(half + 1) * R, (2 * idx + odd) % 4, :],
                                                              bank[odd * R:(odd + 1) * R, :], ACT.Copy))
                        elif kind == "lat":
                            s_lat.wait(act, jb, 0)
                            s_st.wait(act, jb - 2, UNITS - 1)
                            s_latc.done(act.activation(K1[0:R, jp, :], bank[0:R, :], ACT.Copy))
                            s_latc.done(act.activation(K2[0:R, jp, :], bank[0:R, :], ACT.Copy))
                            s_vt.wait(act, jb - 1, 0)
                            s_latc.done(act.activation(LTF[:, :], bank, ACT.Copy))
                        elif kind == "vt":
                            s_vt.wait(act, jb, 0)
                            s_pv.wait(act, jb - 2, UNITS - 1)
                            s_vhi.done(act.activation(V1[:, jp, :, 0:R],
                                                      bank.rearrange("p (c r) -> p c r", c=TC)[:, :, 0:R], ACT.Copy))
                        elif kind == "n1t":
                            s_n1t.wait(act, jb, idx)
                            s_nhl.wait(act, jb - 1, 2 * idx + 1)
                            s_nf.done(act.activation(NF[:, idx, :], bank, ACT.Identity,
                                                     bias=m["SA"][:, idx, bass.ds(jb, 1)], scale=m["CA1"][:, idx, bass.ds(jb, 1)]))
                        elif kind == "h2t":
                            s_h2t.wait(act, jb, idx)
                            s_lg.wait(act, jb - 1, 1)
                            s_h2c.done(act.activation(H2T[:, idx, :, :], bank[:, 0:D].rearrange("p (k n) -> p k n", k=KC),
                                                      ACT.Copy))
                    if 6 <= n < 10 and exists(b + 1):
                        c = n - 6
                        s_norm[0].wait(act, b + 1, NORM_OPS - 1)
                        s_n1t.wait(act, b, 1)
                        s_xn1.done(act.activation(XN1[:, c, :], X1[:, bass.ds((b + 1) * TC + c, 1), :].rearrange("p c n -> p (c n)"),
                                                  ACT.Identity, scale=norm[0]["y"][:, c:c + 1], bias=norm[0]["nmr"][:, c:c + 1]))
                    if n in (11, 12) and exists(b - 1):
                        for c in (2 * n - 22, 2 * n - 21):
                            s_norm[1].wait(act, b - 1, NORM_OPS - 1)
                            s_h2out.wait(act, b - 2, 1)
                            s_h2t.wait(act, b - 2, TC - 1)
                            s_xn2.done(act.activation(H2[:, c, :], X1[:, bass.ds((b - 1) * TC + c, 1), :].rearrange("p c n -> p (c n)"),
                                                      ACT.Identity, scale=norm[1]["y"][:, c:c + 1], bias=norm[1]["nmr"][:, c:c + 1]))
                    if n % 8 == 2:
                        xb, p = (b, n // 8 - 1) if n > 2 else (b - 1, 3)
                        if exists(xb):
                            s_x.wait(act, xb, 4 * (2 * p + 1) + 3)
                            s_proj.wait(act, xb - 1, TC - 1)
                            s_xhi.done(act.activation(XH[:, p, :], XF[:, p % 2, :], ACT.Copy))

            batches(act, body)

        @block.vector
        def _(dve):
            def gate(which, c):
                dve.memset(GATE[:, which * 8 + c:which * 8 + c + 1], 0.0)

            def norm_stats(which, nb, chunks):
                w, st = norm[which], s_norm[which]
                if chunks[0] == 0:
                    st.wait(dve, nb, -1)
                gate(which, chunks[0])
                for c in chunks:
                    st.done(dve.bn_stats(w["s6"][:, c, :], X1[:, bass.ds(nb * TC + c, 1), :].rearrange("p c n -> p (c n)")))
                st.wait(dve, nb, 2 * chunks[0] + len(chunks) - 1)
                gate(which, 4 + chunks[0])
                for c in chunks:
                    st.done(dve.bn_aggr(w["mv"][:, c, :], w["s6"][:, c, :]))

            def norm_scale(which, nb):
                w, st = norm[which], s_norm[which]
                k = [2 * TC]

                def link(ins):
                    st.done(ins)
                    st.wait(dve, nb, k[0])
                    k[0] += 1
                st.wait(dve, nb, k[0] - 1)
                rsqrt_and_shift(dve, link, w["mv"][:, :, :], *(w[x][:, :] for x in ("v", "y", "t", "nmr")))
                assert k[0] == NORM_OPS

            def body(b, par):
                pb, pp, nb = b - 1, 1 - par, b + 1
                for n in range(UNITS):
                    tb, u = unit(b, n + 8)
                    if exists(tb):
                        h, c = u // TC, u % TC
                        s_mx.wait(dve, tb, u)
                        if c == 0:
                            s_mt.wait(dve, tb, h - 2)
                        s_mred.done(dve.tensor_reduce(NMAX[:, h % 2, c:c + 1], mx_bank(u), AX.X, ALU.max, negate=True))
                    for job in JOBS.get(n, []):
                        kind, idx, off = job
                        jb = b + off
                        if not exists(jb):
                            continue
                        bank = job_bank(job)
                        jp = (par + off) % 2
                        if kind == "mrow":
                            s_mt.wait(dve, jb, idx)
                            s_mdma.wait(dve, jb, idx - 2)
                            s_mrow.done(dve.tensor_copy(MROW[:, idx % 2, :], bank[0:TC, 0:P]))
                        elif kind == "q":
                            for odd in range(2):
                                s_qhi.wait(dve, jb, 4 * idx + 2 * odd + 1)
                                h = (2 * idx + odd) % 4
                                s_qlo.done(dve.tensor_tensor(Q2[0:R, h, :], bank[odd * R:(odd + 1) * R, :],
                                                             Q1[odd * R:(odd + 1) * R, h, :].bitcast(F32), ALU.subtract))
                        elif kind == "proj":
                            s_modin[pp].wait(dve, jb)
                            s_proj.wait(dve, jb, idx)
                            s_x1.wait(dve, jb, idx - 1)
                            s_y.done(dve.tensor_tensor(YT[:, idx % 2, :], bank[:, 0:D], MODB[:, pp, 0, :], ALU.mult))
                            s_y.wait(dve, jb, idx)
                            x = X1[:, bass.ds(jb * TC + idx, 1), :].rearrange("p c n -> p (c n)")
                            s_x1.done(dve.tensor_tensor(x, YT[:, idx % 2, :], x, ALU.add))
                            s_x1.wait(dve, jb, idx)
                            norm_stats(1, jb, [idx])
                        elif kind == "n1t":
                            s_nf.wait(dve, jb, idx)
                            s_q.wait(dve, jb - 2, 3)
                            s_nhl.done(dve.tensor_copy(NHI[:, jp, idx, :], NF[:, idx, :]))
                            s_nhl.wait(dve, jb, 2 * idx)
                            s_nhl.done(dve.tensor_tensor(NLO[:, jp, idx, :], NF[:, idx, :], NHI[:, jp, idx, :].bitcast(F32),
                                                         ALU.subtract))
                        elif kind == "lat":
                            s_latc.wait(dve, jb, 2)
                            s_klo.done(dve.tensor_tensor(K1[R:P, jp, :], bank[R:P, :], K1[0:R, jp, :].bitcast(F32), ALU.subtract))
                        elif kind == "vt":
                            s_vhi.wait(dve, jb, 0)
                            s_vlo.done(dve.tensor_tensor(V2[:, jp, :, 0:R], bank.rearrange("p (c r) -> p c r", c=TC)[:, :, 0:R],
                                                         V1[:, jp, :, 0:R].bitcast(F32), ALU.subtract))
                        elif kind == "lg":
                            s_lg.wait(dve, jb, idx)
                            s_lgc.done(dve.tensor_tensor(
                                LOGITS[:, bass.ds(jb * TC + 2 * idx, 2), :], bank[:, 0:2 * E].rearrange("p (c e) -> p c e", c=2),
                                BR[:, :].unsqueeze(1).broadcast_to([P, 2, E]), ALU.add))
                    if n % 4 == 1:
                        xb, h = (b, (n - 5) // 4) if n >= 5 else (b - 1, H - 1)
                        if exists(xb):
                            bank = pv_bank(h)
                            s_pv.wait(dve, xb, TC * h + TC - 1)
                            s_x.wait(dve, xb, 4 * h - 1)
                            s_x.done(dve.transpose(DENT[:, :], bank[R:P, :]))
                            s_x.wait(dve, xb, 4 * h)
                            s_x.done(dve.reciprocal(RDEN[:, :], DENT[:, :].rearrange("p (g j) -> p g j", j=32)[:, :, 0]))
                            s_x.wait(dve, xb, 4 * h + 1)
                            s_x.done(dve.transpose(RECT[:, :], RDEN[:, :].unsqueeze(2).broadcast_to([R, T // 32, 32])))
                            s_x.wait(dve, xb, 4 * h + 2)
                            p, odd = h // 2, h % 2
                            if odd == 0:
                                s_xhi.wait(dve, xb, p - 2)
                                s_xlo.wait(dve, xb, p - 2)
                            s_x.done(dve.tensor_tensor(XF[odd * R:(odd + 1) * R, p % 2, :], bank[0:R, :], RECT[:, :], ALU.mult))
                    if n % 8 == 2:
                        xb, p = (b, n // 8 - 1) if n > 2 else (b - 1, 3)
                        if exists(xb):
                            s_xhi.wait(dve, xb, p)
                            s_xlo.done(dve.tensor_tensor(XL[:, p, :], XF[:, p % 2, :], XH[:, p, :].bitcast(F32), ALU.subtract))
                    if exists(nb):
                        if n in (0, 2):
                            if n == 0:
                                s_xin[1 - par].wait(dve, nb)
                                s_xn1.wait(dve, nb - 1, TC - 1)
                            norm_stats(0, nb, [n, n + 1])
                        if n == 3:
                            norm_scale(0, nb)
                    if n == 10 and exists(pb):
                        s_xn2.wait(dve, pb - 1, TC - 1)
                        norm_scale(1, pb)

            batches(dve, body)

        @block.tensor
        def _(pe):
            pe.wait_ge(s_const, 5)

            def body(b, par):
                for n in range(UNITS):
                    tb, u = unit(b, n + 1)
                    if exists(tb):
                        h, c, kp = u // TC, u % TC, (par + (n + 1) // UNITS) % 2
                        s_exp.wait(pe, tb, 2 * (u - 2) + 1)
                        if c == 0:
                            s_mdma.wait(pe, tb, h)
                            s_qlo.wait(pe, tb, h)
                        keys = slice(c * P, (c + 1) * P)
                        pe.matmul(st_bank(u), K1[:, kp, keys], Q1[:, h % 4, :], start=True, stop=False)
                        s_st.done(pe.matmul(st_bank(u), K2[:, kp, keys], Q2[:, h % 4, :], start=False, stop=True))
                    tb, u = unit(b, n + 8)
                    if exists(tb):
                        h, c, kp = u // TC, u % TC, (par + (n + 8) // UNITS) % 2
                        s_mred.wait(pe, tb, u - 2)
                        if c == 0:
                            s_qlo.wait(pe, tb, h)
                            s_klo.wait(pe, tb, 0)
                        s_mx.done(pe.matmul(mx_bank(u), Q1[:, h % 4, c * P:(c + 1) * P], K1[:, kp, :], start=True, stop=True))
                    for job in JOBS.get(n, []):
                        kind, idx, off = job
                        jb = b + off
                        if not exists(jb):
                            continue
                        wait_job_bank(pe, b, job)
                        bank = job_bank(job)
                        jp = (par + off) % 2
                        if kind == "mrow":
                            s_mred.wait(pe, jb, TC * idx + TC - 1)
                            s_mt.done(pe.transpose(bank[0:TC, 0:P], NMAX[:, idx % 2, :], IDENT[:, :]))
                        elif kind == "q":
                            s_nhl.wait(pe, jb, 3)
                            cols = slice(2 * idx * R, 2 * (idx + 1) * R)
                            for k in range(KC):
                                last = hi_lo_matmul(pe, bank, (AH[:, k, cols], AL[:, k, cols]),
                                                    (NHI[:, jp, k, :], NLO[:, jp, k, :]), k == 0, k == KC - 1)
                            s_q.done(last)
                        elif kind == "lat":
                            s_nhl.wait(pe, jb, 3)
                            for k in range(KC):
                                last = hi_lo_matmul(pe, bank, (DH[:, k, :], DL[:, k, :]),
                                                    (NHI[:, jp, k, :], NLO[:, jp, k, :]), k == 0, k == KC - 1)
                            s_lat.done(last)
                        elif kind == "vt":
                            s_latc.wait(pe, jb, 2)
                            for c in range(TC):
                                last = pe.transpose(bank[:, c * P:(c + 1) * P], LTF[:, c * P:(c + 1) * P], IDENT[:, :])
                            s_vt.done(last)
                        elif kind == "n1t":
                            s_xn1.wait(pe, jb, TC - 1)
                            for c in range(TC):
                                last = pe.transpose(bank[:, c * P:(c + 1) * P], XN1[:, c, idx * P:(idx + 1) * P], IDENT[:, :])
                            s_n1t.done(last)
                        elif kind == "proj":
                            s_xhi.wait(pe, jb, 3)
                            s_xlo.wait(pe, jb, 3)
                            rows = slice(idx * P, (idx + 1) * P)
                            for p in range(H // 2):
                                last = hi_lo_matmul(pe, bank[:, 0:D], (XH[:, p, rows], XL[:, p, rows]),
                                                    (GH[:, p, :], GL[:, p, :]), p == 0, p == H // 2 - 1)
                            s_proj.done(last)
                        elif kind == "h2t":
                            s_hadd.wait(pe, jb, idx)
                            for k in range(KC):
                                last = pe.transpose(bank[:, k * P:(k + 1) * P], H2[:, idx, k * P:(k + 1) * P], IDENT[:, :])
                            s_h2t.done(last)
                        elif kind == "lg":
                            s_h2c.wait(pe, jb, 2 * idx + 1)
                            for c in range(2):
                                for k in range(KC):
                                    last = pe.matmul(bank[:, c * E:(c + 1) * E], H2T[:, 2 * idx + c, k, :], WR[:, k, :],
                                                     start=(k == 0), stop=(k == KC - 1))
                            s_lg.done(last)
                    tb, u = unit(b, n - 1)
                    if exists(tb):
                        h, c, vp = u // TC, u % TC, (par + (n - 1) // UNITS) % 2
                        if c == 0:
                            s_x.wait(pe, tb, 4 * (h - 2) + 3)
                            s_vlo.wait(pe, tb, 0)
                        s_exp.wait(pe, tb, 2 * u)
                        bank = pv_bank(h)
                        pe.matmul(bank, V1[:, vp, c, :], PH[:, u % 4, :], start=(c == 0), stop=False)
                        pe.matmul(bank, V2[:, vp, c, :], PH[:, u % 4, :], start=False, stop=False)
                        s_plo.wait(pe, tb, u)
                        s_pv.done(pe.matmul(bank, V1[:, vp, c, :], PL[:, u % 4, :], start=False, stop=(c == TC - 1)))

            batches(pe, body)


def route(nc, ap, m, sem, sb):
    PS, IDENT, LOGITS = m["PS"], m["IDENT"], m["LOGITS"]
    NS = NCH // TC
    BIG = 127 * P
    SLOTC = E * CAP // P
    RING = 8
    EQ, OH1, OH2, L2 = (sb(x, [P, NCH, E]) for x in ("EQ", "OH1", "OH2", "L2"))
    KEY = sb("KEY", [P, TC, NS, E])
    M1, M2, I1, I2, EX, W1, W2, DEN = (sb(x, [P, NCH]) for x in ("M1", "M2", "I1", "I2", "EX", "W1", "W2", "DENr"))
    RANK8 = sb("RANK8", [P, E])
    KT, JUNK, GT, EQT, SEL, SCAN, DST, ZT = (sb(x, [P, T]) for x in ("KT", "JUNK", "GT", "EQT", "SEL", "SCAN", "DST", "ZT"))
    DIFF, DIFM = sb("DIFF", [P, P], I32), sb("DIFM", [P, P], I32)
    SAME, LOWER, ONES = sb("SAME", [P, P]), sb("LOWER", [P, P]), sb("ONES", [P, P])
    BITU, BITF = sb("BITU", [P, 31], U32), sb("BITF", [P, 31])
    CAND, FOUND, INC = sb("CAND", [P, 1], U32), sb("FOUND", [P, 1], U32), sb("INC", [P, 1], U32)
    CNT = sb("CNT", [P, 8])
    ECOLI, ECOL = sb("ECOLI", [P, 1], I32), sb("ECOL", [P, 1])
    D1, D12 = sb("D1", [P, NCH]), sb("D12", [P, 2, NCH])
    DI, AI, BI = (sb(x, [P, 2 * NCH], U32) for x in ("DI", "AI", "BI"))
    AF, BF = sb("AF", [P, 2 * NCH]), sb("BF", [P, 2 * NCH])
    TOK1, IOT = sb("TOK1", [P, 2, NCH]), sb("IOT", [P, P])
    OB, OA, ZP = sb("OB", [P, RING, P]), sb("OA", [P, RING, SLOTC]), sb("ZP", [P, P])
    SPARE, LF = sb("SPARE", [P, 1]), sb("LF", [P, SLOTC])
    NBR, NBD = sb("NBR", [1, 6, E]), sb("NBD", [P, E])
    ktab = m["ktab_dram"]
    s_pool, s_dve, s_exp, s_key, s_tab = (sem(x) for x in ("s_rpool", "s_rdve", "s_rexp", "s_rkey", "s_rtab"))
    s_kt, s_sum, s_cnt, s_tot, s_dt = (sem(x) for x in ("s_rkt", "s_rsum", "s_rcnt", "s_rtot", "s_rdt"))
    s_ob, s_oa, s_mm, s_list, s_nb, s_dd = (sem(x) for x in ("s_rob", "s_roa", "s_rmm", "s_rlist", "s_rnb", "s_rdd"))
    s_db, s_ab = sem("s_rdb"), sem("s_rab")
    NBITS = 30
    POOL_CONSTS, MASKS_DONE = 7 + 2 * NBITS + 4, 3
    kt_ps = PS[:, 0, :]
    cnt_ps, off_ps, tot_ps = PS[:, 1, 0:1], PS[:, 2, 0:1], PS[:, 3, 0:1]
    dt_ps = PS[:, 4, :]
    list_ps, nb_ps = PS[:, 5, 0:SLOTC], PS[:, 6, 0:E]

    def by_expert(x):
        return x.unsqueeze(2).broadcast_to([P, NCH, E])

    with nc.Block() as block:
        @block.gpsimd
        def _(pool):
            n = [0]

            def link(ins):
                ins.then_inc(s_pool, 1)
                n[0] += 1
                pool.wait_ge(s_pool, n[0])
            link(pool.iota(RANK8[:, :], pattern=[[-1, E]], base=E, channel_multiplier=0, allow_small_or_imprecise_dtypes=True))
            link(pool.iota(DIFF[:, :], pattern=[[1, P]], base=P, channel_multiplier=-1))
            link(pool.iota(ECOLI[:, :], pattern=[[0, 1]], base=0, channel_multiplier=1))
            link(pool.iota(IOT[:, :], pattern=[[1, P]], base=0, channel_multiplier=0, allow_small_or_imprecise_dtypes=True))
            link(pool.iota(SPARE[:, :], pattern=[[0, 1]], base=NT + 1, channel_multiplier=1, allow_small_or_imprecise_dtypes=True))
            for j in range(2):
                link(pool.iota(TOK1[:, j, :].rearrange("p (a b) -> p a b", a=TC), pattern=[[P, TC], [TC * P, NS]], base=1,
                               channel_multiplier=1, allow_small_or_imprecise_dtypes=True))
            for k in range(NBITS):
                pool.memset(BITU[:, k:k + 1], 1 << (NBITS - 1 - k)).then_inc(s_pool, 1)
                pool.memset(BITF[:, k:k + 1], float(1 << (NBITS - 1 - k))).then_inc(s_pool, 1)
            pool.memset(BITU[:, NBITS:], 0).then_inc(s_pool, 1)
            pool.memset(ZT[:, :], 0.0).then_inc(s_pool, 1)
            pool.memset(ZP[:, :], 0.0).then_inc(s_pool, 1)
            pool.memset(ONES[:, :], 1.0).then_inc(s_pool, 1)

        @block.scalar
        def _(act):
            act.wait_ge(s_dd, 1)
            act.activation(EX[:, :], DEN[:, :], ACT.Exp).then_inc(s_exp, 1)
            act.wait_ge(s_kt, 1)
            act.activation(KT[:, :], kt_ps, ACT.Copy).then_inc(s_exp, 1)

        @block.sync
        def _(sp):
            sp.wait_ge(s_key, TC)
            rows = ktab[0:NT, :].rearrange("(c q p) e -> q p c e", p=P, q=TC)
            for q in range(TC):
                sp.dma_start(rows[q], KEY[:, q, :, :]).then_inc(s_tab, 16)
            sp.wait_ge(s_pool, POOL_CONSTS)
            sp.dma_start(ktab[NT:NT + P, :], ZP[:, 0:E]).then_inc(s_tab, 16)
            sp.wait_ge(s_tab, 16 * (TC + 1))

        @block.tensor
        def _(pe):
            pe.wait_ge(s_key, TC)
            for q in range(TC):
                last = pe.transpose(kt_ps[:, q * P:(q + 1) * P], KEY[:, q, :, :].rearrange("p c e -> p (c e)"), IDENT[:, :])
            last.then_inc(s_kt, 1)
            pe.wait_ge(s_dve, MASKS_DONE)
            with pe.Fori(0, NBITS) as i:
                pe.wait_ge(s_cnt, i + 1)
                pe.matmul(cnt_ps, SAME[:, :], CNT[:, 0:1], start=True, stop=True).then_inc(s_sum, 1)
            pe.wait_ge(s_tot, 1)
            pe.matmul(tot_ps, SAME[:, :], CNT[:, 1:2], start=True, stop=True)
            pe.matmul(off_ps, LOWER[:, :], CNT[:, 2:3], start=True, stop=True).then_inc(s_sum, 1)
            pe.wait_ge(s_tot, 2)
            pe.matmul(tot_ps, SAME[:, :], CNT[:, 3:4], start=True, stop=True)
            pe.matmul(off_ps, LOWER[:, :], CNT[:, 3:4], start=True, stop=True).then_inc(s_sum, 1)
            pe.wait_ge(s_tot, 3)
            for q in range(TC):
                last = pe.transpose(dt_ps[:, q * P:(q + 1) * P], DST[:, q * P:(q + 1) * P], IDENT[:, :])
            last.then_inc(s_dt, 1)
            pe.matmul(nb_ps, ONES[:, :], NBD[:, :], start=True, stop=True).then_inc(s_nb, 1)
            pe.wait_ge(s_pool, POOL_CONSTS)
            for r in range(RING):
                pe.matmul(list_ps, ZP[:, :], ZP[:, 0:SLOTC], start=(r == 0), stop=False).then_inc(s_mm, 1)
            with pe.Fori(0, 2 * NCH // RING) as i:
                pe.wait_ge(s_oa, i + 1)
                for r in range(RING):
                    pe.wait_ge(s_ob, i * RING + (r + 1))
                    pe.matmul(list_ps, OB[:, r, :], OA[:, r, :], start=False, stop=False).then_inc(s_mm, 1)
            pe.matmul(list_ps, ZP[:, :], ZP[:, 0:SLOTC], start=False, stop=True).then_inc(s_list, 1)

        @block.vector
        def _(dve):
            n = [0]

            def link(ins):
                ins.then_inc(s_dve, 1)
                n[0] += 1
                dve.wait_ge(s_dve, n[0])
            dve.wait_ge(s_pool, POOL_CONSTS)
            link(dve.tensor_scalar(DIFM[:, :], DIFF[:, :], E - 1, None, ALU.bitwise_and))
            link(dve.tensor_scalar(SAME[:, :], DIFM[:, :], 0.0, None, ALU.is_equal))
            link(dve.scalar_tensor_tensor(out=LOWER[:, :], in0=DIFF[:, :], scalar=float(P), in1=SAME[:, :],
                                          op0=ALU.is_gt, op1=ALU.mult))
            rank8 = RANK8[:, :].unsqueeze(1).broadcast_to([P, NCH, E])
            link(dve.tensor_reduce(M1[:, :], LOGITS[:, :, :], AX.X, ALU.max))
            link(dve.tensor_tensor(EQ[:, :, :], LOGITS[:, :, :], by_expert(M1[:, :]), ALU.is_equal))
            link(dve.tensor_tensor(EQ[:, :, :], EQ[:, :, :], rank8, ALU.mult))
            link(dve.tensor_reduce(I1[:, :], EQ[:, :, :], AX.X, ALU.max))
            link(dve.tensor_tensor(OH1[:, :, :], rank8, by_expert(I1[:, :]), ALU.is_equal))
            link(dve.scalar_tensor_tensor(out=L2[:, :, :], in0=OH1[:, :, :], scalar=-3.0e38, in1=LOGITS[:, :, :],
                                          op0=ALU.mult, op1=ALU.add))
            link(dve.tensor_reduce(M2[:, :], L2[:, :, :], AX.X, ALU.max))
            link(dve.tensor_tensor(DEN[:, :], M2[:, :], M1[:, :], ALU.subtract))
            dve.sem_inc(s_dd, 1)
            link(dve.tensor_tensor(EQ[:, :, :], L2[:, :, :], by_expert(M2[:, :]), ALU.is_equal))
            link(dve.tensor_tensor(EQ[:, :, :], EQ[:, :, :], rank8, ALU.mult))
            link(dve.tensor_reduce(I2[:, :], EQ[:, :, :], AX.X, ALU.max))
            link(dve.tensor_tensor(OH2[:, :, :], rank8, by_expert(I2[:, :]), ALU.is_equal))
            dve.wait_ge(s_exp, 1)
            link(dve.tensor_scalar(DEN[:, :], EX[:, :], 1.0, None, ALU.add))
            link(dve.reciprocal(W1[:, :], DEN[:, :]))
            link(dve.tensor_tensor(W2[:, :], EX[:, :], W1[:, :], ALU.mult))
            link(dve.tensor_tensor(EQ[:, :, :], OH1[:, :, :], OH2[:, :, :], ALU.add))
            link(dve.tensor_tensor(OH1[:, :, :], OH1[:, :, :], by_expert(W1[:, :]), ALU.mult))
            link(dve.tensor_tensor(OH2[:, :, :], OH2[:, :, :], by_expert(W2[:, :]), ALU.mult))
            link(dve.tensor_tensor(OH1[:, :, :], OH1[:, :, :], OH2[:, :, :], ALU.add))
            for q in range(TC):
                dve.scalar_tensor_tensor(out=KEY[:, q, :, :], in0=EQ[:, q::TC, :], scalar=-1.0, in1=OH1[:, q::TC, :],
                                         op0=ALU.add, op1=ALU.add).then_inc(s_key, 1)
            link(dve.memset(FOUND[:, :], 0))
            link(dve.tensor_copy(CAND[:, :].bitcast(F32), BITU[:, 0:1].bitcast(F32)))
            dve.wait_ge(s_exp, 2)
            with dve.Fori(0, NBITS) as i:
                dve.wait_ge(s_db, i)
                dve.tensor_scalar(JUNK[:, :], KT[:, :], CAND[:, :].bitcast(F32), None, ALU.is_ge, ALU.add,
                                  accum_out=CNT[:, 0:1]).then_inc(s_cnt, 1)
                dve.wait_ge(s_sum, i + 1)
                dve.tensor_scalar(INC[:, :], cnt_ps, float(CAP), BITF[:, bass.ds(i, 1)], ALU.is_ge, ALU.mult).then_inc(s_ab, 1)
                dve.wait_ge(s_ab, i * 2 + 1)
                dve.tensor_tensor(FOUND[:, :], FOUND[:, :], INC[:, :], ALU.bitwise_or).then_inc(s_ab, 1)
                dve.wait_ge(s_ab, i * 2 + 2)
                dve.tensor_tensor(CAND[:, :], FOUND[:, :], BITU[:, bass.ds(i + 1, 1)], ALU.bitwise_or).then_inc(s_db, 1)
            dve.wait_ge(s_db, NBITS)
            thr = FOUND[:, :].bitcast(F32)
            link(dve.tensor_scalar(GT[:, :], KT[:, :], thr, None, ALU.is_gt, ALU.add, accum_out=CNT[:, 1:2]))
            link(dve.tensor_scalar(EQT[:, :], KT[:, :], thr, None, ALU.is_equal, ALU.add, accum_out=CNT[:, 2:3]))
            dve.sem_inc(s_tot, 1)
            link(dve.tensor_tensor_scan(SCAN[:, :], EQT[:, :], ZT[:, :], 0.0, ALU.add, ALU.add))
            link(dve.tensor_scalar(ECOLI[:, :], ECOLI[:, :], E - 1, None, ALU.bitwise_and))
            link(dve.tensor_scalar(ECOL[:, :], ECOLI[:, :], float(CAP), float(-1 - BIG), ALU.mult, ALU.add))
            dve.wait_ge(s_sum, NBITS + 1)
            link(dve.tensor_scalar(CNT[:, 4:5], tot_ps, -1.0, float(CAP), ALU.mult, ALU.add))
            link(dve.tensor_tensor(CNT[:, 4:5], CNT[:, 4:5], off_ps, ALU.subtract))
            link(dve.scalar_tensor_tensor(out=SEL[:, :], in0=SCAN[:, :], scalar=CNT[:, 4:5], in1=EQT[:, :],
                                          op0=ALU.is_le, op1=ALU.mult))
            link(dve.tensor_tensor(SEL[:, :], SEL[:, :], GT[:, :], ALU.add))
            link(dve.tensor_reduce(CNT[:, 3:4], SEL[:, :], AX.X, ALU.add))
            dve.sem_inc(s_tot, 1)
            link(dve.tensor_tensor_scan(SCAN[:, :], SEL[:, :], ZT[:, :], 0.0, ALU.add, ALU.add))
            dve.wait_ge(s_sum, NBITS + 2)
            link(dve.tensor_tensor(CNT[:, 5:6], ECOL[:, :], off_ps, ALU.add))
            link(dve.scalar_tensor_tensor(out=DST[:, :], in0=SCAN[:, :], scalar=CNT[:, 5:6], in1=SEL[:, :],
                                          op0=ALU.add, op1=ALU.mult))
            link(dve.tensor_scalar(CNT[:, 6:7], tot_ps, 0.0, None, ALU.is_gt))
            for j in range(1, -(-CAP // BLK)):
                link(dve.scalar_tensor_tensor(out=CNT[:, 6:7], in0=tot_ps, scalar=float(j * BLK), in1=CNT[:, 6:7],
                                              op0=ALU.is_gt, op1=ALU.add))
            link(dve.tensor_scalar(NBD[:, :], IDENT[:, 0:E], CNT[:, 6:7], None, ALU.mult))
            dve.sem_inc(s_tot, 1)
            dve.wait_ge(s_nb, 1)
            nb, act_, cum, cua, z = (NBR[:, j, :] for j in range(5))
            link(dve.tensor_copy(nb, nb_ps[0:1, :]))
            link(dve.tensor_scalar(act_, nb, 0.0, None, ALU.is_gt))
            link(dve.memset(z, 0.0))
            link(dve.tensor_tensor_scan(cum, nb, z, 0.0, ALU.add, ALU.add))
            link(dve.tensor_tensor_scan(cua, act_, z, 0.0, ALU.add, ALU.add))
            link(dve.tensor_tensor(cum, cum, nb, ALU.subtract))
            link(dve.tensor_tensor(cua, cua, act_, ALU.subtract))
            for j, row in enumerate((nb, cum, cua)):
                link(dve.tensor_copy(m["INFO"][:, j * E:(j + 1) * E], row))
            dve.wait_ge(s_dt, 1)
            by_tok = dt_ps.rearrange("p (n e) -> p n e", e=E)
            link(dve.tensor_reduce(D12[:, 0, :], by_tok, AX.X, ALU.min))
            link(dve.tensor_tensor(EQ[:, :, :], by_tok, by_expert(D12[:, 0, :]), ALU.is_equal))
            link(dve.scalar_tensor_tensor(out=EQ[:, :, :], in0=EQ[:, :, :], scalar=float(BIG), in1=by_tok,
                                          op0=ALU.mult, op1=ALU.add))
            link(dve.tensor_reduce(D12[:, 1, :], EQ[:, :, :], AX.X, ALU.min))
            link(dve.tensor_scalar(DI[:, :], D12[:, :, :].rearrange("p j n -> p (j n)"), float(BIG), None, ALU.add))
            link(dve.tensor_scalar(AI[:, :], DI[:, :], 7, None, ALU.logical_shift_right))
            link(dve.tensor_scalar(BI[:, :], DI[:, :], P - 1, None, ALU.bitwise_and))
            link(dve.tensor_copy(BF[:, :], BI[:, :]))
            link(dve.tensor_copy(AF[:, :], AI[:, :]))
            dve.sem_inc(s_dd, 1)
            with dve.Fori(0, 2 * NCH // RING) as i:
                dve.wait_ge(s_mm, (i + 1) * RING)
                dve.tensor_tensor(OA[:, :, :], IOT[:, 0:SLOTC].unsqueeze(1).broadcast_to([P, RING, SLOTC]),
                                  AF[:, bass.ds(i * RING, RING)].unsqueeze(2).broadcast_to([P, RING, SLOTC]),
                                  ALU.is_equal).then_inc(s_oa, 1)
                for r in range(RING):
                    dve.wait_ge(s_mm, i * RING + (r + 1))
                    col = bass.ds(i * RING + r, 1)
                    dve.tensor_scalar(OB[:, r, :], IOT[:, :], BF[:, col], TOK1[:, :, :].rearrange("p j n -> p (j n)")[:, col],
                                      ALU.is_equal, ALU.mult).then_inc(s_ob, 1)
            dve.wait_ge(s_list, 1)
            link(dve.tensor_scalar(LF[:, :], list_ps, 0.0, SPARE[:, :], ALU.is_equal, ALU.mult))
            link(dve.scalar_tensor_tensor(out=m["IDX"][:, :], in0=list_ps, scalar=-1.0, in1=LF[:, :], op0=ALU.add, op1=ALU.add))




def experts(nc, ap, m, sem, sb):
    PS, IDENT, IDX, INFO = m["PS"], m["IDENT"], m["IDX"], m["INFO"]
    FC, BT = F // P, BLK // P
    MAXB = CAP // BLK
    GATES_USED = 4 + BT
    assert CAP % BLK == 0
    W1F, W2F = sb("W1F", [P, KC, F]), sb("W2F", [P, FC, D])
    W1H, W1L = sb("W1H", [P, KC, F], F32R), sb("W1L", [P, KC, F], F32R)
    W2H, W2L = sb("W2H", [P, FC, D], F32R), sb("W2L", [P, FC, D], F32R)
    B1R, B1, B2 = sb("B1R", [E * FC, P]), sb("B1", [P, E * FC]), sb("B2", [P, E, D])
    XG, GK, TOKG, TOKS = sb("XG", [P, BT, D]), sb("GK", [P, BT, E]), sb("TOKG", [P, BT], U32), sb("TOKS", [P, BT], U32)
    XTH, XTL = sb("XTH", [P, KC, BLK], F32R), sb("XTL", [P, KC, BLK], F32R)
    HF, HH, HL = sb("HF", [P, 4, BLK]), sb("HH", [P, 4, BLK], F32R), sb("HL", [P, 4, BLK], F32R)
    YS, GATES, GATE = sb("YS", [P, BT, D]), sb("GATES", [P, BT]), sb("GATEp", [P, GATES_USED + 1])

    def S(name, per, step=1):
        return Stream(sem(name), per, step)
    s_w1, s_w2 = S("fw1", 1, 16), S("fw2", 1, 16)
    s_w1h, s_w2h, s_w1l, s_w2l = S("fw1h", 1), S("fw2h", 1), S("fw1l", 1), S("fw2l", 1)
    s_gx, s_gk, s_sc = S("fgx", 1, 16 * BT), S("fgk", 1, 16 * BT), S("fsc", BT, 16)
    s_tokg, s_toks = S("ftokg", BT), S("ftoks", 1)
    s_t, s_m1, s_m2, s_gate = S("ft", 1), S("fm1", FC), S("fm2", FC), S("fgate", BT)
    s_xh, s_xl, s_gelu, s_hh, s_hl, s_y = S("fxh", 1), S("fxl", 1), S("fgelu", FC), S("fhh", FC), S("fhl", FC), S("fy", 2 * BT)
    s_init, s_b, s_b1t, s_b1 = sem("finit"), sem("fb"), sem("fb1t"), sem("fb1")
    xt_bank = PS[:, 0, :]
    xt = xt_bank.rearrange("p (k n) -> p k n", k=KC)

    def h_bank(f):
        return PS[:, 1 + f % 4, 0:BLK]

    def y_bank(t):
        return PS[:, 5 + t, 0:D]

    def each(eng, expert, block):
        with eng.Fori(0, E) as e:
            nb = eng.value_load(INFO[0:1, bass.ds(e, 1)], min_val=0, max_val=MAXB)
            g0 = eng.value_load(INFO[0:1, bass.ds(e + E, 1)], min_val=0, max_val=E * MAXB)
            a = eng.value_load(INFO[0:1, bass.ds(e + 2 * E, 1)], min_val=0, max_val=E)
            with eng.If(nb > 0):
                if expert is not None:
                    expert(e, a, g0)
                if block is not None:
                    with eng.Fori(0, nb) as k:
                        block(e, a, g0 + k, k)

    with nc.Block() as blk:
        @blk.sync
        def _(sp):
            w1 = ap["L0_ffn_W1"].rearrange("e (k p) f -> p (e k) f", p=P)
            w2 = ap["L0_ffn_W2"].rearrange("e (f p) n -> p (e f) n", p=P)
            sp.dma_start(B1R[:, :], ap["L0_ffn_b1"].rearrange("e (f p) -> (e f) p", p=P)).then_inc(s_b, 16)
            sp.dma_start(B2[:, :, :], ap["L0_ffn_b2"].partition_broadcast(P)).then_inc(s_b, 16)

            def expert(e, a, g):
                k_row, f_row = sp.snap(e * KC), sp.snap(e * FC)
                s_w1l.wait(sp, a, -1)
                s_w1.done(sp.dma_start(W1F[:, :, :], w1[:, bass.ds(k_row, KC), :]))
                s_w2l.wait(sp, a, -1)
                s_w2.done(sp.dma_start(W2F[:, :, :], w2[:, bass.ds(f_row, FC), :]))
            each(sp, expert, None)

        @blk.gpsimd
        def _(pool):
            pool.iota(TOKS[:, :].bitcast(I32), pattern=[[0, BT]], base=NT, channel_multiplier=1).then_inc(s_init, 1)
            pool.memset(YS[:, :, :], 0.0).then_inc(s_init, 1)
            pool.memset(GATE[:, :], 0.0).then_inc(s_init, 1)
            pool.wait_ge(s_init, 3)

            def gate(j):
                pool.tensor_tensor(GATE[:, j:j + 1], GATE[:, GATES_USED:], GATE[:, GATES_USED:], ALU.add)

            def scatter(g):
                s_y.wait(pool, g, -1)
                for t in range(BT):
                    if t:
                        s_sc.wait(pool, g, t - 1)
                    gate(4 + t)
                    off = bass.IndirectOffsetOnAxis(ap=TOKS[:, t:t + 1], axis=0)
                    s_sc.done(pool.indirect_dma_start(out=m["acc_dram"], out_offset=off, in_=YS[:, t, :], in_offset=None,
                                                      compute_op=ALU.add))

            def block(e, a, g, k):
                s_toks.wait(pool, g, -1)
                gate(0)
                for t in range(BT):
                    s_tokg.done(pool.tensor_copy(TOKG[:, t:t + 1], IDX[:, bass.ds(e * (CAP // P) + k * BT + t, 1)]))
                s_tokg.wait(pool, g, BT - 1)
                s_t.wait(pool, g, -1)
                gate(1)
                for t in range(BT):
                    off = bass.IndirectOffsetOnAxis(ap=TOKG[:, t:t + 1], axis=0)
                    pool.indirect_dma_start(out=XG[:, t, :], out_offset=None, in_=m["h2_dram"], in_offset=off).then_inc(s_gx.sem, 16)
                s_gate.wait(pool, g, -1)
                gate(2)
                for t in range(BT):
                    off = bass.IndirectOffsetOnAxis(ap=TOKG[:, t:t + 1], axis=0)
                    pool.indirect_dma_start(out=GK[:, t, :], out_offset=None, in_=m["ktab_dram"], in_offset=off).then_inc(s_gk.sem, 16)
                scatter(g)
                s_sc.wait(pool, g, BT - 1)
                gate(3)
                s_toks.done(pool.tensor_copy(TOKS[:, :], TOKG[:, :]))
            each(pool, None, block)
            total = (pool.value_load(INFO[0:1, E - 1:E], min_val=0, max_val=MAXB)
                     + pool.value_load(INFO[0:1, 2 * E - 1:2 * E], min_val=0, max_val=E * MAXB))
            s_toks.wait(pool, total, -1)
            scatter(total)
            s_sc.wait(pool, total, BT - 1)

        @blk.scalar
        def _(act):
            def expert(e, a, g):
                s_w1.wait(act, a, 0)
                s_m2.wait(act, g, -1)
                s_w1h.done(act.activation(W1H[:, :, :], W1F[:, :, :], ACT.Copy))
                s_w2.wait(act, a, 0)
                s_w2h.done(act.activation(W2H[:, :, :], W2F[:, :, :], ACT.Copy))

            def block(e, a, g, k):
                s_t.wait(act, g, 0)
                s_m1.wait(act, g, -1)
                s_xh.done(act.activation(XTH[:, :, :], xt, ACT.Copy))
                for f in range(FC):
                    s_m1.wait(act, g, f)
                    s_hl.wait(act, g, max(f - 4, -1))
                    s_gelu.done(act.activation(HF[:, f % 4, :], h_bank(f), ACT.Gelu, bias=B1[:, bass.ds(e * FC + f, 1)]))
            act.wait_ge(s_b1t, 1)
            act.activation(B1[:, :], xt_bank[:, 0:E * FC], ACT.Copy).then_inc(s_b1, 1)
            act.wait_ge(s_b1, 1)
            each(act, expert, block)

        @blk.vector
        def _(dve):
            def expert(e, a, g):
                s_w1h.wait(dve, a, 0)
                s_w1l.done(dve.tensor_tensor(W1L[:, :, :], W1F[:, :, :], W1H[:, :, :].bitcast(F32), ALU.subtract))
                s_w2h.wait(dve, a, 0)
                s_w2l.done(dve.tensor_tensor(W2L[:, :, :], W2F[:, :, :], W2H[:, :, :].bitcast(F32), ALU.subtract))

            def block(e, a, g, k):
                s_xh.wait(dve, g, 0)
                s_xl.done(dve.tensor_tensor(XTL[:, :, :], xt, XTH[:, :, :].bitcast(F32), ALU.subtract))
                s_gk.wait(dve, g, 0)
                s_y.wait(dve, g, -1)
                for t in range(BT):
                    s_gate.done(dve.tensor_copy(GATES[:, t:t + 1], GK[:, t, bass.ds(e, 1)]))
                for f in range(FC):
                    s_gelu.wait(dve, g, f)
                    s_m2.wait(dve, g, max(f - 4, -1))
                    s_hh.done(dve.tensor_copy(HH[:, f % 4, :], HF[:, f % 4, :]))
                    s_hh.wait(dve, g, f)
                    s_hl.done(dve.tensor_tensor(HL[:, f % 4, :], HF[:, f % 4, :], HH[:, f % 4, :].bitcast(F32), ALU.subtract))
                s_sc.wait(dve, g, BT - 1)
                s_m2.wait(dve, g, FC - 1)
                for t in range(BT):
                    s_y.done(dve.tensor_tensor(YS[:, t, :], y_bank(t), B2[:, bass.ds(e, 1), :].rearrange("p a n -> p (a n)"), ALU.add))
                s_y.wait(dve, g, BT - 1)
                s_gate.wait(dve, g, BT - 1)
                for t in range(BT):
                    s_y.done(dve.tensor_scalar(YS[:, t, :], YS[:, t, :], GATES[:, t:t + 1], None, ALU.mult))
            dve.wait_ge(s_b, 32)
            each(dve, expert, block)

        @blk.tensor
        def _(pe):
            def block(e, a, g, k):
                s_gx.wait(pe, g, 0)
                s_xl.wait(pe, g, -1)
                for c in range(KC):
                    for t in range(BT):
                        last = pe.transpose(xt_bank[:, c * BLK + t * P:c * BLK + (t + 1) * P], XG[:, t, c * P:(c + 1) * P], IDENT[:, :])
                s_t.done(last)
                s_w1l.wait(pe, a, 0)
                s_xl.wait(pe, g, 0)

                def mm1(f):
                    s_gelu.wait(pe, g, max(f - 4, -1))
                    cols = slice(f * P, (f + 1) * P)
                    for c in range(KC):
                        last = hi_lo_matmul(pe, h_bank(f), (W1H[:, c, cols], W1L[:, c, cols]),
                                            (XTH[:, c, :], XTL[:, c, :]), c == 0, c == KC - 1)
                    s_m1.done(last)

                def mm2(f):
                    if f == 0:
                        s_w2l.wait(pe, a, 0)
                        s_y.wait(pe, g, -1)
                    s_hl.wait(pe, g, f)
                    for t in range(BT):
                        rows = slice(t * P, (t + 1) * P)
                        last = hi_lo_matmul(pe, y_bank(t), (HH[:, f % 4, rows], HL[:, f % 4, rows]),
                                            (W2H[:, f, :], W2L[:, f, :]), f == 0, f == FC - 1)
                    s_m2.done(last)
                for f in range(FC + 2):
                    if f < FC:
                        mm1(f)
                    if f >= 2:
                        mm2(f - 2)
            pe.wait_ge(s_b, 32)
            pe.transpose(xt_bank[:, 0:E * FC], B1R[:, :], IDENT[0:E * FC, 0:E * FC]).then_inc(s_b1t, 1)
            pe.wait_ge(s_b1, 1)
            each(pe, None, block)


def last_norm(nc, out, m, sem, sb):
    X1 = m["X1"]
    RING = 4
    A, XN, GBG = sb("A", [P, RING, TC, D]), sb("XN", [P, RING, TC, D]), sb("GBG", [P, NB, D])
    S6, MV = sb("S6", [P, RING, TC, 6]), sb("MV", [P, RING, TC, 2])
    VAR, Y, TMP, NMR = (sb(x, [P, RING, TC]) for x in ("VAR", "Yr", "TMP", "NMR"))
    GATE = sb("GATEt", [P, 2 * RING])
    OPS = 2 * TC + 15
    s_in = [Stream(sem(f"tin{r}"), 1, 16) for r in range(RING)]
    s_out = [Stream(sem(f"tout{r}"), 1, 16) for r in range(RING)]
    s_n, s_xn, s_mul, s_add = ([Stream(sem(f"{x}{r}"), per) for r in range(RING)] for x, per in (
        ("tn", OPS), ("txn", TC), ("tmul", 1), ("tadd", 1)))
    s_gbg = sem("tgbg")
    acc_rows = m["acc_dram"][0:NT, :].rearrange("(c p) n -> p c n", p=P)
    out_rows = out.rearrange("b (c p) n -> p (b c) n", p=P)
    with nc.Block() as block:
        @block.sync
        def _(sp):
            sp.dma_start(GBG[:, :, :], m["mod_dram"][:, 4, :].partition_broadcast(P)).then_inc(s_gbg, 16)
            with sp.Fori(0, NB // RING) as i:
                for r in range(RING):
                    row = sp.snap((i * RING + r) * TC)
                    s_xn[r].wait(sp, i, -1)
                    s_in[r].done(sp.dma_start(A[:, r, :, :], acc_rows[:, bass.ds(row, TC), :]))

        @block.vector
        def _(dve):
            dve.wait_ge(s_gbg, 16)
            with dve.Fori(0, NB // RING) as i:
                for r in range(RING):
                    k = [0]

                    def link(ins):
                        s_n[r].done(ins)
                        s_n[r].wait(dve, i, k[0])
                        k[0] += 1
                    s_in[r].wait(dve, i, 0)
                    s_xn[r].wait(dve, i, -1)
                    s_n[r].done(dve.memset(GATE[:, 2 * r:2 * r + 1], 0.0))
                    for c in range(TC):
                        s_n[r].done(dve.bn_stats(S6[:, r, c, :], A[:, r, c, :]))
                    k[0] += TC + 1
                    s_n[r].wait(dve, i, k[0] - 1)
                    s_n[r].done(dve.memset(GATE[:, 2 * r + 1:2 * r + 2], 0.0))
                    for c in range(TC):
                        s_n[r].done(dve.bn_aggr(MV[:, r, c, :], S6[:, r, c, :]))
                    k[0] += TC + 1
                    s_n[r].wait(dve, i, k[0] - 1)
                    rsqrt_and_shift(dve, link, MV[:, r, :, :], VAR[:, r, :], Y[:, r, :], TMP[:, r, :], NMR[:, r, :])
                    assert k[0] == OPS
                    s_xn[r].wait(dve, i, TC - 1)
                    s_mul[r].done(dve.tensor_tensor(XN[:, r, :, :], XN[:, r, :, :], GBG[:, bass.ds(i * RING + r, 1), :].broadcast_to([P, TC, D]),
                                                 ALU.mult))

        @block.scalar
        def _(act):
            with act.Fori(0, NB // RING) as i:
                for r in range(RING):
                    s_n[r].wait(act, i, OPS - 1)
                    s_add[r].wait(act, i, -1)
                    for c in range(TC):
                        s_xn[r].done(act.activation(XN[:, r, c, :], A[:, r, c, :], ACT.Identity, scale=Y[:, r, c:c + 1],
                                                 bias=NMR[:, r, c:c + 1]))

        @block.gpsimd
        def _(pool):
            with pool.Fori(0, NB // RING) as i:
                for r in range(RING):
                    row = pool.snap((i * RING + r) * TC)
                    s_mul[r].wait(pool, i, 0)
                    x = X1[:, bass.ds(row, TC), :]
                    s_add[r].done(pool.tensor_tensor(x, x, XN[:, r, :, :], ALU.add))
                    s_add[r].wait(pool, i, 0)
                    s_out[r].wait(pool, i, -1)
                    s_out[r].done(pool.dma_start(out_rows[:, bass.ds(row, TC), :], x))
            for r in range(RING):
                s_out[r].wait(pool, NB // RING - 1, 0)


def kernel(**inputs):
    import numpy as np
    import concourse.bacc as bacc
    from concourse.bass_utils import run_bass_kernel_spmd as run

    nc = bacc.Bacc("TRN2", target_bir_lowering=False, num_devices=1)
    arrays, aps = {}, {}
    for name, value in inputs.items():
        arrays[f"in_{name}"] = np.ascontiguousarray(value)
        aps[name] = nc.dram_tensor(f"in_{name}", arrays[f"in_{name}"].shape, mybir.dt.from_np(arrays[f"in_{name}"].dtype),
                                   kind="ExternalInput").ap()
    out = nc.dram_tensor("out_x", (NB, T, D), F32, kind="ExternalOutput").ap()
    build_program(nc, aps, out)
    return run(nc, [arrays], core_ids=[0]).results[0]["out_x"]
```

```python
from contextlib import ExitStack

import concourse.bass as bass
from concourse import mybir

F32, F32R = mybir.dt.float32, mybir.dt.float32r
U32, I32 = mybir.dt.uint32, mybir.dt.int32
ALU, ACT, AX = mybir.AluOpType, mybir.ActivationFunctionType, mybir.AxisListType

P = 128
NB, T, D = 16, 512, 256
H, R = 8, 64
KC = D // P
TC = T // P
NT = NB * T
NCH = NT // P
E, F = 8, 1024
CAP = -(-NT * 5 // (E * 4))
BLK = 256
EPS = 1e-5
UNITS = H * TC
RSQRT_SEED, RSQRT_OPS = 0x5F3759DF, 13


class Stream:

    def __init__(self, sem, per, step, base):
        self.sem, self.per, self.step, self.base = sem, per, step, base

    def done(self, ins):
        ins.then_inc(self.sem, self.step)

    def wait(self, eng, b, k):
        value = b * (self.per * self.step) + (k + 1) * self.step + self.base
        if not isinstance(value, int) or value > self.base:
            eng.wait_ge(self.sem, value)


def start(eng, streams):
    for stream in streams:
        if stream.base:
            eng.sem_inc(stream.sem, stream.base)


def snap(eng, x):
    return x if isinstance(x, int) else eng.snap(x)


class PairStream:

    def __init__(self, sem, parity):
        self.sem, self.parity = sem, parity

    def done(self, ins):
        ins.then_inc(self.sem, 16)

    def wait(self, eng, b):
        eng.wait_ge(self.sem, b * 8 + (16 - 8 * self.parity))


class Chain:

    def __init__(self, eng, sem):
        self.eng, self.sem, self.n = eng, sem, 0

    def __call__(self, ins):
        ins.then_inc(self.sem, 1)
        self.n += 1
        self.eng.wait_ge(self.sem, self.n)


def hi_lo_matmul(eng, out, lhs, rhs, first=True, last=True):
    eng.matmul(out, lhs[0], rhs[0], start=first, stop=False)
    eng.matmul(out, lhs[0], rhs[1], start=False, stop=False)
    return eng.matmul(out, lhs[1], rhs[0], start=False, stop=last)


def rsqrt_and_shift(dve, mv, v, y, t, nmr):
    newton = [
        lambda: dve.tensor_tensor(t, y, y, ALU.mult),
        lambda: dve.scalar_tensor_tensor(out=t, in0=t, scalar=-0.5, in1=v, op0=ALU.mult, op1=ALU.mult),
        lambda: dve.scalar_tensor_tensor(out=y, in0=t, scalar=1.5, in1=y, op0=ALU.add, op1=ALU.mult)]
    return [
        lambda: dve.tensor_scalar(v, mv[:, :, 1], EPS, None, ALU.add),
        lambda: dve.tensor_scalar(t.bitcast(U32), v.bitcast(U32), 1, None, ALU.logical_shift_right),
        lambda: dve.tensor_scalar(y.bitcast(U32), t.bitcast(U32), -1.0, float(RSQRT_SEED), ALU.mult, ALU.add),
        *newton, *newton, *newton,
        lambda: dve.scalar_tensor_tensor(out=nmr, in0=mv[:, :, 0], scalar=-1.0, in1=y, op0=ALU.mult, op1=ALU.mult)]


def build_program(nc, ap, out):
    top = ExitStack()
    with top:
        def sb(name, shape, dt=F32, ctx=top):
            return ctx.enter_context(nc.sbuf_tensor(name, shape, dt))

        def sem(name, ctx=top):
            return ctx.enter_context(nc.semaphore(name))

        PS = top.enter_context(nc.psum_tensor("PS", [P, 8, 512], F32))
        h2_dram = nc.dram_tensor("h2_rows", [NT + P, D], F32).ap()
        acc_dram = nc.dram_tensor("acc_rows", [NT + P, D], F32).ap()
        mod_dram = nc.dram_tensor("mod_rows", [NB, 5, D], F32).ap()
        ktab_dram = nc.dram_tensor("key_rows", [NT + P, E], F32).ap()
        m = dict(ktab_dram=ktab_dram, PS=PS, h2_dram=h2_dram, acc_dram=acc_dram, mod_dram=mod_dram)
        m["X1"] = sb("X1", [P, NCH, D])
        m["IDENT"] = sb("IDENT", [P, P])
        m["LOGITS"] = sb("LOGITS", [P, NCH, E])
        with ExitStack() as attn:
            def sba(name, shape, dt=F32):
                return sb(name, shape, dt, attn)
            for k, shape, dt in (
                    ("AH", [P, KC, H * R], F32R), ("AL", [P, KC, H * R], F32R),
                    ("DH", [P, KC, 2 * R], F32R), ("DL", [P, KC, 2 * R], F32R),
                    ("GH", [P, H // 2, D], F32R), ("GL", [P, H // 2, D], F32R),
                    ("WR", [P, KC, E], F32), ("BR", [P, E], F32),
                    ("SA", [P, KC, NB], F32), ("CA1", [P, KC, NB], F32)):
                m[k] = sba(k, shape, dt)
            setup(nc, ap, m, sem)
            attention(nc, ap, m, sem, sba)
        m["IDX"] = sb("IDX", [P, E * CAP // P], U32)
        m["INFO"] = sb("INFO", [1, 4 * E], I32)
        for phase in (route, experts):
            with ExitStack() as tiles:
                phase(nc, ap, m, sem, lambda name, shape, dt=F32: sb(name, shape, dt, tiles))
        with ExitStack() as tiles:
            last_norm(nc, out, m, sem, lambda name, shape, dt=F32: sb(name, shape, dt, tiles))


def setup(nc, ap, m, sem):
    PS, IDENT = m["PS"], m["IDENT"]
    with ExitStack() as ctx:
        def sb(name, shape, dt=F32):
            return ctx.enter_context(nc.sbuf_tensor(name, shape, dt))

        C = sb("C", [NB, D]); SG = sb("SG", [NB, D]); ST = sb("STc", [P, KC, NB])
        WM = sb("WM", [P, KC, 6 * D])
        WQ = sb("WQ", [R, H, D]); WK = sb("WK", [R, H, R]); WV = sb("WV", [R, H, R])
        WO = sb("WO", [P, KC, H * R]); WOT = sb("WOT", [R, H, D]); WD = sb("WD", [R, D])
        GB = sb("GBs", [NB, 2, D])
        MR = sb("MR", [NB, 5, D])
        MA = sb("MA", [NB, 2, D]); ZERO = sb("ZERO", [P, D])
        s_in, s_w, s_id, s_out = (sem(x) for x in ("s_in", "s_w", "s_id", "s_setout"))
        s_pe, s_act, s_dve, s_mr = (sem(x) for x in ("s_setpe", "s_setact", "s_setdve", "s_mr"))
        MODS_DONE, AL_DONE = 13, 17
        PE_SILU_T, PE_MODT, PE_WDT, PE_A, PE_WOT, PE_G = 1, 3, 4, 5, 6, 7
        silu_ps = PS[:, 0, 0:KC * NB].rearrange("p (k b) -> p k b", k=KC)
        modt_ps = PS[:, 1, 0:4 * NB].rearrange("p (j b) -> p j b", j=4)
        wdt_ps = PS[:, 2, 0:KC * R].rearrange("p (k r) -> p k r", k=KC)
        with nc.Block() as block:
            @block.sync
            def _(sp):
                sp.dma_start(C[:, :], ap["L0_c"]).then_inc(s_in, 16)
                sp.dma_start(WM[:, :, :], ap["L0_wmod"].rearrange("(k p) n -> p k n", p=P)).then_inc(s_in, 16)
                for j, name in enumerate(("L0_ffn_gamma", "L0_ffn_beta")):
                    sp.dma_start(GB[:, j, :], ap[name].partition_broadcast(NB)).then_inc(s_in, 16)
                sp.dma_start(WD[:, :], ap["L0_attn_Wkv_down"]).then_inc(s_w, 16)
                sp.dma_start(WQ[:, :, :], ap["L0_attn_Wq"].rearrange("(h d) n -> d h n", h=H)).then_inc(s_w, 16)
                sp.dma_start(WK[:, :, :], ap["L0_attn_Wk_up"].rearrange("(h d) n -> d h n", h=H)).then_inc(s_w, 16)
                sp.dma_start(WV[:, :, :], ap["L0_attn_Wv_up"].rearrange("(h d) n -> d h n", h=H)).then_inc(s_w, 16)
                sp.dma_start(WO[:, :, :], ap["L0_attn_Wo"].rearrange("(k p) n -> p k n", p=P)).then_inc(s_w, 16)
                sp.dma_start(m["WR"][:, :, :], ap["L0_ffn_Wr"].rearrange("(k p) n -> p k n", p=P)).then_inc(s_w, 16)
                sp.dma_start(m["BR"][:, :], ap["L0_ffn_br"].partition_broadcast(P)).then_inc(s_w, 16)
                sp.wait_ge(s_mr, 1)
                sp.dma_start(m["mod_dram"], MR[:, :, :]).then_inc(s_out, 16)
                sp.wait_ge(s_id, 3)
                sp.dma_start(m["h2_dram"][NT:NT + P, :], ZERO[:, :]).then_inc(s_out, 16)
                sp.dma_start(m["acc_dram"][NT:NT + P, :], ZERO[:, :]).then_inc(s_out, 16)
                sp.wait_ge(s_out, 48)
                sp.wait_ge(s_w, 16 * 7)

            @block.gpsimd
            def _(pool):
                pool.memset(IDENT[:, :], 0.0).then_inc(s_id, 1)
                pool.wait_ge(s_id, 1)
                pool.affine_select(out=IDENT[:, :], in_=IDENT[:, :], compare_op=ALU.not_equal, fill=1.0, base=0,
                                   pattern=[[-1, P]], channel_multiplier=1).then_inc(s_id, 1)
                pool.memset(ZERO[:, :], 0.0).then_inc(s_id, 1)

            @block.scalar
            def _(act):
                act.wait_ge(s_in, 64)
                act.activation(SG[:, :], C[:, :], ACT.Silu).then_inc(s_act, 1)
                act.wait_ge(s_pe, PE_WDT)
                for j in range(2):
                    act.activation(m["DH"][:, :, j * R:(j + 1) * R], wdt_ps, ACT.Copy).then_inc(s_act, 1)
                act.wait_ge(s_pe, PE_A)
                for k in range(KC):
                    act.activation(m["AH"][:, k, :], PS[:, 3 + k, :], ACT.Copy, scale=float(R) ** -0.5).then_inc(s_act, 1)
                act.wait_ge(s_pe, PE_WOT)
                for j in range(4):
                    act.activation(WOT[:, 2 * j:2 * j + 2, :], PS[0:R, 4 + j, :].rearrange("p (h n) -> p h n", h=2),
                                   ACT.Copy).then_inc(s_act, 1)
                act.wait_ge(s_pe, PE_G)
                for j in range(4):
                    for odd in range(2):
                        act.activation(m["GH"][odd * R:(odd + 1) * R, j, :], PS[0:R, j, odd * D:(odd + 1) * D],
                                       ACT.Copy).then_inc(s_act, 1)
            SILU, DH_DONE, AH_DONE, WOT_DONE, GH_DONE = 1, 3, 5, 9, 17

            @block.tensor
            def _(pe):
                pe.wait_ge(s_id, 2)
                pe.wait_ge(s_act, SILU)
                for k in range(KC):
                    last = pe.transpose(silu_ps[:, k, :], SG[:, k * P:(k + 1) * P], IDENT[0:NB, 0:NB])
                last.then_inc(s_pe, 1)
                pe.wait_ge(s_dve, 1)
                for j in range(3):
                    for k in range(KC):
                        last = pe.matmul(PS[0:NB, 5 + j, :], ST[:, k, :], WM[:, k, j * 512:(j + 1) * 512],
                                         start=(k == 0), stop=(k == KC - 1))
                last.then_inc(s_pe, 1)
                for j in range(4):
                    for k in range(KC):
                        last = pe.matmul(modt_ps[:, j, :], WM[:, k, j * P:(j + 1) * P], ST[:, k, :],
                                         start=(k == 0), stop=(k == KC - 1))
                last.then_inc(s_pe, 1)
                pe.wait_ge(s_w, 16 * 7)
                for k in range(KC):
                    last = pe.transpose(wdt_ps[:, k, :], WD[:, k * P:(k + 1) * P], IDENT[0:R, 0:R])
                last.then_inc(s_pe, 1)
                for k in range(KC):
                    for h in range(H):
                        last = pe.matmul(PS[:, 3 + k, h * R:(h + 1) * R], WQ[:, h, k * P:(k + 1) * P], WK[:, h, :],
                                         start=True, stop=True)
                last.then_inc(s_pe, 1)
                pe.wait_ge(s_dve, MODS_DONE)
                pe.wait_ge(s_act, AH_DONE)
                pe.wait_ge(s_dve, AL_DONE)
                for h in range(H):
                    for k in range(KC):
                        last = pe.transpose(PS[0:R, 4 + h // 2, (h % 2) * D + k * P:(h % 2) * D + (k + 1) * P],
                                            WO[:, k, h * R:(h + 1) * R], IDENT[:, :])
                last.then_inc(s_pe, 1)
                pe.wait_ge(s_act, WOT_DONE)
                for h in range(H):
                    last = pe.matmul(PS[0:R, h // 2, (h % 2) * D:(h % 2 + 1) * D], WV[:, h, :], WOT[:, h, :],
                                     start=True, stop=True)
                last.then_inc(s_pe, 1)
            @block.vector
            def _(dve):
                chain = Chain(dve, s_dve)
                dve.wait_ge(s_pe, PE_SILU_T)
                chain(dve.tensor_copy(ST[:, :, :], silu_ps))
                dve.wait_ge(s_pe, PE_MODT)
                chain(dve.tensor_copy(m["SA"][:, :, :], modt_ps[:, 0:2, :]))
                chain(dve.tensor_scalar(m["CA1"][:, :, :], modt_ps[:, 2:4, :], 1.0, None, ALU.add))
                for j, src in enumerate((PS[0:NB, 6, 0:D], PS[0:NB, 7, D:2 * D])):
                    sign, g = MA[:, j, :], MR[:, 4 * j, :]
                    chain(dve.tensor_scalar(sign, src, 0.0, 2.0, ALU.is_ge, ALU.mult))
                    chain(dve.tensor_scalar(sign, sign, -1.0, None, ALU.add))
                    chain(dve.tensor_tensor(g, src, sign, ALU.mult))
                    chain(dve.scalar_tensor_tensor(out=g, in0=g, scalar=0.25, in1=sign, op0=ALU.max, op1=ALU.mult))
                chain(dve.tensor_scalar(MR[:, 1, :], PS[0:NB, 7, 0:D], 1.0, None, ALU.add))
                chain(dve.tensor_copy(MR[:, 2, :], PS[0:NB, 6, D:2 * D]))
                dve.wait_ge(s_act, DH_DONE)
                for j in range(2):
                    chain(dve.tensor_tensor(m["DL"][:, :, j * R:(j + 1) * R], wdt_ps,
                                            m["DH"][:, :, j * R:(j + 1) * R].bitcast(F32), ALU.subtract))
                dve.wait_ge(s_act, AH_DONE)
                for k in range(KC):
                    chain(dve.scalar_tensor_tensor(out=m["AL"][:, k, :], in0=PS[:, 3 + k, :], scalar=float(R) ** -0.5,
                                                   in1=m["AH"][:, k, :].bitcast(F32), op0=ALU.mult,
                                                   op1=ALU.subtract))
                chain(dve.tensor_tensor(MR[:, 3, :], MR[:, 4, :], GB[:, 1, :], ALU.mult))
                dve.tensor_tensor(MR[:, 4, :], MR[:, 4, :], GB[:, 0, :], ALU.mult).then_inc(s_mr, 1)
                dve.wait_ge(s_act, GH_DONE)
                for j in range(4):
                    for odd in range(2):
                        chain(dve.tensor_tensor(m["GL"][odd * R:(odd + 1) * R, j, :], PS[0:R, j, odd * D:(odd + 1) * D],
                                                m["GH"][odd * R:(odd + 1) * R, j, :].bitcast(F32), ALU.subtract))


def attention(nc, ap, m, sem, sb):
    PS, IDENT, X1, LOGITS = m["PS"], m["IDENT"], m["X1"], m["LOGITS"]
    AH, AL, DH, DL, GH, GL, WR, BR = (m[k] for k in ("AH", "AL", "DH", "DL", "GH", "GL", "WR", "BR"))
    x_rows = ap["L0_attn_x"].rearrange("b (c p) n -> p (b c) n", p=P)
    NHI, NLO = sb("NHI", [P, KC, T], F32R), sb("NLO", [P, KC, T], F32R)
    MODB = sb("MODB", [P, 4, D])
    K1, K2 = sb("K1", [P, 2, T], F32R), sb("K2", [P, 2, T], F32R)
    V1, V2 = sb("V1", [P, 2, TC, 2 * R], F32R), sb("V2", [P, 2, TC, 2 * R], F32R)
    Q1, Q2 = sb("Q1", [P, H, T], F32R), sb("Q2", [P, H, T], F32R)
    NMAX, MROW = sb("NMAX", [P, 2, TC]), sb("MROW", [TC, 2, P], F32R)
    PF, PH, PL = sb("PF", [P, 2, T]), sb("PH", [P, 4, T], F32R), sb("PL", [P, 4, T], F32R)
    RECT, RDEN = sb("RECT", [R, T]), sb("RDEN", [R, T // 32])
    XF = sb("XF", [P, 2, T])
    XH, XL = sb("XH", [P, H // 2, T], F32R), sb("XL", [P, H // 2, T], F32R)
    XN1, LTF, H2 = sb("XN1", [P, TC, D]), sb("LTF", [P, T]), sb("H2", [P, TC, D])
    TR = sb("TR", [P, KC * T])
    NF = TR[:, :].rearrange("p (k n) -> p k n", k=KC)
    H2T = TR[:, :].rearrange("p (c k n) -> p c k n", c=TC, k=KC)
    YT, GATE = sb("YT", [P, 2, D]), sb("GATE", [P, 16])
    norm = [dict(s6=sb(f"s6_{j}", [P, TC, 6]), mv=sb(f"mv_{j}", [P, TC, 2]), v=sb(f"v_{j}", [P, TC]),
                 y=sb(f"y_{j}", [P, TC]), t=sb(f"t_{j}", [P, TC]), nmr=sb(f"nmr_{j}", [P, TC])) for j in range(2)]

    streams = []

    def S(name, per, step=1, base=1):
        streams.append(Stream(sem(name), per, step, base))
        return streams[-1]

    s_st, s_mx, s_pv = S("st", UNITS), S("mx", UNITS), S("pv", UNITS)
    s_mt, s_q, s_proj, s_n1t, s_lat, s_vt, s_h2t, s_lg = (
        S("mt", H), S("q", 4), S("proj", TC), S("n1t", KC), S("lat", 1), S("vt", 1), S("h2t", TC), S("lg", 1))
    s_exp, s_qhi, s_latc, s_vhi, s_nf = S("exp", 2 * UNITS), S("qhi", 16), S("latc", 3), S("vhi", 1), S("nf", KC)
    s_xn1, s_xn2, s_h2c, s_xhi = S("xn1", TC), S("xn2", TC), S("h2c", TC), S("xhi", H // 2)
    s_mred, s_mrow, s_x, s_qlo, s_nhl, s_klo, s_vlo = (
        S("mred", UNITS), S("mrow", H), S("x", 4 * H), S("qlo", 8), S("nhl", 2 * KC), S("klo", 1), S("vlo", 1))
    s_y, s_x1, s_lgc, s_xlo = S("y", TC), S("x1", TC), S("lgc", 1), S("xlo", H // 2)
    NORM_OPS = 2 * TC + RSQRT_OPS
    s_norm = [S("norm1", NORM_OPS), S("norm2", NORM_OPS)]
    s_plo, s_hmul, s_hadd, s_gbb = S("plo", UNITS), S("hmul", TC), S("hadd", TC), S("gbb", TC)
    s_xin = [PairStream(sem(f"xin{j}"), j) for j in range(2)]
    s_modin = [PairStream(sem(f"modin{j}"), j) for j in range(2)]
    s_mdma, s_h2out = S("mdma", H, 16), S("h2out", 2, 16)
    s_const = sem("s_attn_const")

    def st_bank(n):
        return PS[:, n % 2, :]

    def mx_bank(n):
        return PS[:, 2 + n % 2, :]

    def pv_bank(h):
        return PS[:, 4 + h % 2, :]

    AHEAD = 10

    JOBS = {3: [("mrow", 2, 0)], 7: [("mrow", 3, 0)], 11: [("mrow", 4, 0)], 15: [("mrow", 5, 0)],
            19: [("mrow", 6, 0)], 23: [("mrow", 7, 0), ("q", 2, 1)], 27: [("mrow", 0, 1)], 31: [("mrow", 1, 1), ("q", 3, 1)],
            5: [("n1t", 0, 1)], 12: [("n1t", 1, 1)], 14: [("lat", 0, 1)], 17: [("q", 0, 1), ("vt", 0, 1)], 20: [("q", 1, 1)],
            6: [("proj", 0, -1)], 8: [("proj", 1, -1)], 9: [("proj", 2, -1)], 10: [("proj", 3, -1)],
            22: [("h2t", 0, -1)], 25: [("h2t", 1, -1)], 26: [("h2t", 2, -1)], 28: [("h2t", 3, -1)], 29: [("lg", 0, -1)]}
    ORDER = [j for n in range(UNITS) for j in JOBS.get(n, [])]
    LAG = {"mrow": 1, "proj": 1, "q": 2, "n1t": 1, "lat": 2, "vt": 1, "lg": 1, "h2t": 0}
    banks, free = {}, [-1, -1]
    for n, jobs in sorted(JOBS.items()):
        for job in jobs:
            banks[job] = min(x for x in (0, 1) if free[x] <= n)
            free[banks[job]] = n + LAG[job[0]] + 1
    FREED = {"mrow": (s_mrow, 1), "proj": (s_y, 1), "q": (s_qlo, 2), "n1t": (s_nf, 1), "lat": (s_klo, 1),
             "vt": (s_vlo, 1), "h2t": (s_h2c, 1), "lg": (s_lgc, 1)}

    def at_slot(job):
        return next(n for n, jobs in JOBS.items() if job in jobs)

    def exists(b):
        return not isinstance(b, int) or 0 <= b < NB

    def job_bank(job):
        return PS[:, 6 + banks[job], :]

    def wait_job_bank(eng, b, job):
        at = ORDER.index(job) - 1
        while True:
            kind, idx, off = ORDER[at % len(ORDER)]
            bb = b + at // len(ORDER) + off
            if isinstance(bb, int) and bb < 0 and at < -len(ORDER):
                return
            if banks[kind, idx, off] == banks[job] and exists(bb):
                stream, each = FREED[kind]
                stream.wait(eng, bb, idx * each + each - 1)
                return
            at -= 1

    def unit(b, n):
        return b + n // UNITS, n % UNITS

    def batches(eng, body, looped=NB - 4):
        for b in (-2, -1, 0):
            body(b, b % 2)
        with eng.Fori(0, looped // 2) as i:
            for j in range(2):
                body(i * 2 + (1 + j), (1 + j) % 2)
        for b in range(1 + looped, NB + 1):
            body(b, b % 2)

    with nc.Block() as block:
        @block.sync
        def _(sp):
            def load_x(b, par, row):
                sp.dma_start(X1[:, bass.ds(row, TC), :], x_rows[:, bass.ds(row, TC), :]
                             ).then_inc(s_xin[par].sem, 16)

            def body(b, par):
                if isinstance(b, int) and b == -2:
                    sp.wait_ge(s_const, 5)
                    load_x(0, 0, 0)
                    load_x(1, 1, TC)
                elif exists(b + 3):
                    row = snap(sp, (b + 3) * TC)
                    s_norm[0].wait(sp, b + 1, 2 * TC - 1)
                    load_x(b + 3, 1 - par, row)
                for n in range(UNITS):
                    if n % 4 == 3:
                        tb, h = unit(b, n + 5)
                        h = h // TC
                        if exists(tb):
                            s_mrow.wait(sp, tb, h)
                            s_mdma.done(sp.dma_start(Q2[R:R + 1, h, :].bitcast(F32), MROW[:, h % 2, :].bitcast(F32)))
                    if n == 31 and exists(b):
                        row = snap(sp, b + 0)
                        s_gbb.wait(sp, b - 1, TC - 1)
                        sp.dma_start(MODB[:, :, :], m["mod_dram"][bass.ds(row, 1), 0:4, :].rearrange("a j n -> (a j) n").partition_broadcast(P)
                                     ).then_inc(s_modin[par].sem, 16)

            batches(sp, body)

        @block.gpsimd
        def _(pool):
            for i, (part, value) in enumerate(((K2[R:P, :, :], 0.0), (K2[R:R + 1, :, :], 1.0), (Q2[R:P, :, :], 0.0),
                                               (V1[:, :, :, R:2 * R], 1.0), (V2[:, :, :, R:2 * R], 0.0))):
                pool.memset(part.bitcast(F32), value).then_inc(s_const, 1)
                pool.wait_ge(s_const, i + 1)
            start(pool, streams)

            def body(b, par):
                for n in range(UNITS):
                    tb, u = unit(b, n + 1)
                    if exists(tb):
                        s_exp.wait(pool, tb, 2 * u + 1)
                        s_pv.wait(pool, tb, u - 4)
                        s_plo.done(pool.tensor_tensor(PL[:, u % 4, :], PF[:, u % 2, :], PH[:, u % 4, :].bitcast(F32),
                                                      ALU.subtract))
                    pb, pp = b - 1, 1 - par
                    if exists(pb):
                        if 18 <= n < 26:
                            c = (n - 18) // 2
                            if n % 2 == 0:
                                s_xn2.wait(pool, pb, c)
                                s_hmul.done(pool.tensor_tensor(H2[:, c, :], H2[:, c, :], MODB[:, 1, :], ALU.mult))
                            else:
                                s_hmul.wait(pool, pb, c)
                                s_hadd.done(pool.tensor_tensor(H2[:, c, :], H2[:, c, :], MODB[:, 2, :], ALU.add))
                        if 26 <= n < 30:
                            c = n - 26
                            x = X1[:, bass.ds(pb * TC + c, 1), :].rearrange("p c n -> p (c n)")
                            s_gbb.done(pool.tensor_tensor(x, x, MODB[:, 3, :], ALU.add))

            batches(pool, body)

        @block.scalar
        def _(act):
            def body(b, par):
                for n in range(UNITS):
                    tb, u = unit(b, n + 1)
                    if exists(tb):
                        s_st.wait(act, tb, u)
                        s_pv.wait(act, tb, u - 4)
                        s_exp.done(act.activation(PH[:, u % 4, :], st_bank(u), ACT.Exp))
                        s_plo.wait(act, tb, u - 2)
                        s_exp.done(act.activation(PF[:, u % 2, :], st_bank(u), ACT.Exp))
                    for job in JOBS.get(n, []):
                        kind, idx, off = job
                        jb = b + off
                        if not exists(jb):
                            continue
                        bank = job_bank(job)
                        jp = (par + off) % 2
                        if kind == "q":
                            s_q.wait(act, jb, idx)
                            s_st.wait(act, jb - 1, 8 * idx + 7)
                            for odd in range(2):
                                for half in range(2):
                                    s_qhi.done(act.activation(Q1[half * R:(half + 1) * R, 2 * idx + odd, :],
                                                              bank[odd * R:(odd + 1) * R, :], ACT.Copy))
                        elif kind == "lat":
                            s_lat.wait(act, jb, 0)
                            s_st.wait(act, jb - 2, UNITS - 1)
                            s_latc.done(act.activation(K1[0:R, jp, :], bank[0:R, :], ACT.Copy))
                            s_latc.done(act.activation(K2[0:R, jp, :], bank[0:R, :], ACT.Copy))
                            s_vt.wait(act, jb - 1, 0)
                            s_latc.done(act.activation(LTF[:, :], bank, ACT.Copy))
                        elif kind == "vt":
                            s_vt.wait(act, jb, 0)
                            s_pv.wait(act, jb - 2, UNITS - 1)
                            s_vhi.done(act.activation(V1[:, jp, :, 0:R],
                                                      bank.rearrange("p (c r) -> p c r", c=TC)[:, :, 0:R], ACT.Copy))
                        elif kind == "n1t":
                            s_n1t.wait(act, jb, idx)
                            s_nhl.wait(act, jb - 1, 2 * idx + 1)
                            s_lg.wait(act, jb - 3, 0)
                            s_nf.done(act.activation(NF[:, idx, :], bank, ACT.Identity,
                                                     bias=m["SA"][:, idx, bass.ds(jb, 1)], scale=m["CA1"][:, idx, bass.ds(jb, 1)]))
                        elif kind == "h2t":
                            s_h2t.wait(act, jb, idx)
                            s_lg.wait(act, jb - 1, 0)
                            if exists(jb + 2):
                                s_nhl.wait(act, jb + 2, 2 * KC - 1)
                            s_h2c.done(act.activation(H2T[:, idx, :, :], bank[:, 0:D].rearrange("p (k n) -> p k n", k=KC),
                                                      ACT.Copy))
                    if n == 30 and exists(b - 1):
                        row = snap(act, (b - 1) * T)
                        s_hadd.wait(act, b - 1, TC - 1)
                        for dram in (m["h2_dram"], m["acc_dram"]):
                            rows = dram[bass.ds(row, T), :].rearrange("(c p) n -> p c n", p=P)
                            s_h2out.done(act.dma_start(rows, H2[:, :, :]))
                    if n < 4 and exists(b + 1):
                        c = n
                        s_norm[0].wait(act, b + 1, NORM_OPS - 1)
                        s_n1t.wait(act, b, 1)
                        s_xn1.done(act.activation(XN1[:, c, :], X1[:, bass.ds((b + 1) * TC + c, 1), :].rearrange("p c n -> p (c n)"),
                                                  ACT.Identity, scale=norm[0]["y"][:, c:c + 1], bias=norm[0]["nmr"][:, c:c + 1]))
                    if n in (17, 18) and exists(b - 1):
                        for c in (2 * n - 34, 2 * n - 33):
                            s_norm[1].wait(act, b - 1, NORM_OPS - 1)
                            s_h2out.wait(act, b - 2, 1)
                            s_h2t.wait(act, b - 2, TC - 1)
                            s_xn2.done(act.activation(H2[:, c, :], X1[:, bass.ds((b - 1) * TC + c, 1), :].rearrange("p c n -> p (c n)"),
                                                      ACT.Identity, scale=norm[1]["y"][:, c:c + 1], bias=norm[1]["nmr"][:, c:c + 1]))
                    if n % 8 == 4:
                        xb, p = (b, n // 8 - 1) if n > 4 else (b - 1, 3)
                        if exists(xb):
                            s_x.wait(act, xb, 4 * (2 * p + 1) + 3)
                            s_proj.wait(act, xb - 1, TC - 1)
                            s_xhi.done(act.activation(XH[:, p, :], XF[:, p % 2, :], ACT.Copy))

            batches(act, body)
            s_h2out.wait(act, NB - 1, 1)

        @block.vector
        def _(dve):
            def gate(which, c):
                dve.memset(GATE[:, which * 8 + c:which * 8 + c + 1], 0.0)

            def norm_stats(which, nb, chunks):
                w, st = norm[which], s_norm[which]
                if chunks[0] == 0:
                    st.wait(dve, nb, -1)
                gate(which, chunks[0])
                for c in chunks:
                    st.done(dve.bn_stats(w["s6"][:, c, :], X1[:, bass.ds(nb * TC + c, 1), :].rearrange("p c n -> p (c n)")))
                st.wait(dve, nb, 2 * chunks[0] + len(chunks) - 1)
                gate(which, 4 + chunks[0])
                for c in chunks:
                    st.done(dve.bn_aggr(w["mv"][:, c, :], w["s6"][:, c, :]))

            pending = []

            def step():
                if pending:
                    pending.pop(0)()

            def norm_scale(which, nb):
                w, st = norm[which], s_norm[which]

                def queue(k, issue):
                    def go():
                        if k == 2 * TC:
                            (s_xn1, s_xn2)[which].wait(dve, nb - 1, TC - 1)
                        st.wait(dve, nb, k - 1)
                        st.done(issue())
                    pending.append(go)
                for k, issue in enumerate(rsqrt_and_shift(dve, w["mv"][:, :, :], *(w[x][:, :] for x in ("v", "y", "t", "nmr")))):
                    queue(2 * TC + k, issue)

            def normalise(b, n, place):
                xb, h = (b, (n - 5) // 4) if n >= 5 else (b - 1, H - 1)
                part = (n - 1) % 4
                if n == 0 or not exists(xb):
                    return
                bank, p, odd = pv_bank(h), h // 2, h % 2
                if (part, place) == (0, 1):
                    s_pv.wait(dve, xb, TC * h + TC - 1)
                    s_x.wait(dve, xb, 4 * h - 1)
                    s_x.done(dve.transpose(RECT[:, :], bank[R:P, :]))
                elif (part, place) == (1, 0):
                    s_x.wait(dve, xb, 4 * h)
                    s_x.done(dve.reciprocal(RDEN[:, :], RECT[:, :].rearrange("p (g j) -> p g j", j=32)[:, :, 0]))
                elif (part, place) == (1, 1):
                    s_x.wait(dve, xb, 4 * h + 1)
                    s_x.done(dve.transpose(RECT[:, :], RDEN[:, :].unsqueeze(2).broadcast_to([R, T // 32, 32])))
                elif (part, place) == (2, 0):
                    s_x.wait(dve, xb, 4 * h + 2)
                    if odd == 0:
                        s_xhi.wait(dve, xb, p - 2)
                        s_xlo.wait(dve, xb, p - 2)
                    s_x.done(dve.tensor_tensor(XF[odd * R:(odd + 1) * R, p % 2, :], bank[0:R, :], RECT[:, :], ALU.mult))

            def body(b, par):
                pb, pp, nb = b - 1, 1 - par, b + 2
                for n in range(UNITS):
                    normalise(b, n, 0)
                    step()
                    tb, u = unit(b, n + AHEAD)
                    if exists(tb):
                        h, c = u // TC, u % TC
                        s_mx.wait(dve, tb, u)
                        if c == 0:
                            s_mt.wait(dve, tb, h - 2)
                        s_mred.done(dve.tensor_reduce(NMAX[:, h % 2, c:c + 1], mx_bank(u), AX.X, ALU.max, negate=True))
                    normalise(b, n, 1)
                    step()
                    if n % 8 == 5:
                        xb, p = (b, n // 8 - 1) if n > 5 else (b - 1, 3)
                        if exists(xb):
                            s_xhi.wait(dve, xb, p)
                            s_xlo.done(dve.tensor_tensor(XL[:, p, :], XF[:, p % 2, :], XH[:, p, :].bitcast(F32), ALU.subtract))
                    for job in [x for x in ORDER if (at_slot(x) + LAG[x[0]]) % UNITS == n]:
                        kind, idx, off = job
                        jb = b + off - (at_slot(job) + LAG[kind]) // UNITS
                        if not exists(jb):
                            continue
                        bank = job_bank(job)
                        jp = (par + off + (at_slot(job) + LAG[kind]) // UNITS) % 2
                        if kind == "mrow":
                            s_mt.wait(dve, jb, idx)
                            s_mdma.wait(dve, jb, idx - 2)
                            s_mrow.done(dve.tensor_copy(MROW[:, idx % 2, :], bank[0:TC, 0:P]))
                        elif kind == "q":
                            for odd in range(2):
                                s_qhi.wait(dve, jb, 4 * idx + 2 * odd + 1)
                                h = 2 * idx + odd
                                s_qlo.done(dve.tensor_tensor(Q2[0:R, h, :], bank[odd * R:(odd + 1) * R, :],
                                                             Q1[odd * R:(odd + 1) * R, h, :].bitcast(F32), ALU.subtract))
                        elif kind == "proj":
                            s_modin[pp].wait(dve, jb)
                            s_proj.wait(dve, jb, idx)
                            s_x1.wait(dve, jb, idx - 1)
                            s_y.done(dve.tensor_tensor(YT[:, idx % 2, :], bank[:, 0:D], MODB[:, 0, :], ALU.mult))
                            s_y.wait(dve, jb, idx)
                            x = X1[:, bass.ds(jb * TC + idx, 1), :].rearrange("p c n -> p (c n)")
                            s_x1.done(dve.tensor_tensor(x, YT[:, idx % 2, :], x, ALU.add))
                            s_x1.wait(dve, jb, idx)
                            norm_stats(1, jb, [idx])
                        elif kind == "n1t":
                            s_nf.wait(dve, jb, idx)
                            s_q.wait(dve, jb - 1, 3)
                            s_nhl.done(dve.tensor_copy(NHI[:, idx, :], NF[:, idx, :]))
                            s_nhl.wait(dve, jb, 2 * idx)
                            s_nhl.done(dve.tensor_tensor(NLO[:, idx, :], NF[:, idx, :], NHI[:, idx, :].bitcast(F32),
                                                         ALU.subtract))
                        elif kind == "lat":
                            s_latc.wait(dve, jb, 2)
                            s_klo.done(dve.tensor_tensor(K1[R:P, jp, :], bank[R:P, :], K1[0:R, jp, :].bitcast(F32), ALU.subtract))
                        elif kind == "vt":
                            s_vhi.wait(dve, jb, 0)
                            s_vlo.done(dve.tensor_tensor(V2[:, jp, :, 0:R], bank.rearrange("p (c r) -> p c r", c=TC)[:, :, 0:R],
                                                         V1[:, jp, :, 0:R].bitcast(F32), ALU.subtract))
                        elif kind == "lg":
                            s_lg.wait(dve, jb, idx)
                            s_lgc.done(dve.tensor_tensor(
                                LOGITS[:, bass.ds(jb * TC, TC), :], bank[:, 0:TC * E].rearrange("p (c e) -> p c e", c=TC),
                                BR[:, :].unsqueeze(1).broadcast_to([P, TC, E]), ALU.add))
                    step()
                    if n in (18, 20, 22, 24) and exists(nb):
                        if n == 18:
                            s_xin[par].wait(dve, nb)
                        norm_stats(0, nb, [(n - 18) // 2])
                    if n == 26 and exists(nb):
                        norm_scale(0, nb)
                    if n == 13 and exists(pb):
                        norm_scale(1, pb)
                    step()

            batches(dve, body)

        @block.tensor
        def _(pe):
            pe.wait_ge(s_const, 5)

            def body(b, par):
                for n in range(UNITS):
                    tb, u = unit(b, n + 1)
                    if exists(tb):
                        h, c, kp = u // TC, u % TC, (par + (n + 1) // UNITS) % 2
                        s_exp.wait(pe, tb, 2 * (u - 2) + 1)
                        if c == 0:
                            s_mdma.wait(pe, tb, h)
                            s_qlo.wait(pe, tb, h)
                        keys = slice(c * P, (c + 1) * P)
                        pe.matmul(st_bank(u), K1[:, kp, keys], Q1[:, h, :], start=True, stop=False)
                        s_st.done(pe.matmul(st_bank(u), K2[:, kp, keys], Q2[:, h, :], start=False, stop=True))
                    tb, u = unit(b, n + AHEAD)
                    if exists(tb):
                        h, c, kp = u // TC, u % TC, (par + (n + AHEAD) // UNITS) % 2
                        s_mred.wait(pe, tb, u - 2)
                        if c == 0:
                            s_qlo.wait(pe, tb, h)
                            s_klo.wait(pe, tb, 0)
                        s_mx.done(pe.matmul(mx_bank(u), Q1[:, h, c * P:(c + 1) * P], K1[:, kp, :], start=True, stop=True))
                    for job in JOBS.get(n, []):
                        kind, idx, off = job
                        jb = b + off
                        if not exists(jb):
                            continue
                        wait_job_bank(pe, b, job)
                        bank = job_bank(job)
                        jp = (par + off) % 2
                        if kind == "mrow":
                            s_mred.wait(pe, jb, TC * idx + TC - 1)
                            s_mt.done(pe.transpose(bank[0:TC, 0:P], NMAX[:, idx % 2, :], IDENT[:, :]))
                        elif kind == "q":
                            s_nhl.wait(pe, jb, 3)
                            cols = slice(2 * idx * R, 2 * (idx + 1) * R)
                            for k in range(KC):
                                last = hi_lo_matmul(pe, bank, (AH[:, k, cols], AL[:, k, cols]),
                                                    (NHI[:, k, :], NLO[:, k, :]), k == 0, k == KC - 1)
                            s_q.done(last)
                        elif kind == "lat":
                            s_nhl.wait(pe, jb, 3)
                            for k in range(KC):
                                last = hi_lo_matmul(pe, bank, (DH[:, k, :], DL[:, k, :]),
                                                    (NHI[:, k, :], NLO[:, k, :]), k == 0, k == KC - 1)
                            s_lat.done(last)
                        elif kind == "vt":
                            s_latc.wait(pe, jb, 2)
                            for c in range(TC):
                                last = pe.transpose(bank[:, c * P:(c + 1) * P], LTF[:, c * P:(c + 1) * P], IDENT[:, :])
                            s_vt.done(last)
                        elif kind == "n1t":
                            s_xn1.wait(pe, jb, TC - 1)
                            for c in range(TC):
                                last = pe.transpose(bank[:, c * P:(c + 1) * P], XN1[:, c, idx * P:(idx + 1) * P], IDENT[:, :])
                            s_n1t.done(last)
                        elif kind == "proj":
                            s_xhi.wait(pe, jb, 3)
                            s_xlo.wait(pe, jb, 3)
                            rows = slice(idx * P, (idx + 1) * P)
                            for p in range(H // 2):
                                last = hi_lo_matmul(pe, bank[:, 0:D], (XH[:, p, rows], XL[:, p, rows]),
                                                    (GH[:, p, :], GL[:, p, :]), p == 0, p == H // 2 - 1)
                            s_proj.done(last)
                        elif kind == "h2t":
                            s_hadd.wait(pe, jb, idx)
                            for k in range(KC):
                                last = pe.transpose(bank[:, k * P:(k + 1) * P], H2[:, idx, k * P:(k + 1) * P], IDENT[:, :])
                            s_h2t.done(last)
                        elif kind == "lg":
                            s_h2c.wait(pe, jb, TC - 1)
                            for c in range(TC):
                                for k in range(KC):
                                    last = pe.matmul(bank[:, c * E:(c + 1) * E], H2T[:, c, k, :], WR[:, k, :],
                                                     start=(k == 0), stop=(k == KC - 1))
                            s_lg.done(last)
                    tb, u = unit(b, n - 1)
                    if exists(tb):
                        h, c, vp = u // TC, u % TC, (par + (n - 1) // UNITS) % 2
                        if c == 0:
                            s_x.wait(pe, tb, 4 * (h - 2) + 3)
                            s_vlo.wait(pe, tb, 0)
                        s_exp.wait(pe, tb, 2 * u)
                        bank = pv_bank(h)
                        pe.matmul(bank, V1[:, vp, c, :], PH[:, u % 4, :], start=(c == 0), stop=False)
                        pe.matmul(bank, V2[:, vp, c, :], PH[:, u % 4, :], start=False, stop=False)
                        s_plo.wait(pe, tb, u)
                        s_pv.done(pe.matmul(bank, V1[:, vp, c, :], PL[:, u % 4, :], start=False, stop=(c == TC - 1)))

            batches(pe, body)


def route(nc, ap, m, sem, sb):
    PS, IDENT, LOGITS = m["PS"], m["IDENT"], m["LOGITS"]
    NS = NCH // TC
    BIG = 127 * P
    SLOTC = E * CAP // P
    RING = 8
    EQ, OH1, OH2, L2 = (sb(x, [P, NCH, E]) for x in ("EQ", "OH1", "OH2", "L2"))
    KEY = sb("KEY", [P, TC, NS, E])
    M1, M2, I1, I2, EX, W1, W2, DEN = (sb(x, [P, NCH]) for x in ("M1", "M2", "I1", "I2", "EX", "W1", "W2", "DENr"))
    RANK8 = sb("RANK8", [P, E])
    KT, JUNK, GT, EQT, SEL, SCAN, DST, ZT = (sb(x, [P, T]) for x in ("KT", "JUNK", "GT", "EQT", "SEL", "SCAN", "DST", "ZT"))
    DIFF, DIFM = sb("DIFF", [P, P], I32), sb("DIFM", [P, P], I32)
    SAME, LOWER, ONES = sb("SAME", [P, P]), sb("LOWER", [P, P]), sb("ONES", [P, P])
    BITU, BITF = sb("BITU", [P, 31], U32), sb("BITF", [P, 31])
    CAND, FOUND, INC = sb("CAND", [P, 1], U32), sb("FOUND", [P, 1], U32), sb("INC", [P, 1], U32)
    CNT = sb("CNT", [P, 8])
    ECOLI, ECOL = sb("ECOLI", [P, 1], I32), sb("ECOL", [P, 1])
    D1, D12 = sb("D1", [P, NCH]), sb("D12", [P, 2, NCH])
    DI, AI, BI = (sb(x, [P, 2 * NCH], U32) for x in ("DI", "AI", "BI"))
    AF, BF = sb("AF", [P, 2 * NCH]), sb("BF", [P, 2 * NCH])
    TOK1, IOT = sb("TOK1", [P, 2, NCH]), sb("IOT", [P, P])
    OB, OA, ZP = sb("OB", [P, RING, P]), sb("OA", [P, RING, SLOTC]), sb("ZP", [P, P])
    SPARE, LF = sb("SPARE", [P, 1]), sb("LF", [P, SLOTC])
    NBR, NBD = sb("NBR", [1, 6, E]), sb("NBD", [P, E])
    ktab = m["ktab_dram"]
    s_pool, s_dve, s_exp, s_key, s_tab = (sem(x) for x in ("s_rpool", "s_rdve", "s_rexp", "s_rkey", "s_rtab"))
    s_kt, s_sum, s_cnt, s_tot, s_dt = (sem(x) for x in ("s_rkt", "s_rsum", "s_rcnt", "s_rtot", "s_rdt"))
    s_ob, s_oa, s_mm, s_list, s_nb, s_dd = (sem(x) for x in ("s_rob", "s_roa", "s_rmm", "s_rlist", "s_rnb", "s_rdd"))
    s_db, s_ab = sem("s_rdb"), sem("s_rab")
    NBITS = 30
    POOL_CONSTS, MASKS_DONE = 7 + 2 * NBITS + 4, 3
    kt_ps = PS[:, 0, :]
    cnt_ps, off_ps, tot_ps = PS[:, 1, 0:1], PS[:, 2, 0:1], PS[:, 3, 0:1]
    dt_ps = PS[:, 4, :]
    list_ps, nb_ps = PS[:, 5, 0:SLOTC], PS[:, 6, 0:E]

    def by_expert(x):
        return x.unsqueeze(2).broadcast_to([P, NCH, E])

    with nc.Block() as block:
        @block.gpsimd
        def _(pool):
            n = [0]

            def link(ins):
                ins.then_inc(s_pool, 1)
                n[0] += 1
                pool.wait_ge(s_pool, n[0])
            link(pool.iota(RANK8[:, :], pattern=[[-1, E]], base=E, channel_multiplier=0, allow_small_or_imprecise_dtypes=True))
            link(pool.iota(DIFF[:, :], pattern=[[1, P]], base=P, channel_multiplier=-1))
            link(pool.iota(ECOLI[:, :], pattern=[[0, 1]], base=0, channel_multiplier=1))
            link(pool.iota(IOT[:, :], pattern=[[1, P]], base=0, channel_multiplier=0, allow_small_or_imprecise_dtypes=True))
            link(pool.iota(SPARE[:, :], pattern=[[0, 1]], base=NT + 1, channel_multiplier=1, allow_small_or_imprecise_dtypes=True))
            for j in range(2):
                link(pool.iota(TOK1[:, j, :].rearrange("p (a b) -> p a b", a=TC), pattern=[[P, TC], [TC * P, NS]], base=1,
                               channel_multiplier=1, allow_small_or_imprecise_dtypes=True))
            for k in range(NBITS):
                pool.memset(BITU[:, k:k + 1], 1 << (NBITS - 1 - k)).then_inc(s_pool, 1)
                pool.memset(BITF[:, k:k + 1], float(1 << (NBITS - 1 - k))).then_inc(s_pool, 1)
            pool.memset(BITU[:, NBITS:], 0).then_inc(s_pool, 1)
            pool.memset(ZT[:, :], 0.0).then_inc(s_pool, 1)
            pool.memset(ZP[:, :], 0.0).then_inc(s_pool, 1)
            pool.memset(ONES[:, :], 1.0).then_inc(s_pool, 1)

        @block.scalar
        def _(act):
            act.wait_ge(s_dd, 1)
            act.activation(EX[:, :], DEN[:, :], ACT.Exp).then_inc(s_exp, 1)
            act.wait_ge(s_kt, 1)
            act.activation(KT[:, :], kt_ps, ACT.Copy).then_inc(s_exp, 1)

        @block.sync
        def _(sp):
            sp.wait_ge(s_key, TC)
            rows = ktab[0:NT, :].rearrange("(c q p) e -> q p c e", p=P, q=TC)
            for q in range(TC):
                sp.dma_start(rows[q], KEY[:, q, :, :]).then_inc(s_tab, 16)
            sp.wait_ge(s_pool, POOL_CONSTS)
            sp.dma_start(ktab[NT:NT + P, :], ZP[:, 0:E]).then_inc(s_tab, 16)
            sp.wait_ge(s_tab, 16 * (TC + 1))

        @block.tensor
        def _(pe):
            pe.wait_ge(s_key, TC)
            for q in range(TC):
                last = pe.transpose(kt_ps[:, q * P:(q + 1) * P], KEY[:, q, :, :].rearrange("p c e -> p (c e)"), IDENT[:, :])
            last.then_inc(s_kt, 1)
            pe.wait_ge(s_dve, MASKS_DONE)
            with pe.Fori(0, NBITS) as i:
                pe.wait_ge(s_cnt, i + 1)
                pe.matmul(cnt_ps, SAME[:, :], CNT[:, 0:1], start=True, stop=True).then_inc(s_sum, 1)
            pe.wait_ge(s_tot, 1)
            pe.matmul(tot_ps, SAME[:, :], CNT[:, 1:2], start=True, stop=True)
            pe.matmul(off_ps, LOWER[:, :], CNT[:, 2:3], start=True, stop=True).then_inc(s_sum, 1)
            pe.wait_ge(s_tot, 2)
            pe.matmul(tot_ps, SAME[:, :], CNT[:, 3:4], start=True, stop=True)
            pe.matmul(off_ps, LOWER[:, :], CNT[:, 3:4], start=True, stop=True).then_inc(s_sum, 1)
            pe.wait_ge(s_tot, 3)
            for q in range(TC):
                last = pe.transpose(dt_ps[:, q * P:(q + 1) * P], DST[:, q * P:(q + 1) * P], IDENT[:, :])
            last.then_inc(s_dt, 1)
            pe.matmul(nb_ps, ONES[:, :], NBD[:, :], start=True, stop=True).then_inc(s_nb, 1)
            pe.wait_ge(s_pool, POOL_CONSTS)
            for r in range(RING):
                pe.matmul(list_ps, ZP[:, :], ZP[:, 0:SLOTC], start=(r == 0), stop=False).then_inc(s_mm, 1)
            with pe.Fori(0, 2 * NCH // RING) as i:
                pe.wait_ge(s_oa, i + 1)
                for r in range(RING):
                    pe.wait_ge(s_ob, i * RING + (r + 1))
                    pe.matmul(list_ps, OB[:, r, :], OA[:, r, :], start=False, stop=False).then_inc(s_mm, 1)
            pe.matmul(list_ps, ZP[:, :], ZP[:, 0:SLOTC], start=False, stop=True).then_inc(s_list, 1)

        @block.vector
        def _(dve):
            n = [0]

            def link(ins):
                ins.then_inc(s_dve, 1)
                n[0] += 1
                dve.wait_ge(s_dve, n[0])
            dve.wait_ge(s_pool, POOL_CONSTS)
            link(dve.tensor_scalar(DIFM[:, :], DIFF[:, :], E - 1, None, ALU.bitwise_and))
            link(dve.tensor_scalar(SAME[:, :], DIFM[:, :], 0.0, None, ALU.is_equal))
            link(dve.scalar_tensor_tensor(out=LOWER[:, :], in0=DIFF[:, :], scalar=float(P), in1=SAME[:, :],
                                          op0=ALU.is_gt, op1=ALU.mult))
            rank8 = RANK8[:, :].unsqueeze(1).broadcast_to([P, NCH, E])
            link(dve.tensor_reduce(M1[:, :], LOGITS[:, :, :], AX.X, ALU.max))
            link(dve.tensor_tensor(EQ[:, :, :], LOGITS[:, :, :], by_expert(M1[:, :]), ALU.is_equal))
            link(dve.tensor_tensor(EQ[:, :, :], EQ[:, :, :], rank8, ALU.mult))
            link(dve.tensor_reduce(I1[:, :], EQ[:, :, :], AX.X, ALU.max))
            link(dve.tensor_tensor(OH1[:, :, :], rank8, by_expert(I1[:, :]), ALU.is_equal))
            link(dve.scalar_tensor_tensor(out=L2[:, :, :], in0=OH1[:, :, :], scalar=-3.0e38, in1=LOGITS[:, :, :],
                                          op0=ALU.mult, op1=ALU.add))
            link(dve.tensor_reduce(M2[:, :], L2[:, :, :], AX.X, ALU.max))
            link(dve.tensor_tensor(DEN[:, :], M2[:, :], M1[:, :], ALU.subtract))
            dve.sem_inc(s_dd, 1)
            link(dve.tensor_tensor(EQ[:, :, :], L2[:, :, :], by_expert(M2[:, :]), ALU.is_equal))
            link(dve.tensor_tensor(EQ[:, :, :], EQ[:, :, :], rank8, ALU.mult))
            link(dve.tensor_reduce(I2[:, :], EQ[:, :, :], AX.X, ALU.max))
            link(dve.tensor_tensor(OH2[:, :, :], rank8, by_expert(I2[:, :]), ALU.is_equal))
            dve.wait_ge(s_exp, 1)
            link(dve.tensor_scalar(DEN[:, :], EX[:, :], 1.0, None, ALU.add))
            link(dve.reciprocal(W1[:, :], DEN[:, :]))
            link(dve.tensor_tensor(W2[:, :], EX[:, :], W1[:, :], ALU.mult))
            link(dve.tensor_tensor(EQ[:, :, :], OH1[:, :, :], OH2[:, :, :], ALU.add))
            link(dve.tensor_tensor(OH1[:, :, :], OH1[:, :, :], by_expert(W1[:, :]), ALU.mult))
            link(dve.tensor_tensor(OH2[:, :, :], OH2[:, :, :], by_expert(W2[:, :]), ALU.mult))
            link(dve.tensor_tensor(OH1[:, :, :], OH1[:, :, :], OH2[:, :, :], ALU.add))
            for q in range(TC):
                dve.scalar_tensor_tensor(out=KEY[:, q, :, :], in0=EQ[:, q::TC, :], scalar=-1.0, in1=OH1[:, q::TC, :],
                                         op0=ALU.add, op1=ALU.add).then_inc(s_key, 1)
            link(dve.memset(FOUND[:, :], 0))
            dve.tensor_copy(CAND[:, :].bitcast(F32), BITU[:, 0:1].bitcast(F32)).then_inc(s_db, 1)
            dve.wait_ge(s_exp, 2)
            with dve.Fori(0, NBITS) as i:
                dve.wait_ge(s_db, i + 1)
                dve.tensor_scalar(JUNK[:, :], KT[:, :], CAND[:, :].bitcast(F32), None, ALU.is_ge, ALU.add,
                                  accum_out=CNT[:, 0:1]).then_inc(s_cnt, 1)
                dve.wait_ge(s_sum, i + 1)
                dve.tensor_scalar(INC[:, :], cnt_ps, float(CAP), BITF[:, bass.ds(i, 1)], ALU.is_ge, ALU.mult).then_inc(s_ab, 1)
                dve.wait_ge(s_ab, i * 2 + 1)
                dve.tensor_tensor(FOUND[:, :], FOUND[:, :], INC[:, :], ALU.bitwise_or).then_inc(s_ab, 1)
                dve.wait_ge(s_ab, i * 2 + 2)
                dve.tensor_tensor(CAND[:, :], FOUND[:, :], BITU[:, bass.ds(i + 1, 1)], ALU.bitwise_or).then_inc(s_db, 1)
            dve.wait_ge(s_db, NBITS + 1)
            thr = FOUND[:, :].bitcast(F32)
            link(dve.tensor_scalar(GT[:, :], KT[:, :], thr, None, ALU.is_gt, ALU.add, accum_out=CNT[:, 1:2]))
            link(dve.tensor_scalar(EQT[:, :], KT[:, :], thr, None, ALU.is_equal, ALU.add, accum_out=CNT[:, 2:3]))
            dve.sem_inc(s_tot, 1)
            link(dve.tensor_tensor_scan(SCAN[:, :], EQT[:, :], ZT[:, :], 0.0, ALU.add, ALU.add))
            link(dve.tensor_scalar(ECOLI[:, :], ECOLI[:, :], E - 1, None, ALU.bitwise_and))
            link(dve.tensor_scalar(ECOL[:, :], ECOLI[:, :], float(CAP), float(-1 - BIG), ALU.mult, ALU.add))
            dve.wait_ge(s_sum, NBITS + 1)
            link(dve.tensor_scalar(CNT[:, 4:5], tot_ps, -1.0, float(CAP), ALU.mult, ALU.add))
            link(dve.tensor_tensor(CNT[:, 4:5], CNT[:, 4:5], off_ps, ALU.subtract))
            link(dve.scalar_tensor_tensor(out=SEL[:, :], in0=SCAN[:, :], scalar=CNT[:, 4:5], in1=EQT[:, :],
                                          op0=ALU.is_le, op1=ALU.mult))
            link(dve.tensor_tensor(SEL[:, :], SEL[:, :], GT[:, :], ALU.add))
            link(dve.tensor_reduce(CNT[:, 3:4], SEL[:, :], AX.X, ALU.add))
            dve.sem_inc(s_tot, 1)
            link(dve.tensor_tensor_scan(SCAN[:, :], SEL[:, :], ZT[:, :], 0.0, ALU.add, ALU.add))
            dve.wait_ge(s_sum, NBITS + 2)
            link(dve.tensor_tensor(CNT[:, 5:6], ECOL[:, :], off_ps, ALU.add))
            link(dve.scalar_tensor_tensor(out=DST[:, :], in0=SCAN[:, :], scalar=CNT[:, 5:6], in1=SEL[:, :],
                                          op0=ALU.add, op1=ALU.mult))
            link(dve.tensor_scalar(CNT[:, 6:7], tot_ps, 0.0, None, ALU.is_gt))
            for j in range(1, -(-CAP // BLK)):
                link(dve.scalar_tensor_tensor(out=CNT[:, 6:7], in0=tot_ps, scalar=float(j * BLK), in1=CNT[:, 6:7],
                                              op0=ALU.is_gt, op1=ALU.add))
            link(dve.tensor_scalar(NBD[:, :], IDENT[:, 0:E], CNT[:, 6:7], None, ALU.mult))
            dve.sem_inc(s_tot, 1)
            dve.wait_ge(s_nb, 1)
            nb, act_, cum, cua, z = (NBR[:, j, :] for j in range(5))
            link(dve.tensor_copy(nb, nb_ps[0:1, :]))
            link(dve.tensor_scalar(act_, nb, 0.0, None, ALU.is_gt))
            link(dve.memset(z, 0.0))
            link(dve.tensor_tensor_scan(cum, nb, z, 0.0, ALU.add, ALU.add))
            link(dve.tensor_tensor_scan(cua, act_, z, 0.0, ALU.add, ALU.add))
            link(dve.tensor_tensor(cum, cum, nb, ALU.subtract))
            link(dve.tensor_tensor(cua, cua, act_, ALU.subtract))
            for j, row in enumerate((nb, cum, cua)):
                link(dve.tensor_copy(m["INFO"][:, j * E:(j + 1) * E], row))
            dve.wait_ge(s_dt, 1)
            by_tok = dt_ps.rearrange("p (n e) -> p n e", e=E)
            link(dve.tensor_reduce(D12[:, 0, :], by_tok, AX.X, ALU.min))
            link(dve.tensor_tensor(EQ[:, :, :], by_tok, by_expert(D12[:, 0, :]), ALU.is_equal))
            link(dve.scalar_tensor_tensor(out=EQ[:, :, :], in0=EQ[:, :, :], scalar=float(BIG), in1=by_tok,
                                          op0=ALU.mult, op1=ALU.add))
            link(dve.tensor_reduce(D12[:, 1, :], EQ[:, :, :], AX.X, ALU.min))
            link(dve.tensor_scalar(DI[:, :], D12[:, :, :].rearrange("p j n -> p (j n)"), float(BIG), None, ALU.add))
            link(dve.tensor_scalar(AI[:, :], DI[:, :], 7, None, ALU.logical_shift_right))
            link(dve.tensor_scalar(BI[:, :], DI[:, :], P - 1, None, ALU.bitwise_and))
            link(dve.tensor_copy(BF[:, :], BI[:, :]))
            link(dve.tensor_copy(AF[:, :], AI[:, :]))
            dve.sem_inc(s_dd, 1)
            with dve.Fori(0, 2 * NCH // RING) as i:
                dve.wait_ge(s_mm, (i + 1) * RING)
                dve.tensor_tensor(OA[:, :, :], IOT[:, 0:SLOTC].unsqueeze(1).broadcast_to([P, RING, SLOTC]),
                                  AF[:, bass.ds(i * RING, RING)].unsqueeze(2).broadcast_to([P, RING, SLOTC]),
                                  ALU.is_equal).then_inc(s_oa, 1)
                for r in range(RING):
                    dve.wait_ge(s_mm, i * RING + (r + 1))
                    col = bass.ds(i * RING + r, 1)
                    dve.tensor_scalar(OB[:, r, :], IOT[:, :], BF[:, col], TOK1[:, :, :].rearrange("p j n -> p (j n)")[:, col],
                                      ALU.is_equal, ALU.mult).then_inc(s_ob, 1)
            dve.wait_ge(s_list, 1)
            link(dve.tensor_scalar(LF[:, :], list_ps, 0.0, SPARE[:, :], ALU.is_equal, ALU.mult))
            link(dve.scalar_tensor_tensor(out=m["IDX"][:, :], in0=list_ps, scalar=-1.0, in1=LF[:, :], op0=ALU.add, op1=ALU.add))




def experts(nc, ap, m, sem, sb):
    PS, IDENT, IDX, INFO = m["PS"], m["IDENT"], m["IDX"], m["INFO"]
    FC, BT = F // P, BLK // P
    MAXB = CAP // BLK
    GATES_USED = 4 + BT
    assert CAP % BLK == 0
    W1F, W2F = sb("W1F", [P, KC, F]), sb("W2F", [P, FC, D])
    W1H, W1L = sb("W1H", [P, KC, F], F32R), sb("W1L", [P, KC, F], F32R)
    W2H, W2L = sb("W2H", [P, FC, D], F32R), sb("W2L", [P, FC, D], F32R)
    B1R, B1, B2 = sb("B1R", [E * FC, P]), sb("B1", [P, E * FC]), sb("B2", [P, E, D])
    XG, GK, TOKG, TOKS = sb("XG", [P, BT, D]), sb("GK", [P, BT, E]), sb("TOKG", [P, BT], U32), sb("TOKS", [P, BT], U32)
    XTH, XTL = sb("XTH", [P, KC, BLK], F32R), sb("XTL", [P, KC, BLK], F32R)
    HF, HH, HL = sb("HF", [P, 4, BLK]), sb("HH", [P, 4, BLK], F32R), sb("HL", [P, 4, BLK], F32R)
    YS, GATES, GATE = sb("YS", [P, BT, D]), sb("GATES", [P, BT]), sb("GATEp", [P, GATES_USED + 1])

    streams = []

    def S(name, per, step=1, base=1):
        streams.append(Stream(sem(name), per, step, base))
        return streams[-1]
    s_w1, s_w2 = S("fw1", 1, 16), S("fw2", 1, 16)
    s_w1h, s_w2h, s_w1l, s_w2l = S("fw1h", 1), S("fw2h", 1), S("fw1l", 1), S("fw2l", 1)
    s_gx, s_gk, s_sc = S("fgx", 1, 16 * BT, 0), S("fgk", 1, 16 * BT, 0), S("fsc", BT, 16, 0)
    s_tokg, s_toks = S("ftokg", BT), S("ftoks", 1)
    s_t, s_m1, s_m2, s_gate = S("ft", 1), S("fm1", FC), S("fm2", FC), S("fgate", BT)
    s_xh, s_xl, s_gelu, s_hh, s_hl, s_y = S("fxh", 1), S("fxl", 1), S("fgelu", FC), S("fhh", FC), S("fhl", FC), S("fy", 2 * BT)
    s_init, s_b, s_b1t, s_b1 = sem("finit"), sem("fb"), sem("fb1t"), sem("fb1")
    xt_bank = PS[:, 0, :]
    xt = xt_bank.rearrange("p (k n) -> p k n", k=KC)

    def h_bank(f):
        return PS[:, 1 + f % 4, 0:BLK]

    def y_bank(t):
        return PS[:, 5 + t, 0:D]

    def each(eng, expert, block):
        with eng.Fori(0, E) as e:
            nb = eng.value_load(INFO[0:1, bass.ds(e, 1)], min_val=0, max_val=MAXB)
            g0 = eng.value_load(INFO[0:1, bass.ds(e + E, 1)], min_val=0, max_val=E * MAXB)
            a = eng.value_load(INFO[0:1, bass.ds(e + 2 * E, 1)], min_val=0, max_val=E)
            with eng.If(nb > 0):
                if expert is not None:
                    expert(e, a, g0)
                if block is not None:
                    with eng.Fori(0, nb) as k:
                        block(e, a, g0 + k, k)

    with nc.Block() as blk:
        @blk.sync
        def _(sp):
            w1 = ap["L0_ffn_W1"].rearrange("e (k p) f -> p (e k) f", p=P)
            w2 = ap["L0_ffn_W2"].rearrange("e (f p) n -> p (e f) n", p=P)
            sp.dma_start(B1R[:, :], ap["L0_ffn_b1"].rearrange("e (f p) -> (e f) p", p=P)).then_inc(s_b, 16)
            sp.dma_start(B2[:, :, :], ap["L0_ffn_b2"].partition_broadcast(P)).then_inc(s_b, 16)

            def expert(e, a, g):
                k_row, f_row = sp.snap(e * KC), sp.snap(e * FC)
                s_w1l.wait(sp, a, -1)
                s_w1.done(sp.dma_start(W1F[:, :, :], w1[:, bass.ds(k_row, KC), :]))
                s_w2l.wait(sp, a, -1)
                s_w2.done(sp.dma_start(W2F[:, :, :], w2[:, bass.ds(f_row, FC), :]))
            each(sp, expert, None)

        @blk.gpsimd
        def _(pool):
            start(pool, streams)
            pool.iota(TOKS[:, :].bitcast(I32), pattern=[[0, BT]], base=NT, channel_multiplier=1).then_inc(s_init, 1)
            pool.memset(YS[:, :, :], 0.0).then_inc(s_init, 1)
            pool.memset(GATE[:, :], 0.0).then_inc(s_init, 1)
            pool.wait_ge(s_init, 3)

            def gate(j):
                pool.tensor_tensor(GATE[:, j:j + 1], GATE[:, GATES_USED:], GATE[:, GATES_USED:], ALU.add)

            def scatter(g):
                s_y.wait(pool, g, -1)
                for t in range(BT):
                    if t:
                        s_sc.wait(pool, g, t - 1)
                    gate(4 + t)
                    off = bass.IndirectOffsetOnAxis(ap=TOKS[:, t:t + 1], axis=0)
                    s_sc.done(pool.indirect_dma_start(out=m["acc_dram"], out_offset=off, in_=YS[:, t, :], in_offset=None,
                                                      compute_op=ALU.add))

            def block(e, a, g, k):
                s_toks.wait(pool, g, -1)
                gate(0)
                for t in range(BT):
                    s_tokg.done(pool.tensor_copy(TOKG[:, t:t + 1], IDX[:, bass.ds(e * (CAP // P) + k * BT + t, 1)]))
                s_tokg.wait(pool, g, BT - 1)
                s_t.wait(pool, g, -1)
                gate(1)
                for t in range(BT):
                    off = bass.IndirectOffsetOnAxis(ap=TOKG[:, t:t + 1], axis=0)
                    pool.indirect_dma_start(out=XG[:, t, :], out_offset=None, in_=m["h2_dram"], in_offset=off).then_inc(s_gx.sem, 16)
                s_gate.wait(pool, g, -1)
                gate(2)
                for t in range(BT):
                    off = bass.IndirectOffsetOnAxis(ap=TOKG[:, t:t + 1], axis=0)
                    pool.indirect_dma_start(out=GK[:, t, :], out_offset=None, in_=m["ktab_dram"], in_offset=off).then_inc(s_gk.sem, 16)
                scatter(g)
                s_sc.wait(pool, g, BT - 1)
                gate(3)
                s_toks.done(pool.tensor_copy(TOKS[:, :], TOKG[:, :]))
            each(pool, None, block)
            total = (pool.value_load(INFO[0:1, E - 1:E], min_val=0, max_val=MAXB)
                     + pool.value_load(INFO[0:1, 2 * E - 1:2 * E], min_val=0, max_val=E * MAXB))
            s_toks.wait(pool, total, -1)
            scatter(total)
            s_sc.wait(pool, total, BT - 1)

        @blk.scalar
        def _(act):
            def expert(e, a, g):
                s_w1.wait(act, a, 0)
                s_m2.wait(act, g, -1)
                s_w1h.done(act.activation(W1H[:, :, :], W1F[:, :, :], ACT.Copy))
                s_w2.wait(act, a, 0)
                s_w2h.done(act.activation(W2H[:, :, :], W2F[:, :, :], ACT.Copy))

            def block(e, a, g, k):
                s_t.wait(act, g, 0)
                s_m1.wait(act, g, -1)
                s_xh.done(act.activation(XTH[:, :, :], xt, ACT.Copy))
                for f in range(FC):
                    s_m1.wait(act, g, f)
                    s_hl.wait(act, g, max(f - 4, -1))
                    s_gelu.done(act.activation(HF[:, f % 4, :], h_bank(f), ACT.Gelu, bias=B1[:, bass.ds(e * FC + f, 1)]))
            act.wait_ge(s_b1t, 1)
            act.activation(B1[:, :], xt_bank[:, 0:E * FC], ACT.Copy).then_inc(s_b1, 1)
            act.wait_ge(s_b1, 1)
            each(act, expert, block)

        @blk.vector
        def _(dve):
            def expert(e, a, g):
                s_w1h.wait(dve, a, 0)
                s_w1l.done(dve.tensor_tensor(W1L[:, :, :], W1F[:, :, :], W1H[:, :, :].bitcast(F32), ALU.subtract))
                s_w2h.wait(dve, a, 0)
                s_w2l.done(dve.tensor_tensor(W2L[:, :, :], W2F[:, :, :], W2H[:, :, :].bitcast(F32), ALU.subtract))

            def block(e, a, g, k):
                s_xh.wait(dve, g, 0)
                s_xl.done(dve.tensor_tensor(XTL[:, :, :], xt, XTH[:, :, :].bitcast(F32), ALU.subtract))
                s_gk.wait(dve, g, 0)
                s_y.wait(dve, g, -1)
                for t in range(BT):
                    s_gate.done(dve.tensor_copy(GATES[:, t:t + 1], GK[:, t, bass.ds(e, 1)]))
                for f in range(FC):
                    s_gelu.wait(dve, g, f)
                    s_m2.wait(dve, g, max(f - 4, -1))
                    s_hh.done(dve.tensor_copy(HH[:, f % 4, :], HF[:, f % 4, :]))
                    s_hh.wait(dve, g, f)
                    s_hl.done(dve.tensor_tensor(HL[:, f % 4, :], HF[:, f % 4, :], HH[:, f % 4, :].bitcast(F32), ALU.subtract))
                s_sc.wait(dve, g, BT - 1)
                s_m2.wait(dve, g, FC - 1)
                for t in range(BT):
                    s_y.done(dve.tensor_tensor(YS[:, t, :], y_bank(t), B2[:, bass.ds(e, 1), :].rearrange("p a n -> p (a n)"), ALU.add))
                s_y.wait(dve, g, BT - 1)
                s_gate.wait(dve, g, BT - 1)
                for t in range(BT):
                    s_y.done(dve.tensor_scalar(YS[:, t, :], YS[:, t, :], GATES[:, t:t + 1], None, ALU.mult))
            dve.wait_ge(s_b, 32)
            each(dve, expert, block)

        @blk.tensor
        def _(pe):
            def block(e, a, g, k):
                s_gx.wait(pe, g, 0)
                s_xl.wait(pe, g, -1)
                for c in range(KC):
                    for t in range(BT):
                        last = pe.transpose(xt_bank[:, c * BLK + t * P:c * BLK + (t + 1) * P], XG[:, t, c * P:(c + 1) * P], IDENT[:, :])
                s_t.done(last)
                s_w1l.wait(pe, a, 0)
                s_xl.wait(pe, g, 0)

                def mm1(f):
                    s_gelu.wait(pe, g, max(f - 4, -1))
                    cols = slice(f * P, (f + 1) * P)
                    for c in range(KC):
                        last = hi_lo_matmul(pe, h_bank(f), (W1H[:, c, cols], W1L[:, c, cols]),
                                            (XTH[:, c, :], XTL[:, c, :]), c == 0, c == KC - 1)
                    s_m1.done(last)

                def mm2(f):
                    if f == 0:
                        s_w2l.wait(pe, a, 0)
                        s_y.wait(pe, g, -1)
                    s_hl.wait(pe, g, f)
                    for t in range(BT):
                        rows = slice(t * P, (t + 1) * P)
                        last = hi_lo_matmul(pe, y_bank(t), (HH[:, f % 4, rows], HL[:, f % 4, rows]),
                                            (W2H[:, f, :], W2L[:, f, :]), f == 0, f == FC - 1)
                    s_m2.done(last)
                for f in range(FC + 2):
                    if f < FC:
                        mm1(f)
                    if f >= 2:
                        mm2(f - 2)
            pe.wait_ge(s_b, 32)
            pe.transpose(xt_bank[:, 0:E * FC], B1R[:, :], IDENT[0:E * FC, 0:E * FC]).then_inc(s_b1t, 1)
            pe.wait_ge(s_b1, 1)
            each(pe, None, block)


def last_norm(nc, out, m, sem, sb):
    X1 = m["X1"]
    RING = 4
    A, XN, GBG = sb("A", [P, RING, TC, D]), sb("XN", [P, RING, TC, D]), sb("GBG", [P, NB, D])
    S6, MV = sb("S6", [P, RING, TC, 6]), sb("MV", [P, RING, TC, 2])
    VAR, Y, TMP, NMR = (sb(x, [P, RING, TC]) for x in ("VAR", "Yr", "TMP", "NMR"))
    GATE = sb("GATEt", [P, 2 * RING])
    OPS = 2 * TC + 2 + RSQRT_OPS
    streams = []

    def S(name, per, step=1, base=1):
        streams.append(Stream(sem(name), per, step, base))
        return streams[-1]
    s_in = [S(f"tin{r}", 1, 16) for r in range(RING)]
    s_n, s_xn, s_mul, s_add = ([S(f"{x}{r}", per) for r in range(RING)] for x, per in (
        ("tn", OPS), ("txn", TC), ("tmul", 1), ("tadd", 1)))
    s_gbg, s_out = sem("tgbg"), sem("tout")
    acc_rows = m["acc_dram"][0:NT, :].rearrange("(c p) n -> p c n", p=P)
    out_rows = out.rearrange("b (c p) n -> p (b c) n", p=P)
    with nc.Block() as block:
        @block.sync
        def _(sp):
            sp.dma_start(GBG[:, :, :], m["mod_dram"][:, 4, :].partition_broadcast(P)).then_inc(s_gbg, 16)
            with sp.Fori(0, NB // RING) as i:
                for r in range(RING):
                    row = sp.snap((i * RING + r) * TC)
                    s_xn[r].wait(sp, i, -1)
                    s_in[r].done(sp.dma_start(A[:, r, :, :], acc_rows[:, bass.ds(row, TC), :]))

        @block.vector
        def _(dve):
            dve.wait_ge(s_gbg, 16)
            with dve.Fori(0, NB // RING) as i:
                for r in range(RING):
                    k = [0]

                    def link(ins):
                        s_n[r].done(ins)
                        s_n[r].wait(dve, i, k[0])
                        k[0] += 1
                    s_in[r].wait(dve, i, 0)
                    s_xn[r].wait(dve, i, -1)
                    s_n[r].done(dve.memset(GATE[:, 2 * r:2 * r + 1], 0.0))
                    for c in range(TC):
                        s_n[r].done(dve.bn_stats(S6[:, r, c, :], A[:, r, c, :]))
                    k[0] += TC + 1
                    s_n[r].wait(dve, i, k[0] - 1)
                    s_n[r].done(dve.memset(GATE[:, 2 * r + 1:2 * r + 2], 0.0))
                    for c in range(TC):
                        s_n[r].done(dve.bn_aggr(MV[:, r, c, :], S6[:, r, c, :]))
                    k[0] += TC + 1
                    s_n[r].wait(dve, i, k[0] - 1)
                    for issue in rsqrt_and_shift(dve, MV[:, r, :, :], VAR[:, r, :], Y[:, r, :], TMP[:, r, :], NMR[:, r, :]):
                        link(issue())
                    assert k[0] == OPS
                    s_xn[r].wait(dve, i, TC - 1)
                    s_mul[r].done(dve.tensor_tensor(XN[:, r, :, :], XN[:, r, :, :], GBG[:, bass.ds(i * RING + r, 1), :].broadcast_to([P, TC, D]),
                                                 ALU.mult))

        @block.scalar
        def _(act):
            with act.Fori(0, NB // RING) as i:
                for r in range(RING):
                    s_n[r].wait(act, i, OPS - 1)
                    s_add[r].wait(act, i, -1)
                    for c in range(TC):
                        s_xn[r].done(act.activation(XN[:, r, c, :], A[:, r, c, :], ACT.Identity, scale=Y[:, r, c:c + 1],
                                                 bias=NMR[:, r, c:c + 1]))

        @block.gpsimd
        def _(pool):
            start(pool, streams)
            with pool.Fori(0, NB // RING) as i:
                for r in range(RING):
                    row = pool.snap((i * RING + r) * TC)
                    s_mul[r].wait(pool, i, 0)
                    x = X1[:, bass.ds(row, TC), :]
                    s_add[r].done(pool.tensor_tensor(x, x, XN[:, r, :, :], ALU.add))
                    s_add[r].wait(pool, i, 0)
                    pool.dma_start(out_rows[:, bass.ds(row, TC), :], x).then_inc(s_out, 16)
            pool.wait_ge(s_out, 16 * NB)


def kernel(**inputs):
    import numpy as np
    import concourse.bacc as bacc
    from concourse.bass_utils import run_bass_kernel_spmd as run

    nc = bacc.Bacc("TRN2", target_bir_lowering=False, num_devices=1)
    arrays, aps = {}, {}
    for name, value in inputs.items():
        arrays[f"in_{name}"] = np.ascontiguousarray(value)
        aps[name] = nc.dram_tensor(f"in_{name}", arrays[f"in_{name}"].shape, mybir.dt.from_np(arrays[f"in_{name}"].dtype),
                                   kind="ExternalInput").ap()
    out = nc.dram_tensor("out_x", (NB, T, D), F32, kind="ExternalOutput").ap()
    build_program(nc, aps, out)
    return run(nc, [arrays], core_ids=[0]).results[0]["out_x"]
```

```python
from contextlib import ExitStack

import concourse.bass as bass
from concourse import mybir

F32, F32R = mybir.dt.float32, mybir.dt.float32r
U32, I32 = mybir.dt.uint32, mybir.dt.int32
ALU, ACT, AX = mybir.AluOpType, mybir.ActivationFunctionType, mybir.AxisListType

P = 128
NB, T, D = 16, 512, 256
H, R = 8, 64
KC = D // P
TC = T // P
NT = NB * T
NCH = NT // P
E, F = 8, 1024
CAP = -(-NT * 5 // (E * 4))
BLK = 256
EPS = 1e-5
UNITS = H * TC
RSQRT_SEED, RSQRT_OPS = 0x5F3759DF, 13


class Stream:

    def __init__(self, sem, per, step, base):
        self.sem, self.per, self.step, self.base = sem, per, step, base

    def done(self, ins):
        ins.then_inc(self.sem, self.step)

    def wait(self, eng, b, k):
        value = b * (self.per * self.step) + (k + 1) * self.step + self.base
        if not isinstance(value, int) or value > self.base:
            eng.wait_ge(self.sem, value)


def start(eng, streams):
    for stream in streams:
        if stream.base:
            eng.sem_inc(stream.sem, stream.base)


def snap(eng, x):
    return x if isinstance(x, int) else eng.snap(x)


class PairStream:

    def __init__(self, sem, parity):
        self.sem, self.parity = sem, parity

    def done(self, ins):
        ins.then_inc(self.sem, 16)

    def wait(self, eng, b):
        eng.wait_ge(self.sem, b * 8 + (16 - 8 * self.parity))


class Chain:

    def __init__(self, eng, sem):
        self.eng, self.sem, self.n = eng, sem, 0

    def __call__(self, ins):
        ins.then_inc(self.sem, 1)
        self.n += 1
        self.eng.wait_ge(self.sem, self.n)


def hi_lo_matmul(eng, out, lhs, rhs, first=True, last=True):
    eng.matmul(out, lhs[0], rhs[0], start=first, stop=False)
    eng.matmul(out, lhs[0], rhs[1], start=False, stop=False)
    return eng.matmul(out, lhs[1], rhs[0], start=False, stop=last)


def rsqrt_and_shift(dve, mv, v, y, t, nmr):
    newton = [
        lambda: dve.tensor_tensor(t, y, y, ALU.mult),
        lambda: dve.scalar_tensor_tensor(out=t, in0=t, scalar=-0.5, in1=v, op0=ALU.mult, op1=ALU.mult),
        lambda: dve.scalar_tensor_tensor(out=y, in0=t, scalar=1.5, in1=y, op0=ALU.add, op1=ALU.mult)]
    return [
        lambda: dve.tensor_scalar(v, mv[:, :, 1], EPS, None, ALU.add),
        lambda: dve.tensor_scalar(t.bitcast(U32), v.bitcast(U32), 1, None, ALU.logical_shift_right),
        lambda: dve.tensor_scalar(y.bitcast(U32), t.bitcast(U32), -1.0, float(RSQRT_SEED), ALU.mult, ALU.add),
        *newton, *newton, *newton,
        lambda: dve.scalar_tensor_tensor(out=nmr, in0=mv[:, :, 0], scalar=-1.0, in1=y, op0=ALU.mult, op1=ALU.mult)]


def build_program(nc, ap, out):
    top = ExitStack()
    with top:
        def sb(name, shape, dt=F32, ctx=top):
            return ctx.enter_context(nc.sbuf_tensor(name, shape, dt))

        def sem(name, ctx=top):
            return ctx.enter_context(nc.semaphore(name))

        PS = top.enter_context(nc.psum_tensor("PS", [P, 8, 512], F32))
        h2_dram = nc.dram_tensor("h2_rows", [NT + P, D], F32).ap()
        acc_dram = nc.dram_tensor("acc_rows", [NT + P, D], F32).ap()
        mod_dram = nc.dram_tensor("mod_rows", [NB, 5, D], F32).ap()
        ktab_dram = nc.dram_tensor("key_rows", [NT + P, E], F32).ap()
        m = dict(ktab_dram=ktab_dram, PS=PS, h2_dram=h2_dram, acc_dram=acc_dram, mod_dram=mod_dram)
        m["X1"] = sb("X1", [P, NCH, D])
        m["IDENT"] = sb("IDENT", [P, P])
        m["LOGITS"] = sb("LOGITS", [P, NCH, E])
        with ExitStack() as attn:
            def sba(name, shape, dt=F32):
                return sb(name, shape, dt, attn)
            for k, shape, dt in (
                    ("AH", [P, KC, H * R], F32R), ("AL", [P, KC, H * R], F32R),
                    ("DH", [P, KC, 2 * R], F32R), ("DL", [P, KC, 2 * R], F32R),
                    ("GH", [P, H // 2, D], F32R), ("GL", [P, H // 2, D], F32R),
                    ("WR", [P, KC, E], F32), ("BR", [P, E], F32),
                    ("SA", [P, KC, NB], F32), ("CA1", [P, KC, NB], F32),
                    ("K2", [P, 2, T], F32R), ("Q2", [P, H, T], F32R),
                    ("V1", [P, 2, TC, 2 * R], F32R), ("V2", [P, 2, TC, 2 * R], F32R)):
                m[k] = sba(k, shape, dt)
            m["s_xin"] = [PairStream(sem(f"xin{j}"), j) for j in range(2)]
            setup(nc, ap, m, sem)
            attention(nc, ap, m, sem, sba)
        m["IDX"] = sb("IDX", [P, E * CAP // P], U32)
        m["INFO"] = sb("INFO", [1, 4 * E], I32)
        for phase in (route, experts):
            with ExitStack() as tiles:
                phase(nc, ap, m, sem, lambda name, shape, dt=F32: sb(name, shape, dt, tiles))
        with ExitStack() as tiles:
            last_norm(nc, out, m, sem, lambda name, shape, dt=F32: sb(name, shape, dt, tiles))


def setup(nc, ap, m, sem):
    PS, IDENT = m["PS"], m["IDENT"]
    with ExitStack() as ctx:
        def sb(name, shape, dt=F32):
            return ctx.enter_context(nc.sbuf_tensor(name, shape, dt))

        C = sb("C", [NB, D]); SG = sb("SG", [NB, D]); ST = sb("STc", [P, KC, NB])
        WM = sb("WM", [P, KC, 6 * D])
        WQ = sb("WQ", [R, H, D]); WK = sb("WK", [R, H, R]); WV = sb("WV", [R, H, R])
        WO = sb("WO", [P, KC, H * R]); WOT = sb("WOT", [R, H, D]); WD = sb("WD", [R, D])
        GB = sb("GBs", [NB, 2, D])
        MR = sb("MR", [NB, 5, D])
        MA = sb("MA", [NB, 2, D]); ZERO = sb("ZERO", [P, D])
        s_in, s_w, s_id, s_const, s_out = (sem(x) for x in ("s_in", "s_w", "s_id", "s_const", "s_setout"))
        s_pe, s_act, s_dve, s_mr = (sem(x) for x in ("s_setpe", "s_setact", "s_setdve", "s_mr"))
        MODS_DONE, AL_DONE = 13, 17
        PE_SILU_T, PE_MODT, PE_WDT, PE_A, PE_WOT, PE_G = 1, 3, 4, 5, 6, 7
        silu_ps = PS[:, 0, 0:KC * NB].rearrange("p (k b) -> p k b", k=KC)
        modt_ps = PS[:, 1, 0:4 * NB].rearrange("p (j b) -> p j b", j=4)
        wdt_ps = PS[:, 2, 0:KC * R].rearrange("p (k r) -> p k r", k=KC)
        with nc.Block() as block:
            @block.sync
            def _(sp):
                sp.dma_start(C[:, :], ap["L0_c"]).then_inc(s_in, 16)
                sp.dma_start(WM[:, :, :], ap["L0_wmod"].rearrange("(k p) n -> p k n", p=P)).then_inc(s_in, 16)
                for j, name in enumerate(("L0_ffn_gamma", "L0_ffn_beta")):
                    sp.dma_start(GB[:, j, :], ap[name].partition_broadcast(NB)).then_inc(s_in, 16)
                sp.dma_start(WD[:, :], ap["L0_attn_Wkv_down"]).then_inc(s_w, 16)
                sp.dma_start(WQ[:, :, :], ap["L0_attn_Wq"].rearrange("(h d) n -> d h n", h=H)).then_inc(s_w, 16)
                sp.dma_start(WK[:, :, :], ap["L0_attn_Wk_up"].rearrange("(h d) n -> d h n", h=H)).then_inc(s_w, 16)
                sp.dma_start(WV[:, :, :], ap["L0_attn_Wv_up"].rearrange("(h d) n -> d h n", h=H)).then_inc(s_w, 16)
                sp.dma_start(WO[:, :, :], ap["L0_attn_Wo"].rearrange("(k p) n -> p k n", p=P)).then_inc(s_w, 16)
                sp.dma_start(m["WR"][:, :, :], ap["L0_ffn_Wr"].rearrange("(k p) n -> p k n", p=P)).then_inc(s_w, 16)
                sp.dma_start(m["BR"][:, :], ap["L0_ffn_br"].partition_broadcast(P)).then_inc(s_w, 16)
                for b in range(2):
                    m["s_xin"][b].done(sp.dma_start(m["X1"][:, b * TC:(b + 1) * TC, :],
                                                    ap["L0_attn_x"][b].rearrange("(c p) n -> p c n", p=P)))
                sp.wait_ge(s_mr, 1)
                sp.dma_start(m["mod_dram"], MR[:, :, :]).then_inc(s_out, 16)
                sp.wait_ge(s_id, 3)
                sp.dma_start(m["h2_dram"][NT:NT + P, :], ZERO[:, :]).then_inc(s_out, 16)
                sp.dma_start(m["acc_dram"][NT:NT + P, :], ZERO[:, :]).then_inc(s_out, 16)
                sp.wait_ge(s_out, 48)
                sp.wait_ge(s_w, 16 * 7)

            @block.gpsimd
            def _(pool):
                pool.memset(IDENT[:, :], 0.0).then_inc(s_id, 1)
                pool.wait_ge(s_id, 1)
                pool.affine_select(out=IDENT[:, :], in_=IDENT[:, :], compare_op=ALU.not_equal, fill=1.0, base=0,
                                   pattern=[[-1, P]], channel_multiplier=1).then_inc(s_id, 1)
                pool.memset(ZERO[:, :], 0.0).then_inc(s_id, 1)
                pool.wait_ge(s_id, 3)
                K2, Q2, V1, V2 = (m[x] for x in ("K2", "Q2", "V1", "V2"))
                for i, (part, value) in enumerate(((K2[R:P, :, :], 0.0), (K2[R:R + 1, :, :], 1.0), (Q2[R:P, :, :], 0.0),
                                                   (V1[:, :, :, R:2 * R], 1.0), (V2[:, :, :, R:2 * R], 0.0))):
                    pool.memset(part.bitcast(F32), value).then_inc(s_const, 1)
                    pool.wait_ge(s_const, i + 1)

            @block.scalar
            def _(act):
                act.wait_ge(s_in, 64)
                act.activation(SG[:, :], C[:, :], ACT.Silu).then_inc(s_act, 1)
                act.wait_ge(s_pe, PE_WDT)
                for j in range(2):
                    act.activation(m["DH"][:, :, j * R:(j + 1) * R], wdt_ps, ACT.Copy).then_inc(s_act, 1)
                act.wait_ge(s_pe, PE_A)
                for k in range(KC):
                    act.activation(m["AH"][:, k, :], PS[:, 3 + k, :], ACT.Copy, scale=float(R) ** -0.5).then_inc(s_act, 1)
                act.wait_ge(s_pe, PE_WOT)
                for j in range(4):
                    act.activation(WOT[:, 2 * j:2 * j + 2, :], PS[0:R, 4 + j, :].rearrange("p (h n) -> p h n", h=2),
                                   ACT.Copy).then_inc(s_act, 1)
                for j in range(4):
                    act.wait_ge(s_pe, PE_G + j)
                    for odd in range(2):
                        act.activation(m["GH"][odd * R:(odd + 1) * R, j, :], PS[0:R, j, odd * D:(odd + 1) * D],
                                       ACT.Copy).then_inc(s_act, 1)
            SILU, DH_DONE, AH_DONE, WOT_DONE = 1, 3, 5, 9

            @block.tensor
            def _(pe):
                pe.wait_ge(s_id, 2)
                pe.wait_ge(s_act, SILU)
                for k in range(KC):
                    last = pe.transpose(silu_ps[:, k, :], SG[:, k * P:(k + 1) * P], IDENT[0:NB, 0:NB])
                last.then_inc(s_pe, 1)
                pe.wait_ge(s_dve, 1)
                for j in range(3):
                    for k in range(KC):
                        last = pe.matmul(PS[0:NB, 5 + j, :], ST[:, k, :], WM[:, k, j * 512:(j + 1) * 512],
                                         start=(k == 0), stop=(k == KC - 1))
                last.then_inc(s_pe, 1)
                for j in range(4):
                    for k in range(KC):
                        last = pe.matmul(modt_ps[:, j, :], WM[:, k, j * P:(j + 1) * P], ST[:, k, :],
                                         start=(k == 0), stop=(k == KC - 1))
                last.then_inc(s_pe, 1)
                pe.wait_ge(s_w, 16 * 7)
                for k in range(KC):
                    last = pe.transpose(wdt_ps[:, k, :], WD[:, k * P:(k + 1) * P], IDENT[0:R, 0:R])
                last.then_inc(s_pe, 1)
                for k in range(KC):
                    for h in range(H):
                        last = pe.matmul(PS[:, 3 + k, h * R:(h + 1) * R], WQ[:, h, k * P:(k + 1) * P], WK[:, h, :],
                                         start=True, stop=True)
                last.then_inc(s_pe, 1)
                pe.wait_ge(s_dve, MODS_DONE)
                pe.wait_ge(s_act, AH_DONE)
                pe.wait_ge(s_dve, AL_DONE)
                for h in range(H):
                    for k in range(KC):
                        last = pe.transpose(PS[0:R, 4 + h // 2, (h % 2) * D + k * P:(h % 2) * D + (k + 1) * P],
                                            WO[:, k, h * R:(h + 1) * R], IDENT[:, :])
                last.then_inc(s_pe, 1)
                pe.wait_ge(s_act, WOT_DONE)
                for h in range(H):
                    last = pe.matmul(PS[0:R, h // 2, (h % 2) * D:(h % 2 + 1) * D], WV[:, h, :], WOT[:, h, :],
                                     start=True, stop=True)
                    if h % 2:
                        last.then_inc(s_pe, 1)
            @block.vector
            def _(dve):
                chain = Chain(dve, s_dve)
                dve.wait_ge(s_pe, PE_SILU_T)
                chain(dve.tensor_copy(ST[:, :, :], silu_ps))
                dve.wait_ge(s_pe, PE_MODT)
                chain(dve.tensor_copy(m["SA"][:, :, :], modt_ps[:, 0:2, :]))
                chain(dve.tensor_scalar(m["CA1"][:, :, :], modt_ps[:, 2:4, :], 1.0, None, ALU.add))
                for j, src in enumerate((PS[0:NB, 6, 0:D], PS[0:NB, 7, D:2 * D])):
                    sign, g = MA[:, j, :], MR[:, 4 * j, :]
                    chain(dve.tensor_scalar(sign, src, 0.0, 2.0, ALU.is_ge, ALU.mult))
                    chain(dve.tensor_scalar(sign, sign, -1.0, None, ALU.add))
                    chain(dve.tensor_tensor(g, src, sign, ALU.mult))
                    chain(dve.scalar_tensor_tensor(out=g, in0=g, scalar=0.25, in1=sign, op0=ALU.max, op1=ALU.mult))
                chain(dve.tensor_scalar(MR[:, 1, :], PS[0:NB, 7, 0:D], 1.0, None, ALU.add))
                chain(dve.tensor_copy(MR[:, 2, :], PS[0:NB, 6, D:2 * D]))
                dve.wait_ge(s_act, DH_DONE)
                for j in range(2):
                    chain(dve.tensor_tensor(m["DL"][:, :, j * R:(j + 1) * R], wdt_ps,
                                            m["DH"][:, :, j * R:(j + 1) * R].bitcast(F32), ALU.subtract))
                dve.wait_ge(s_act, AH_DONE)
                for k in range(KC):
                    chain(dve.scalar_tensor_tensor(out=m["AL"][:, k, :], in0=PS[:, 3 + k, :], scalar=float(R) ** -0.5,
                                                   in1=m["AH"][:, k, :].bitcast(F32), op0=ALU.mult,
                                                   op1=ALU.subtract))
                chain(dve.tensor_tensor(MR[:, 3, :], MR[:, 4, :], GB[:, 1, :], ALU.mult))
                dve.tensor_tensor(MR[:, 4, :], MR[:, 4, :], GB[:, 0, :], ALU.mult).then_inc(s_mr, 1)
                for j in range(4):
                    dve.wait_ge(s_act, WOT_DONE + 2 * j + 2)
                    for odd in range(2):
                        chain(dve.tensor_tensor(m["GL"][odd * R:(odd + 1) * R, j, :], PS[0:R, j, odd * D:(odd + 1) * D],
                                                m["GH"][odd * R:(odd + 1) * R, j, :].bitcast(F32), ALU.subtract))


def attention(nc, ap, m, sem, sb):
    PS, IDENT, X1, LOGITS = m["PS"], m["IDENT"], m["X1"], m["LOGITS"]
    AH, AL, DH, DL, GH, GL, WR, BR = (m[k] for k in ("AH", "AL", "DH", "DL", "GH", "GL", "WR", "BR"))
    x_rows = ap["L0_attn_x"].rearrange("b (c p) n -> p (b c) n", p=P)
    NHI, NLO = sb("NHI", [P, KC, T], F32R), sb("NLO", [P, KC, T], F32R)
    MODB = sb("MODB", [P, 4, D])
    K1, K2 = sb("K1", [P, 2, T], F32R), m["K2"]
    V1, V2 = m["V1"], m["V2"]
    Q1, Q2 = sb("Q1", [P, H, T], F32R), m["Q2"]
    NMAX, MROW = sb("NMAX", [P, 2, TC]), sb("MROW", [TC, 2, P], F32R)
    PF, PH, PL = sb("PF", [P, 2, T]), sb("PH", [P, 4, T], F32R), sb("PL", [P, 4, T], F32R)
    RECT, RDEN = sb("RECT", [R, T]), sb("RDEN", [R, T // 32])
    XF = sb("XF", [P, 2, T])
    XH, XL = sb("XH", [P, H // 2, T], F32R), sb("XL", [P, H // 2, T], F32R)
    XN1, LTF, H2 = sb("XN1", [P, TC, D]), sb("LTF", [P, T]), sb("H2", [P, TC, D])
    TR = sb("TR", [P, KC * T])
    NF = TR[:, :].rearrange("p (k n) -> p k n", k=KC)
    H2T = TR[:, :].rearrange("p (c k n) -> p c k n", c=TC, k=KC)
    YT, GATE = sb("YT", [P, 2, D]), sb("GATE", [P, 16])
    norm = [dict(s6=sb(f"s6_{j}", [P, TC, 6]), mv=sb(f"mv_{j}", [P, TC, 2]), v=sb(f"v_{j}", [P, TC]),
                 y=sb(f"y_{j}", [P, TC]), t=sb(f"t_{j}", [P, TC]), nmr=sb(f"nmr_{j}", [P, TC])) for j in range(2)]

    streams = []

    def S(name, per, step=1, base=1):
        streams.append(Stream(sem(name), per, step, base))
        return streams[-1]

    s_st, s_mx, s_pv = S("st", UNITS), S("mx", UNITS), S("pv", UNITS)
    s_mt, s_q, s_proj, s_n1t, s_lat, s_vt, s_h2t, s_lg = (
        S("mt", H), S("q", 4), S("proj", TC), S("n1t", KC), S("lat", 1), S("vt", 1), S("h2t", TC), S("lg", 1))
    s_exp, s_qhi, s_latc, s_vhi, s_nf = S("exp", 2 * UNITS), S("qhi", 16), S("latc", 3), S("vhi", 1), S("nf", KC)
    s_xn1, s_xn2, s_h2c, s_xhi, s_mrow = S("xn1", TC), S("xn2", TC), S("h2c", TC), S("xhi", H // 2), S("mrow", H)
    s_mred, s_x, s_qlo, s_nhl, s_klo, s_vlo = (
        S("mred", UNITS), S("x", 4 * H), S("qlo", 8), S("nhl", 2 * KC), S("klo", 1), S("vlo", 1))
    s_y, s_x1, s_lgc, s_xlo = S("y", TC), S("x1", TC), S("lgc", 1), S("xlo", H // 2)
    NORM_OPS = 2 * TC + RSQRT_OPS
    s_norm = [S("norm1", NORM_OPS), S("norm2", NORM_OPS)]
    s_plo, s_hmul, s_hadd, s_gbb = S("plo", UNITS), S("hmul", TC), S("hadd", TC), S("gbb", TC)
    s_xin = m["s_xin"]
    s_modin = [PairStream(sem(f"modin{j}"), j) for j in range(2)]
    s_mdma, s_h2out = S("mdma", H, 16), S("h2out", 2, 16)

    def st_bank(n):
        return PS[:, n % 2, :]

    def mx_bank(n):
        return PS[:, 2 + n % 2, :]

    def pv_bank(h):
        return PS[:, 4 + h % 2, :]

    AHEAD = 10

    JOBS = {3: [("mrow", 2, 0)], 5: [("n1t", 0, 1)], 6: [("proj", 0, -1)], 7: [("mrow", 3, 0)], 8: [("proj", 1, -1)],
            9: [("n1t", 1, 1)], 10: [("proj", 2, -1)], 11: [("mrow", 4, 0)], 12: [("proj", 3, -1)],
            13: [("lat", 0, 1)], 15: [("mrow", 5, 0)], 16: [("q", 0, 1)], 19: [("mrow", 6, 0), ("q", 1, 1)],
            22: [("h2t", 0, -1)], 23: [("mrow", 7, 0), ("h2t", 1, -1)], 24: [("q", 2, 1)], 26: [("h2t", 2, -1)],
            27: [("mrow", 0, 1)], 28: [("h2t", 3, -1)], 29: [("vt", 0, 1), ("lg", 0, -1)],
            31: [("mrow", 1, 1), ("q", 3, 1)]}
    ORDER = [j for n in range(UNITS) for j in JOBS.get(n, [])]
    LAG = {"mrow": 1, "proj": 1, "q": 2, "n1t": 1, "lat": 2, "vt": 1, "lg": 1, "h2t": 0}
    banks, free = {}, [-1, -1]
    for n, jobs in sorted(JOBS.items()):
        for job in jobs:
            banks[job] = min(x for x in (0, 1) if free[x] <= n)
            free[banks[job]] = n + LAG[job[0]] + 1
    FREED = {"mrow": (s_mrow, 1), "proj": (s_y, 1), "q": (s_qlo, 2), "n1t": (s_nf, 1), "lat": (s_klo, 1),
             "vt": (s_vlo, 1), "h2t": (s_h2c, 1), "lg": (s_lgc, 1)}

    def at_slot(job):
        return next(n for n, jobs in JOBS.items() if job in jobs)

    def exists(b):
        return not isinstance(b, int) or 0 <= b < NB

    def job_bank(job):
        return PS[:, 6 + banks[job], :]

    def wait_job_bank(eng, b, job):
        at = ORDER.index(job) - 1
        while True:
            kind, idx, off = ORDER[at % len(ORDER)]
            bb = b + at // len(ORDER) + off
            if isinstance(bb, int) and bb < 0 and at < -len(ORDER):
                return
            if banks[kind, idx, off] == banks[job] and exists(bb):
                stream, each = FREED[kind]
                stream.wait(eng, bb, idx * each + each - 1)
                return
            at -= 1

    def unit(b, n):
        return b + n // UNITS, n % UNITS

    def batches(eng, body, looped=NB - 4):
        for b in (-2, -1, 0):
            body(b, b % 2)
        with eng.Fori(0, looped // 2) as i:
            for j in range(2):
                body(i * 2 + (1 + j), (1 + j) % 2)
        for b in range(1 + looped, NB + 1):
            body(b, b % 2)

    with nc.Block() as block:
        @block.sync
        def _(sp):
            def load_x(b, par, row):
                sp.dma_start(X1[:, bass.ds(row, TC), :], x_rows[:, bass.ds(row, TC), :]
                             ).then_inc(s_xin[par].sem, 16)

            def body(b, par):
                if not (isinstance(b, int) and b == -2) and exists(b + 3):
                    row = snap(sp, (b + 3) * TC)
                    s_norm[0].wait(sp, b + 1, 2 * TC - 1)
                    load_x(b + 3, 1 - par, row)
                for n in range(UNITS):
                    if n % 4 == 3:
                        tb, h = unit(b, n + 5)
                        h = h // TC
                        if exists(tb):
                            s_mrow.wait(sp, tb, h)
                            s_mdma.done(sp.dma_start(Q2[R:R + 1, h, :].bitcast(F32), MROW[:, h % 2, :].bitcast(F32)))
                    if n == 31 and exists(b):
                        row = snap(sp, b + 0)
                        s_gbb.wait(sp, b - 1, TC - 1)
                        sp.dma_start(MODB[:, :, :], m["mod_dram"][bass.ds(row, 1), 0:4, :].rearrange("a j n -> (a j) n").partition_broadcast(P)
                                     ).then_inc(s_modin[par].sem, 16)

            batches(sp, body)

        @block.gpsimd
        def _(pool):
            start(pool, streams)

            def body(b, par):
                for n in range(UNITS):
                    tb, u = unit(b, n + 1)
                    if exists(tb):
                        s_exp.wait(pool, tb, 2 * u + 1)
                        s_pv.wait(pool, tb, u - 4)
                        s_plo.done(pool.tensor_tensor(PL[:, u % 4, :], PF[:, u % 2, :], PH[:, u % 4, :].bitcast(F32),
                                                      ALU.subtract))
                    pb, pp = b - 1, 1 - par
                    if exists(pb):
                        if 18 <= n < 26:
                            c = (n - 18) // 2
                            if n % 2 == 0:
                                s_xn2.wait(pool, pb, c)
                                s_hmul.done(pool.tensor_tensor(H2[:, c, :], H2[:, c, :], MODB[:, 1, :], ALU.mult))
                            else:
                                s_hmul.wait(pool, pb, c)
                                s_hadd.done(pool.tensor_tensor(H2[:, c, :], H2[:, c, :], MODB[:, 2, :], ALU.add))
                        if 26 <= n < 30:
                            c = n - 26
                            x = X1[:, bass.ds(pb * TC + c, 1), :].rearrange("p c n -> p (c n)")
                            s_gbb.done(pool.tensor_tensor(x, x, MODB[:, 3, :], ALU.add))

            batches(pool, body)

        @block.scalar
        def _(act):
            def body(b, par):
                for n in range(UNITS):
                    tb, u = unit(b, n + 1)
                    if exists(tb):
                        s_st.wait(act, tb, u)
                        s_pv.wait(act, tb, u - 4)
                        s_exp.done(act.activation(PH[:, u % 4, :], st_bank(u), ACT.Exp))
                        s_plo.wait(act, tb, u - 2)
                        s_exp.done(act.activation(PF[:, u % 2, :], st_bank(u), ACT.Exp))
                    for job in JOBS.get(n, []):
                        kind, idx, off = job
                        jb = b + off
                        if not exists(jb):
                            continue
                        bank = job_bank(job)
                        jp = (par + off) % 2
                        if kind == "mrow":
                            s_mt.wait(act, jb, idx)
                            s_mdma.wait(act, jb, idx - 2)
                            s_mrow.done(act.activation(MROW[:, idx % 2, :], bank[0:TC, 0:P], ACT.Copy))
                        elif kind == "q":
                            s_q.wait(act, jb, idx)
                            s_st.wait(act, jb - 1, 8 * idx + 7)
                            for odd in range(2):
                                for half in range(2):
                                    s_qhi.done(act.activation(Q1[half * R:(half + 1) * R, 2 * idx + odd, :],
                                                              bank[odd * R:(odd + 1) * R, :], ACT.Copy))
                        elif kind == "lat":
                            s_lat.wait(act, jb, 0)
                            s_st.wait(act, jb - 2, UNITS - 1)
                            s_latc.done(act.activation(K1[0:R, jp, :], bank[0:R, :], ACT.Copy))
                            s_vt.wait(act, jb - 1, 0)
                            s_latc.done(act.activation(LTF[:, :], bank, ACT.Copy))
                            s_latc.wait(act, jb, 0)
                            s_latc.done(act.activation(K2[0:R, jp, :], K1[0:R, jp, :].bitcast(F32), ACT.Copy))
                        elif kind == "vt":
                            s_vt.wait(act, jb, 0)
                            s_pv.wait(act, jb - 2, UNITS - 1)
                            s_vhi.done(act.activation(V1[:, jp, :, 0:R],
                                                      bank.rearrange("p (c r) -> p c r", c=TC)[:, :, 0:R], ACT.Copy))
                        elif kind == "n1t":
                            s_n1t.wait(act, jb, idx)
                            s_nhl.wait(act, jb - 1, 2 * idx + 1)
                            s_lg.wait(act, jb - 3, 0)
                            s_nf.done(act.activation(NF[:, idx, :], bank, ACT.Identity,
                                                     bias=m["SA"][:, idx, bass.ds(jb, 1)], scale=m["CA1"][:, idx, bass.ds(jb, 1)]))
                        elif kind == "h2t":
                            s_h2t.wait(act, jb, idx)
                            s_lg.wait(act, jb - 1, 0)
                            if exists(jb + 2):
                                s_nhl.wait(act, jb + 2, 2 * KC - 1)
                            s_h2c.done(act.activation(H2T[:, idx, :, :], bank[:, 0:D].rearrange("p (k n) -> p k n", k=KC),
                                                      ACT.Copy))
                    if n == 30 and exists(b - 1):
                        row = snap(act, (b - 1) * T)
                        s_hadd.wait(act, b - 1, TC - 1)
                        for dram in (m["h2_dram"], m["acc_dram"]):
                            rows = dram[bass.ds(row, T), :].rearrange("(c p) n -> p c n", p=P)
                            s_h2out.done(act.dma_start(rows, H2[:, :, :]))
                    if n < 4 and exists(b + 1):
                        c = n
                        s_norm[0].wait(act, b + 1, NORM_OPS - 1)
                        s_n1t.wait(act, b, 1)
                        s_xn1.done(act.activation(XN1[:, c, :], X1[:, bass.ds((b + 1) * TC + c, 1), :].rearrange("p c n -> p (c n)"),
                                                  ACT.Identity, scale=norm[0]["y"][:, c:c + 1], bias=norm[0]["nmr"][:, c:c + 1]))
                    if n in (17, 18) and exists(b - 1):
                        for c in (2 * n - 34, 2 * n - 33):
                            s_norm[1].wait(act, b - 1, NORM_OPS - 1)
                            s_h2out.wait(act, b - 2, 1)
                            s_h2t.wait(act, b - 2, TC - 1)
                            s_xn2.done(act.activation(H2[:, c, :], X1[:, bass.ds((b - 1) * TC + c, 1), :].rearrange("p c n -> p (c n)"),
                                                      ACT.Identity, scale=norm[1]["y"][:, c:c + 1], bias=norm[1]["nmr"][:, c:c + 1]))
                    if n % 8 == 4:
                        xb, p = (b, n // 8 - 1) if n > 4 else (b - 1, 3)
                        if exists(xb):
                            s_x.wait(act, xb, 4 * (2 * p + 1) + 3)
                            s_proj.wait(act, xb - 1, TC - 1)
                            s_xhi.done(act.activation(XH[:, p, :], XF[:, p % 2, :], ACT.Copy))

            batches(act, body)
            s_h2out.wait(act, NB - 1, 1)

        @block.vector
        def _(dve):
            def gate(which, c):
                dve.memset(GATE[:, which * 8 + c:which * 8 + c + 1], 0.0)

            def norm_stats(which, nb, c):
                w, st = norm[which], s_norm[which]
                if c == 0:
                    st.wait(dve, nb, -1)
                gate(which, c)
                st.done(dve.bn_stats(w["s6"][:, c, :], X1[:, bass.ds(nb * TC + c, 1), :].rearrange("p c n -> p (c n)")))
                if c == TC - 1:
                    st.wait(dve, nb, c)
                    gate(which, TC)
                    for k in range(TC):
                        st.done(dve.bn_aggr(w["mv"][:, k, :], w["s6"][:, k, :]))

            pending = []

            def step():
                if pending:
                    pending.pop(0)()

            def norm_scale(which, nb):
                w, st = norm[which], s_norm[which]

                def queue(k, issue):
                    def go():
                        if k == 2 * TC:
                            (s_xn1, s_xn2)[which].wait(dve, nb - 1, TC - 1)
                        st.wait(dve, nb, k - 1)
                        st.done(issue())
                    pending.append(go)
                for k, issue in enumerate(rsqrt_and_shift(dve, w["mv"][:, :, :], *(w[x][:, :] for x in ("v", "y", "t", "nmr")))):
                    queue(2 * TC + k, issue)

            def normalise(b, n, place):
                xb, h = (b, (n - 5) // 4) if n >= 5 else (b - 1, H - 1)
                part = (n - 1) % 4
                if n == 0 or not exists(xb):
                    return
                bank, p, odd = pv_bank(h), h // 2, h % 2
                if (part, place) == (0, 1):
                    s_pv.wait(dve, xb, TC * h + TC - 1)
                    s_x.wait(dve, xb, 4 * h - 1)
                    s_x.done(dve.transpose(RECT[:, :], bank[R:P, :]))
                elif (part, place) == (1, 0):
                    s_x.wait(dve, xb, 4 * h)
                    s_x.done(dve.reciprocal(RDEN[:, :], RECT[:, :].rearrange("p (g j) -> p g j", j=32)[:, :, 0]))
                elif (part, place) == (1, 1):
                    s_x.wait(dve, xb, 4 * h + 1)
                    s_x.done(dve.transpose(RECT[:, :], RDEN[:, :].unsqueeze(2).broadcast_to([R, T // 32, 32])))
                elif (part, place) == (2, 0):
                    s_x.wait(dve, xb, 4 * h + 2)
                    if odd == 0:
                        s_xhi.wait(dve, xb, p - 2)
                        s_xlo.wait(dve, xb, p - 2)
                    s_x.done(dve.tensor_tensor(XF[odd * R:(odd + 1) * R, p % 2, :], bank[0:R, :], RECT[:, :], ALU.mult))

            def body(b, par):
                pb, pp, nb = b - 1, 1 - par, b + 2
                for n in range(UNITS):
                    normalise(b, n, 0)
                    step()
                    for job in [x for x in ORDER if (at_slot(x) + LAG[x[0]]) % UNITS == n]:
                        kind, idx, off = job
                        jb = b + off - (at_slot(job) + LAG[kind]) // UNITS
                        if not exists(jb):
                            continue
                        bank = job_bank(job)
                        jp = (par + off + (at_slot(job) + LAG[kind]) // UNITS) % 2
                        if kind == "q":
                            for odd in range(2):
                                s_qhi.wait(dve, jb, 4 * idx + 2 * odd + 1)
                                h = 2 * idx + odd
                                s_qlo.done(dve.tensor_tensor(Q2[0:R, h, :], bank[odd * R:(odd + 1) * R, :],
                                                             Q1[odd * R:(odd + 1) * R, h, :].bitcast(F32), ALU.subtract))
                        elif kind == "proj":
                            s_modin[pp].wait(dve, jb)
                            s_proj.wait(dve, jb, idx)
                            s_x1.wait(dve, jb, idx - 1)
                            s_y.done(dve.tensor_tensor(YT[:, idx % 2, :], bank[:, 0:D], MODB[:, 0, :], ALU.mult))
                            s_y.wait(dve, jb, idx)
                            x = X1[:, bass.ds(jb * TC + idx, 1), :].rearrange("p c n -> p (c n)")
                            s_x1.done(dve.tensor_tensor(x, YT[:, idx % 2, :], x, ALU.add))
                            s_x1.wait(dve, jb, idx)
                            norm_stats(1, jb, idx)
                        elif kind == "n1t":
                            s_nf.wait(dve, jb, idx)
                            s_q.wait(dve, jb - 1, 3)
                            s_nhl.done(dve.tensor_copy(NHI[:, idx, :], NF[:, idx, :]))
                            s_nhl.wait(dve, jb, 2 * idx)
                            s_nhl.done(dve.tensor_tensor(NLO[:, idx, :], NF[:, idx, :], NHI[:, idx, :].bitcast(F32),
                                                         ALU.subtract))
                        elif kind == "lat":
                            s_latc.wait(dve, jb, 1)
                            s_klo.done(dve.tensor_tensor(K1[R:P, jp, :], bank[R:P, :], K1[0:R, jp, :].bitcast(F32), ALU.subtract))
                        elif kind == "vt":
                            s_vhi.wait(dve, jb, 0)
                            s_vlo.done(dve.tensor_tensor(V2[:, jp, :, 0:R], bank.rearrange("p (c r) -> p c r", c=TC)[:, :, 0:R],
                                                         V1[:, jp, :, 0:R].bitcast(F32), ALU.subtract))
                        elif kind == "lg":
                            s_lg.wait(dve, jb, idx)
                            s_lgc.done(dve.tensor_tensor(
                                LOGITS[:, bass.ds(jb * TC, TC), :], bank[:, 0:TC * E].rearrange("p (c e) -> p c e", c=TC),
                                BR[:, :].unsqueeze(1).broadcast_to([P, TC, E]), ALU.add))
                    step()
                    tb, u = unit(b, n + AHEAD)
                    if exists(tb):
                        h, c = u // TC, u % TC
                        s_mx.wait(dve, tb, u)
                        if c == 0:
                            s_mt.wait(dve, tb, h - 2)
                        s_mred.done(dve.tensor_reduce(NMAX[:, h % 2, c:c + 1], mx_bank(u), AX.X, ALU.max, negate=True))
                    if n % 8 == 5:
                        xb, p = (b, n // 8 - 1) if n > 5 else (b - 1, 3)
                        if exists(xb):
                            s_xhi.wait(dve, xb, p)
                            s_xlo.done(dve.tensor_tensor(XL[:, p, :], XF[:, p % 2, :], XH[:, p, :].bitcast(F32), ALU.subtract))
                    normalise(b, n, 1)
                    step()
                    if n in (18, 20, 22, 24) and exists(nb):
                        if n == 18:
                            s_xin[par].wait(dve, nb)
                        norm_stats(0, nb, (n - 18) // 2)
                    if n == 26 and exists(nb):
                        norm_scale(0, nb)
                    if n == 13 and exists(pb):
                        norm_scale(1, pb)
                    step()

            batches(dve, body)

        @block.tensor
        def _(pe):
            def body(b, par):
                for n in range(UNITS):
                    tb, u = unit(b, n + 1)
                    if exists(tb):
                        h, c, kp = u // TC, u % TC, (par + (n + 1) // UNITS) % 2
                        s_exp.wait(pe, tb, 2 * (u - 2) + 1)
                        if c == 0:
                            s_mdma.wait(pe, tb, h)
                            s_qlo.wait(pe, tb, h)
                        keys = slice(c * P, (c + 1) * P)
                        pe.matmul(st_bank(u), K1[:, kp, keys], Q1[:, h, :], start=True, stop=False)
                        s_st.done(pe.matmul(st_bank(u), K2[:, kp, keys], Q2[:, h, :], start=False, stop=True))
                    tb, u = unit(b, n + AHEAD)
                    if exists(tb):
                        h, c, kp = u // TC, u % TC, (par + (n + AHEAD) // UNITS) % 2
                        s_mred.wait(pe, tb, u - 2)
                        if c == 0:
                            s_qlo.wait(pe, tb, h)
                            s_klo.wait(pe, tb, 0)
                        s_mx.done(pe.matmul(mx_bank(u), Q1[:, h, c * P:(c + 1) * P], K1[:, kp, :], start=True, stop=True))
                    for job in JOBS.get(n, []):
                        kind, idx, off = job
                        jb = b + off
                        if not exists(jb):
                            continue
                        wait_job_bank(pe, b, job)
                        bank = job_bank(job)
                        jp = (par + off) % 2
                        if kind == "mrow":
                            s_mred.wait(pe, jb, TC * idx + TC - 1)
                            s_mt.done(pe.transpose(bank[0:TC, 0:P], NMAX[:, idx % 2, :], IDENT[:, :]))
                        elif kind == "q":
                            s_nhl.wait(pe, jb, 3)
                            cols = slice(2 * idx * R, 2 * (idx + 1) * R)
                            for k in range(KC):
                                last = hi_lo_matmul(pe, bank, (AH[:, k, cols], AL[:, k, cols]),
                                                    (NHI[:, k, :], NLO[:, k, :]), k == 0, k == KC - 1)
                            s_q.done(last)
                        elif kind == "lat":
                            s_nhl.wait(pe, jb, 3)
                            for k in range(KC):
                                last = hi_lo_matmul(pe, bank, (DH[:, k, :], DL[:, k, :]),
                                                    (NHI[:, k, :], NLO[:, k, :]), k == 0, k == KC - 1)
                            s_lat.done(last)
                        elif kind == "vt":
                            s_latc.wait(pe, jb, 2)
                            for c in range(TC):
                                last = pe.transpose(bank[:, c * P:(c + 1) * P], LTF[:, c * P:(c + 1) * P], IDENT[:, :])
                            s_vt.done(last)
                        elif kind == "n1t":
                            s_xn1.wait(pe, jb, TC - 1)
                            for c in range(TC):
                                last = pe.transpose(bank[:, c * P:(c + 1) * P], XN1[:, c, idx * P:(idx + 1) * P], IDENT[:, :])
                            s_n1t.done(last)
                        elif kind == "proj":
                            s_xhi.wait(pe, jb, 3)
                            s_xlo.wait(pe, jb, 3)
                            rows = slice(idx * P, (idx + 1) * P)
                            for p in range(H // 2):
                                last = hi_lo_matmul(pe, bank[:, 0:D], (XH[:, p, rows], XL[:, p, rows]),
                                                    (GH[:, p, :], GL[:, p, :]), p == 0, p == H // 2 - 1)
                            s_proj.done(last)
                        elif kind == "h2t":
                            s_hadd.wait(pe, jb, idx)
                            for k in range(KC):
                                last = pe.transpose(bank[:, k * P:(k + 1) * P], H2[:, idx, k * P:(k + 1) * P], IDENT[:, :])
                            s_h2t.done(last)
                        elif kind == "lg":
                            s_h2c.wait(pe, jb, TC - 1)
                            for c in range(TC):
                                for k in range(KC):
                                    last = pe.matmul(bank[:, c * E:(c + 1) * E], H2T[:, c, k, :], WR[:, k, :],
                                                     start=(k == 0), stop=(k == KC - 1))
                            s_lg.done(last)
                    tb, u = unit(b, n - 1)
                    if exists(tb):
                        h, c, vp = u // TC, u % TC, (par + (n - 1) // UNITS) % 2
                        if c == 0:
                            s_x.wait(pe, tb, 4 * (h - 2) + 3)
                            s_vlo.wait(pe, tb, 0)
                        s_exp.wait(pe, tb, 2 * u)
                        bank = pv_bank(h)
                        pe.matmul(bank, V1[:, vp, c, :], PH[:, u % 4, :], start=(c == 0), stop=False)
                        pe.matmul(bank, V2[:, vp, c, :], PH[:, u % 4, :], start=False, stop=False)
                        s_plo.wait(pe, tb, u)
                        s_pv.done(pe.matmul(bank, V1[:, vp, c, :], PL[:, u % 4, :], start=False, stop=(c == TC - 1)))

            batches(pe, body)


def route(nc, ap, m, sem, sb):
    PS, IDENT, LOGITS = m["PS"], m["IDENT"], m["LOGITS"]
    NS = NCH // TC
    BIG = 127 * P
    SLOTC = E * CAP // P
    NDIG = 15
    RING = 8
    STEPS = 2 * NCH // RING
    EQ, OH1, OH2, L2 = (sb(x, [P, NCH, E]) for x in ("EQ", "OH1", "OH2", "L2"))
    KEY = sb("KEY", [P, TC, NS, E])
    M1, M2, I1, I2, EX, W1, W2, DEN = (sb(x, [P, NCH]) for x in ("M1", "M2", "I1", "I2", "EX", "W1", "W2", "DENr"))
    RANK8 = sb("RANK8", [P, E])
    KT, JUNK, GT, EQT, SEL, SCAN, DST, ZT = (sb(x, [P, T]) for x in ("KT", "JUNK", "GT", "EQT", "SEL", "SCAN", "DST", "ZT"))
    DIFF, DIFM = sb("DIFF", [P, P], I32), sb("DIFM", [P, P], I32)
    SAME, LOWER, ONES = sb("SAME", [P, P]), sb("LOWER", [P, P]), sb("ONES", [P, P])
    DIGU, DIGF = sb("DIGU", [P, NDIG + 1, 4], U32), sb("DIGF", [P, NDIG])
    CAND, CNTS = sb("CAND", [P, 2, 4], U32), sb("CNTS", [P, 4])
    PASS, DIG = sb("PASS", [P, 3]), sb("DIG", [P, 1], U32)
    CNT = sb("CNT", [P, 8])
    ECOLI, ECOL = sb("ECOLI", [P, 1], I32), sb("ECOL", [P, 1])
    D1, D12 = sb("D1", [P, NCH]), sb("D12", [P, 2, NCH])
    DI, AI, BI = (sb(x, [P, 2 * NCH], U32) for x in ("DI", "AI", "BI"))
    AF, BF = sb("AF", [P, 2 * NCH]), sb("BF", [P, 2 * NCH])
    TOK1, IOT = sb("TOK1", [P, 2, NCH]), sb("IOT", [P, P])
    OB, OE, OA = sb("OB", [P, 2, RING, P]), sb("OE", [P, 2, RING, SLOTC]), sb("OA", [P, 2, RING, SLOTC])
    ZP = sb("ZP", [P, P])
    SPARE, LF = sb("SPARE", [P, 1]), sb("LF", [P, SLOTC])
    NBR, NBD = sb("NBR", [1, 6, E]), sb("NBD", [P, E])
    ktab = m["ktab_dram"]
    s_pool, s_dve, s_exp, s_key, s_tab = (sem(x) for x in ("s_rpool", "s_rdve", "s_rexp", "s_rkey", "s_rtab"))
    s_kt, s_sum, s_cnt, s_tot, s_dt = (sem(x) for x in ("s_rkt", "s_rsum", "s_rcnt", "s_rtot", "s_rdt"))
    s_ob, s_oa, s_mm, s_list, s_nb, s_dd = (sem(x) for x in ("s_rob", "s_roa", "s_rmm", "s_rlist", "s_rnb", "s_rdd"))
    s_db, s_ab, s_oe = sem("s_rdb"), sem("s_rab"), sem("s_roe")
    POOL_CONSTS, MASKS_DONE = 7 + 4 * NDIG + 5, 3
    kt_ps = PS[:, 0, :]
    cnt_ps, off_ps, tot_ps = PS[:, 1, 0:3], PS[:, 2, 0:1], PS[:, 3, 0:1]
    dt_ps = PS[:, 4, :]
    list_ps, nb_ps = PS[:, 5, 0:SLOTC], PS[:, 6, 0:E]

    def by_expert(x):
        return x.unsqueeze(2).broadcast_to([P, NCH, E])

    with nc.Block() as block:
        @block.gpsimd
        def _(pool):
            n = [0]

            def link(ins):
                ins.then_inc(s_pool, 1)
                n[0] += 1
                pool.wait_ge(s_pool, n[0])
            link(pool.iota(RANK8[:, :], pattern=[[-1, E]], base=E, channel_multiplier=0, allow_small_or_imprecise_dtypes=True))
            link(pool.iota(DIFF[:, :], pattern=[[1, P]], base=P, channel_multiplier=-1))
            link(pool.iota(ECOLI[:, :], pattern=[[0, 1]], base=0, channel_multiplier=1))
            link(pool.iota(IOT[:, :], pattern=[[1, P]], base=0, channel_multiplier=0, allow_small_or_imprecise_dtypes=True))
            link(pool.iota(SPARE[:, :], pattern=[[0, 1]], base=NT + 1, channel_multiplier=1, allow_small_or_imprecise_dtypes=True))
            for j in range(2):
                link(pool.iota(TOK1[:, j, :].rearrange("p (a b) -> p a b", a=TC), pattern=[[P, TC], [TC * P, NS]], base=1,
                               channel_multiplier=1, allow_small_or_imprecise_dtypes=True))
            for d in range(NDIG):
                for v in range(1, 4):
                    pool.memset(DIGU[:, d, v:v + 1], v << (2 * (NDIG - 1 - d))).then_inc(s_pool, 1)
                pool.memset(DIGF[:, d:d + 1], float(1 << (2 * (NDIG - 1 - d)))).then_inc(s_pool, 1)
            pool.memset(DIGU[:, :, 0], 0).then_inc(s_pool, 1)
            pool.memset(DIGU[:, NDIG, 1:], 0).then_inc(s_pool, 1)
            pool.memset(ZT[:, :], 0.0).then_inc(s_pool, 1)
            pool.memset(ZP[:, :], 0.0).then_inc(s_pool, 1)
            pool.memset(ONES[:, :], 1.0).then_inc(s_pool, 1)
            tok = TOK1[:, :, :].rearrange("p j n -> p (j n)")
            with pool.Fori(0, STEPS // 2) as i:
                for par in range(2):
                    j = i * 2 + par
                    pool.wait_ge(s_oe, j + 1)
                    pool.tensor_tensor(OA[:, par, :, :], OE[:, par, :, :],
                                       tok[:, bass.ds(j * RING, RING)].unsqueeze(2).broadcast_to([P, RING, SLOTC]),
                                       ALU.mult).then_inc(s_oa, 1)

        @block.scalar
        def _(act):
            act.wait_ge(s_dd, 1)
            act.activation(EX[:, :], DEN[:, :], ACT.Exp).then_inc(s_exp, 1)
            act.wait_ge(s_kt, 1)
            act.activation(KT[:, :], kt_ps, ACT.Copy).then_inc(s_exp, 1)

        @block.sync
        def _(sp):
            sp.wait_ge(s_key, TC)
            rows = ktab[0:NT, :].rearrange("(c q p) e -> q p c e", p=P, q=TC)
            for q in range(TC):
                sp.dma_start(rows[q], KEY[:, q, :, :]).then_inc(s_tab, 16)
            sp.wait_ge(s_pool, POOL_CONSTS)
            sp.dma_start(ktab[NT:NT + P, :], ZP[:, 0:E]).then_inc(s_tab, 16)
            sp.wait_ge(s_tab, 16 * (TC + 1))

        @block.tensor
        def _(pe):
            pe.wait_ge(s_key, TC)
            for q in range(TC):
                last = pe.transpose(kt_ps[:, q * P:(q + 1) * P], KEY[:, q, :, :].rearrange("p c e -> p (c e)"), IDENT[:, :])
            last.then_inc(s_kt, 1)
            pe.wait_ge(s_dve, MASKS_DONE)
            with pe.Fori(0, NDIG) as i:
                pe.wait_ge(s_cnt, i * 3 + 3)
                pe.matmul(cnt_ps, SAME[:, :], CNTS[:, 1:4], start=True, stop=True).then_inc(s_sum, 1)
            pe.wait_ge(s_tot, 1)
            pe.matmul(tot_ps, SAME[:, :], CNT[:, 1:2], start=True, stop=True)
            pe.matmul(off_ps, LOWER[:, :], CNT[:, 2:3], start=True, stop=True).then_inc(s_sum, 1)
            pe.wait_ge(s_tot, 2)
            pe.matmul(tot_ps, SAME[:, :], CNT[:, 3:4], start=True, stop=True)
            pe.matmul(off_ps, LOWER[:, :], CNT[:, 3:4], start=True, stop=True).then_inc(s_sum, 1)
            pe.wait_ge(s_tot, 3)
            for q in range(TC):
                last = pe.transpose(dt_ps[:, q * P:(q + 1) * P], DST[:, q * P:(q + 1) * P], IDENT[:, :])
            last.then_inc(s_dt, 1)
            pe.matmul(nb_ps, ONES[:, :], NBD[:, :], start=True, stop=True).then_inc(s_nb, 1)
            pe.wait_ge(s_pool, POOL_CONSTS)
            for par in range(2):
                pe.matmul(list_ps, ZP[:, :], ZP[:, 0:SLOTC], start=(par == 0), stop=False).then_inc(s_mm, 1)
            with pe.Fori(0, STEPS // 2) as i:
                for par in range(2):
                    pe.wait_ge(s_ob, i * 2 + (par + 1))
                    pe.wait_ge(s_oa, i * 2 + (par + 1))
                    for r in range(RING):
                        last = pe.matmul(list_ps, OB[:, par, r, :], OA[:, par, r, :], start=False, stop=False)
                    last.then_inc(s_mm, 1)
            pe.matmul(list_ps, ZP[:, :], ZP[:, 0:SLOTC], start=False, stop=True).then_inc(s_list, 1)

        @block.vector
        def _(dve):
            n = [0]

            def link(ins):
                ins.then_inc(s_dve, 1)
                n[0] += 1
                dve.wait_ge(s_dve, n[0])
            dve.wait_ge(s_pool, 7)
            link(dve.tensor_scalar(DIFM[:, :], DIFF[:, :], E - 1, None, ALU.bitwise_and))
            link(dve.tensor_scalar(SAME[:, :], DIFM[:, :], 0.0, None, ALU.is_equal))
            link(dve.scalar_tensor_tensor(out=LOWER[:, :], in0=DIFF[:, :], scalar=float(P), in1=SAME[:, :],
                                          op0=ALU.is_gt, op1=ALU.mult))
            rank8 = RANK8[:, :].unsqueeze(1).broadcast_to([P, NCH, E])
            link(dve.tensor_reduce(M1[:, :], LOGITS[:, :, :], AX.X, ALU.max))
            link(dve.tensor_tensor(EQ[:, :, :], LOGITS[:, :, :], by_expert(M1[:, :]), ALU.is_equal))
            link(dve.tensor_tensor(EQ[:, :, :], EQ[:, :, :], rank8, ALU.mult))
            link(dve.tensor_reduce(I1[:, :], EQ[:, :, :], AX.X, ALU.max))
            link(dve.tensor_tensor(OH1[:, :, :], rank8, by_expert(I1[:, :]), ALU.is_equal))
            link(dve.scalar_tensor_tensor(out=L2[:, :, :], in0=OH1[:, :, :], scalar=-3.0e38, in1=LOGITS[:, :, :],
                                          op0=ALU.mult, op1=ALU.add))
            link(dve.tensor_reduce(M2[:, :], L2[:, :, :], AX.X, ALU.max))
            link(dve.tensor_tensor(DEN[:, :], M2[:, :], M1[:, :], ALU.subtract))
            dve.sem_inc(s_dd, 1)
            link(dve.tensor_tensor(EQ[:, :, :], L2[:, :, :], by_expert(M2[:, :]), ALU.is_equal))
            link(dve.tensor_tensor(EQ[:, :, :], EQ[:, :, :], rank8, ALU.mult))
            link(dve.tensor_reduce(I2[:, :], EQ[:, :, :], AX.X, ALU.max))
            link(dve.tensor_tensor(OH2[:, :, :], rank8, by_expert(I2[:, :]), ALU.is_equal))
            dve.wait_ge(s_exp, 1)
            link(dve.tensor_scalar(DEN[:, :], EX[:, :], 1.0, None, ALU.add))
            link(dve.reciprocal(W1[:, :], DEN[:, :]))
            link(dve.tensor_tensor(W2[:, :], EX[:, :], W1[:, :], ALU.mult))
            link(dve.tensor_tensor(EQ[:, :, :], OH1[:, :, :], OH2[:, :, :], ALU.add))
            link(dve.tensor_tensor(OH1[:, :, :], OH1[:, :, :], by_expert(W1[:, :]), ALU.mult))
            link(dve.tensor_tensor(OH2[:, :, :], OH2[:, :, :], by_expert(W2[:, :]), ALU.mult))
            link(dve.tensor_tensor(OH1[:, :, :], OH1[:, :, :], OH2[:, :, :], ALU.add))
            for q in range(TC):
                dve.scalar_tensor_tensor(out=KEY[:, q, :, :], in0=EQ[:, q::TC, :], scalar=-1.0, in1=OH1[:, q::TC, :],
                                         op0=ALU.add, op1=ALU.add).then_inc(s_key, 1)
            dve.wait_ge(s_pool, POOL_CONSTS)
            dve.tensor_copy(CAND[:, 0, :].bitcast(F32), DIGU[:, 0, :].bitcast(F32)).then_inc(s_db, 1)
            dve.wait_ge(s_exp, 2)

            def digit(d, par):
                dve.wait_ge(s_db, d + 1)
                for v, junk in ((1, JUNK), (2, GT), (3, EQT)):
                    dve.tensor_scalar(junk[:, :], KT[:, :], CAND[:, par, v:v + 1].bitcast(F32), None, ALU.is_ge, ALU.add,
                                      accum_out=CNTS[:, v:v + 1]).then_inc(s_cnt, 1)
                dve.wait_ge(s_sum, d + 1)
                dve.tensor_scalar(PASS[:, :], cnt_ps, float(CAP), DIGF[:, bass.ds(d, 1)], ALU.is_ge, ALU.mult).then_inc(s_ab, 1)
                dve.wait_ge(s_ab, d * 2 + 1)
                dve.scalar_tensor_tensor(out=DIG[:, :], in0=PASS[:, 0:1], scalar=PASS[:, 1:2], in1=PASS[:, 2:3],
                                         op0=ALU.add, op1=ALU.add).then_inc(s_ab, 1)
                dve.wait_ge(s_ab, d * 2 + 2)
                dve.scalar_tensor_tensor(out=CAND[:, 1 - par, :], in0=DIGU[:, bass.ds(d + 1, 1), :].rearrange("p a v -> p (a v)"),
                                         scalar=DIG[:, :], in1=CAND[:, par, 0:1].broadcast_to([P, 4]), op0=ALU.bitwise_or,
                                         op1=ALU.bitwise_or).then_inc(s_db, 1)

            with dve.Fori(0, NDIG // 2) as i:
                for par in range(2):
                    digit(i * 2 + par, par)
            digit(NDIG - 1, 0)
            dve.wait_ge(s_db, NDIG + 1)
            thr = CAND[:, 1, 0:1].bitcast(F32)
            link(dve.tensor_scalar(GT[:, :], KT[:, :], thr, None, ALU.is_gt, ALU.add, accum_out=CNT[:, 1:2]))
            link(dve.tensor_scalar(EQT[:, :], KT[:, :], thr, None, ALU.is_equal, ALU.add, accum_out=CNT[:, 2:3]))
            dve.sem_inc(s_tot, 1)
            link(dve.tensor_tensor_scan(SCAN[:, :], EQT[:, :], ZT[:, :], 0.0, ALU.add, ALU.add))
            link(dve.tensor_scalar(ECOLI[:, :], ECOLI[:, :], E - 1, None, ALU.bitwise_and))
            link(dve.tensor_scalar(ECOL[:, :], ECOLI[:, :], float(CAP), float(-1 - BIG), ALU.mult, ALU.add))
            dve.wait_ge(s_sum, NDIG + 1)
            link(dve.tensor_scalar(CNT[:, 4:5], tot_ps, -1.0, float(CAP), ALU.mult, ALU.add))
            link(dve.tensor_tensor(CNT[:, 4:5], CNT[:, 4:5], off_ps, ALU.subtract))
            link(dve.scalar_tensor_tensor(out=SEL[:, :], in0=SCAN[:, :], scalar=CNT[:, 4:5], in1=EQT[:, :],
                                          op0=ALU.is_le, op1=ALU.mult))
            link(dve.tensor_tensor(SEL[:, :], SEL[:, :], GT[:, :], ALU.add))
            link(dve.tensor_reduce(CNT[:, 3:4], SEL[:, :], AX.X, ALU.add))
            dve.sem_inc(s_tot, 1)
            link(dve.tensor_tensor_scan(SCAN[:, :], SEL[:, :], ZT[:, :], 0.0, ALU.add, ALU.add))
            dve.wait_ge(s_sum, NDIG + 2)
            link(dve.tensor_tensor(CNT[:, 5:6], ECOL[:, :], off_ps, ALU.add))
            link(dve.scalar_tensor_tensor(out=DST[:, :], in0=SCAN[:, :], scalar=CNT[:, 5:6], in1=SEL[:, :],
                                          op0=ALU.add, op1=ALU.mult))
            link(dve.tensor_scalar(CNT[:, 6:7], tot_ps, 0.0, None, ALU.is_gt))
            for j in range(1, -(-CAP // BLK)):
                link(dve.scalar_tensor_tensor(out=CNT[:, 6:7], in0=tot_ps, scalar=float(j * BLK), in1=CNT[:, 6:7],
                                              op0=ALU.is_gt, op1=ALU.add))
            link(dve.tensor_scalar(NBD[:, :], IDENT[:, 0:E], CNT[:, 6:7], None, ALU.mult))
            dve.sem_inc(s_tot, 1)
            dve.wait_ge(s_nb, 1)
            nb, act_, cum, cua, z = (NBR[:, j, :] for j in range(5))
            link(dve.tensor_copy(nb, nb_ps[0:1, :]))
            link(dve.tensor_scalar(act_, nb, 0.0, None, ALU.is_gt))
            link(dve.memset(z, 0.0))
            link(dve.tensor_tensor_scan(cum, nb, z, 0.0, ALU.add, ALU.add))
            link(dve.tensor_tensor_scan(cua, act_, z, 0.0, ALU.add, ALU.add))
            link(dve.tensor_tensor(cum, cum, nb, ALU.subtract))
            link(dve.tensor_tensor(cua, cua, act_, ALU.subtract))
            for j, row in enumerate((nb, cum, cua)):
                link(dve.tensor_copy(m["INFO"][:, j * E:(j + 1) * E], row))
            dve.wait_ge(s_dt, 1)
            by_tok = dt_ps.rearrange("p (n e) -> p n e", e=E)
            link(dve.tensor_reduce(D12[:, 0, :], by_tok, AX.X, ALU.min))
            link(dve.tensor_tensor(EQ[:, :, :], by_tok, by_expert(D12[:, 0, :]), ALU.is_equal))
            link(dve.scalar_tensor_tensor(out=EQ[:, :, :], in0=EQ[:, :, :], scalar=float(BIG), in1=by_tok,
                                          op0=ALU.mult, op1=ALU.add))
            link(dve.tensor_reduce(D12[:, 1, :], EQ[:, :, :], AX.X, ALU.min))
            link(dve.tensor_scalar(DI[:, :], D12[:, :, :].rearrange("p j n -> p (j n)"), float(BIG), None, ALU.add))
            link(dve.tensor_scalar(AI[:, :], DI[:, :], 7, None, ALU.logical_shift_right))
            link(dve.tensor_scalar(BI[:, :], DI[:, :], P - 1, None, ALU.bitwise_and))
            link(dve.tensor_copy(BF[:, :], BI[:, :]))
            link(dve.tensor_copy(AF[:, :], AI[:, :]))
            dve.sem_inc(s_dd, 1)
            with dve.Fori(0, STEPS // 2) as i:
                for par in range(2):
                    j = i * 2 + par
                    dve.wait_ge(s_mm, j + 1)
                    dve.tensor_tensor(OE[:, par, :, :], IOT[:, 0:SLOTC].unsqueeze(1).broadcast_to([P, RING, SLOTC]),
                                      AF[:, bass.ds(j * RING, RING)].unsqueeze(2).broadcast_to([P, RING, SLOTC]),
                                      ALU.is_equal).then_inc(s_oe, 1)
                    dve.tensor_tensor(OB[:, par, :, :], IOT[:, :].unsqueeze(1).broadcast_to([P, RING, P]),
                                      BF[:, bass.ds(j * RING, RING)].unsqueeze(2).broadcast_to([P, RING, P]),
                                      ALU.is_equal).then_inc(s_ob, 1)
            dve.wait_ge(s_list, 1)
            link(dve.tensor_scalar(LF[:, :], list_ps, 0.0, SPARE[:, :], ALU.is_equal, ALU.mult))
            link(dve.scalar_tensor_tensor(out=m["IDX"][:, :], in0=list_ps, scalar=-1.0, in1=LF[:, :], op0=ALU.add, op1=ALU.add))




def experts(nc, ap, m, sem, sb):
    PS, IDENT, IDX, INFO = m["PS"], m["IDENT"], m["IDX"], m["INFO"]
    FC, BT = F // P, BLK // P
    MAXB = CAP // BLK
    GATES_USED = 4 + BT
    assert CAP % BLK == 0
    W1F, W2F = sb("W1F", [P, KC, F]), sb("W2F", [P, FC, D])
    W1H, W1L = sb("W1H", [P, KC, F], F32R), sb("W1L", [P, KC, F], F32R)
    W2H, W2L = sb("W2H", [P, FC, D], F32R), sb("W2L", [P, FC, D], F32R)
    B1R, B1, B2 = sb("B1R", [E * FC, P]), sb("B1", [P, E * FC]), sb("B2", [P, E, D])
    XG, GK, TOKG, TOKS = sb("XG", [P, BT, D]), sb("GK", [P, BT, E]), sb("TOKG", [P, BT], U32), sb("TOKS", [P, BT], U32)
    XTH, XTL = sb("XTH", [P, KC, BLK], F32R), sb("XTL", [P, KC, BLK], F32R)
    HF, HH, HL = sb("HF", [P, 4, BLK]), sb("HH", [P, 4, BLK], F32R), sb("HL", [P, 4, BLK], F32R)
    YB, YS, GATES, GATE = sb("YB", [P, BT, D]), sb("YS", [P, BT, D]), sb("GATES", [P, BT]), sb("GATEp", [P, GATES_USED + 1])

    streams = []

    def S(name, per, step=1, base=1):
        streams.append(Stream(sem(name), per, step, base))
        return streams[-1]
    s_w1, s_w2 = S("fw1", 1, 16), S("fw2", 1, 16)
    s_w1h, s_w2h, s_w1l, s_w2l = S("fw1h", 1), S("fw2h", 1), S("fw1l", 1), S("fw2l", 1)
    s_gx, s_gk, s_sc = S("fgx", 1, 16 * BT, 0), S("fgk", 1, 16 * BT, 0), S("fsc", BT, 16, 0)
    s_tokg, s_toks = S("ftokg", BT), S("ftoks", 1)
    s_t, s_m1, s_m2, s_gate, s_yb = S("ft", 1), S("fm1", FC), S("fm2", FC), S("fgate", BT), S("fyb", BT)
    s_xh, s_xl, s_gelu, s_hh, s_hl, s_y = S("fxh", KC), S("fxl", KC), S("fgelu", FC), S("fhh", FC), S("fhl", FC), S("fy", BT)
    s_init, s_b, s_b1t, s_b1 = sem("finit"), sem("fb"), sem("fb1t"), sem("fb1")
    xt_bank = PS[:, 0, :]
    xt = xt_bank.rearrange("p (k n) -> p k n", k=KC)

    def h_bank(f):
        return PS[:, 1 + f % 4, 0:BLK]

    def y_bank(t):
        return PS[:, 5 + t, 0:D]

    def each(eng, expert, block):
        with eng.Fori(0, E) as e:
            nb = eng.value_load(INFO[0:1, bass.ds(e, 1)], min_val=0, max_val=MAXB)
            g0 = eng.value_load(INFO[0:1, bass.ds(e + E, 1)], min_val=0, max_val=E * MAXB)
            a = eng.value_load(INFO[0:1, bass.ds(e + 2 * E, 1)], min_val=0, max_val=E)
            with eng.If(nb > 0):
                if expert is not None:
                    expert(e, a, g0)
                if block is not None:
                    with eng.Fori(0, nb) as k:
                        block(e, a, g0 + k, k)

    with nc.Block() as blk:
        @blk.sync
        def _(sp):
            w1 = ap["L0_ffn_W1"].rearrange("e (k p) f -> p (e k) f", p=P)
            w2 = ap["L0_ffn_W2"].rearrange("e (f p) n -> p (e f) n", p=P)
            sp.dma_start(B1R[:, :], ap["L0_ffn_b1"].rearrange("e (f p) -> (e f) p", p=P)).then_inc(s_b, 16)
            sp.dma_start(B2[:, :, :], ap["L0_ffn_b2"].partition_broadcast(P)).then_inc(s_b, 16)

            def expert(e, a, g):
                k_row, f_row = sp.snap(e * KC), sp.snap(e * FC)
                s_w1l.wait(sp, a, -1)
                s_w1.done(sp.dma_start(W1F[:, :, :], w1[:, bass.ds(k_row, KC), :]))
                s_w2l.wait(sp, a, -1)
                s_w2.done(sp.dma_start(W2F[:, :, :], w2[:, bass.ds(f_row, FC), :]))
            each(sp, expert, None)

        @blk.gpsimd
        def _(pool):
            start(pool, streams)
            pool.iota(TOKS[:, :].bitcast(I32), pattern=[[0, BT]], base=NT, channel_multiplier=1).then_inc(s_init, 1)
            pool.memset(YS[:, :, :], 0.0).then_inc(s_init, 1)
            pool.memset(GATE[:, :], 0.0).then_inc(s_init, 1)
            pool.wait_ge(s_init, 3)

            def gate(j):
                pool.tensor_tensor(GATE[:, j:j + 1], GATE[:, GATES_USED:], GATE[:, GATES_USED:], ALU.add)

            def scatter(g):
                s_y.wait(pool, g, -1)
                for t in range(BT):
                    if t:
                        s_sc.wait(pool, g, t - 1)
                    gate(4 + t)
                    off = bass.IndirectOffsetOnAxis(ap=TOKS[:, t:t + 1], axis=0)
                    s_sc.done(pool.indirect_dma_start(out=m["acc_dram"], out_offset=off, in_=YS[:, t, :], in_offset=None,
                                                      compute_op=ALU.add))

            def block(e, a, g, k):
                s_toks.wait(pool, g, -1)
                gate(0)
                for t in range(BT):
                    s_tokg.done(pool.tensor_copy(TOKG[:, t:t + 1], IDX[:, bass.ds(e * (CAP // P) + k * BT + t, 1)]))
                s_tokg.wait(pool, g, BT - 1)
                s_t.wait(pool, g, -1)
                gate(1)
                for t in range(BT):
                    off = bass.IndirectOffsetOnAxis(ap=TOKG[:, t:t + 1], axis=0)
                    pool.indirect_dma_start(out=XG[:, t, :], out_offset=None, in_=m["h2_dram"], in_offset=off).then_inc(s_gx.sem, 16)
                s_gate.wait(pool, g, -1)
                gate(2)
                for t in range(BT):
                    off = bass.IndirectOffsetOnAxis(ap=TOKG[:, t:t + 1], axis=0)
                    pool.indirect_dma_start(out=GK[:, t, :], out_offset=None, in_=m["ktab_dram"], in_offset=off).then_inc(s_gk.sem, 16)
                scatter(g)
                s_sc.wait(pool, g, BT - 1)
                gate(3)
                s_toks.done(pool.tensor_copy(TOKS[:, :], TOKG[:, :]))
            each(pool, None, block)
            total = (pool.value_load(INFO[0:1, E - 1:E], min_val=0, max_val=MAXB)
                     + pool.value_load(INFO[0:1, 2 * E - 1:2 * E], min_val=0, max_val=E * MAXB))
            s_toks.wait(pool, total, -1)
            scatter(total)
            s_sc.wait(pool, total, BT - 1)

        @blk.scalar
        def _(act):
            def expert(e, a, g):
                s_w1.wait(act, a, 0)
                s_m2.wait(act, g, -1)
                s_w1h.done(act.activation(W1H[:, :, :], W1F[:, :, :], ACT.Copy))
                s_w2.wait(act, a, 0)
                s_w2h.done(act.activation(W2H[:, :, :], W2F[:, :, :], ACT.Copy))

            def block(e, a, g, k):
                for f in range(FC):
                    s_m1.wait(act, g, f)
                    s_hl.wait(act, g, max(f - 4, -1))
                    s_gelu.done(act.activation(HF[:, f % 4, :], h_bank(f), ACT.Gelu, bias=B1[:, bass.ds(e * FC + f, 1)]))
            act.wait_ge(s_b1t, 1)
            act.activation(B1[:, :], xt_bank[:, 0:E * FC], ACT.Copy).then_inc(s_b1, 1)
            act.wait_ge(s_b1, 1)
            each(act, expert, block)

        @blk.vector
        def _(dve):
            def expert(e, a, g):
                s_w1h.wait(dve, a, 0)
                s_w1l.done(dve.tensor_tensor(W1L[:, :, :], W1F[:, :, :], W1H[:, :, :].bitcast(F32), ALU.subtract))
                s_w2h.wait(dve, a, 0)
                s_w2l.done(dve.tensor_tensor(W2L[:, :, :], W2F[:, :, :], W2H[:, :, :].bitcast(F32), ALU.subtract))

            def block(e, a, g, k):
                s_t.wait(dve, g, 0)
                s_m1.wait(dve, g, -1)
                for c in range(KC):
                    s_xh.done(dve.tensor_copy(XTH[:, c, :], xt[:, c, :]))
                for c in range(KC):
                    s_xh.wait(dve, g, c)
                    s_xl.done(dve.tensor_tensor(XTL[:, c, :], xt[:, c, :], XTH[:, c, :].bitcast(F32), ALU.subtract))
                s_gk.wait(dve, g, 0)
                s_y.wait(dve, g, -1)
                for t in range(BT):
                    s_gate.done(dve.tensor_copy(GATES[:, t:t + 1], GK[:, t, bass.ds(e, 1)]))
                b2 = B2[:, bass.ds(e, 1), :].rearrange("p a n -> p (a n)")
                s_gate.wait(dve, g, BT - 1)
                for t in range(BT):
                    s_yb.done(dve.tensor_scalar(YB[:, t, :], b2, GATES[:, t:t + 1], None, ALU.mult))
                for f in range(FC):
                    s_gelu.wait(dve, g, f)
                    s_m2.wait(dve, g, max(f - 4, -1))
                    s_hh.done(dve.tensor_copy(HH[:, f % 4, :], HF[:, f % 4, :]))
                    s_hh.wait(dve, g, f)
                    s_hl.done(dve.tensor_tensor(HL[:, f % 4, :], HF[:, f % 4, :], HH[:, f % 4, :].bitcast(F32), ALU.subtract))
                s_sc.wait(dve, g, BT - 1)
                s_m2.wait(dve, g, FC - 1)
                s_yb.wait(dve, g, BT - 1)
                for t in range(BT):
                    s_y.done(dve.scalar_tensor_tensor(out=YS[:, t, :], in0=y_bank(t), scalar=GATES[:, t:t + 1], in1=YB[:, t, :],
                                                      op0=ALU.mult, op1=ALU.add))
            dve.wait_ge(s_b, 32)
            each(dve, expert, block)

        @blk.tensor
        def _(pe):
            def block(e, a, g, k):
                s_gx.wait(pe, g, 0)
                s_xl.wait(pe, g, -1)
                for c in range(KC):
                    for t in range(BT):
                        last = pe.transpose(xt_bank[:, c * BLK + t * P:c * BLK + (t + 1) * P], XG[:, t, c * P:(c + 1) * P], IDENT[:, :])
                s_t.done(last)
                s_w1l.wait(pe, a, 0)

                def mm1(f):
                    s_gelu.wait(pe, g, max(f - 4, -1))
                    cols = slice(f * P, (f + 1) * P)
                    for c in range(KC):
                        if f == 0:
                            s_xl.wait(pe, g, c)
                        last = hi_lo_matmul(pe, h_bank(f), (W1H[:, c, cols], W1L[:, c, cols]),
                                            (XTH[:, c, :], XTL[:, c, :]), c == 0, c == KC - 1)
                    s_m1.done(last)

                def mm2(f):
                    if f == 0:
                        s_w2l.wait(pe, a, 0)
                        s_y.wait(pe, g, -1)
                    s_hl.wait(pe, g, f)
                    for t in range(BT):
                        rows = slice(t * P, (t + 1) * P)
                        last = hi_lo_matmul(pe, y_bank(t), (HH[:, f % 4, rows], HL[:, f % 4, rows]),
                                            (W2H[:, f, :], W2L[:, f, :]), f == 0, f == FC - 1)
                    s_m2.done(last)
                for f in range(FC + 2):
                    if f < FC:
                        mm1(f)
                    if f >= 2:
                        mm2(f - 2)
            pe.wait_ge(s_b, 32)
            pe.transpose(xt_bank[:, 0:E * FC], B1R[:, :], IDENT[0:E * FC, 0:E * FC]).then_inc(s_b1t, 1)
            pe.wait_ge(s_b1, 1)
            each(pe, None, block)


def last_norm(nc, out, m, sem, sb):
    X1 = m["X1"]
    GB = 4
    GC, GROUPS = GB * TC, NB // GB
    A, GBG = sb("A", [P, NCH, D]), sb("GBG", [P, NB, D])
    S6, MV = sb("S6", [P, 2, GC, 6]), sb("MV", [P, 2, GC, 2])
    VAR, Y, TMP, NMR = (sb(x, [P, 2, GC]) for x in ("VAR", "Yr", "TMP", "NMR"))
    GATE = sb("GATEt", [P, 2 * (GB + 1)])
    OPS = 2 * GC + 1 + GB + RSQRT_OPS

    def S(name, per, step=1, base=1):
        return Stream(sem(name), per, step, base)
    s_in = [[S(f"tin{par}{q}", 1, 16) for q in range(GB)] for par in range(2)]
    s_n, s_xn, s_mul, s_add = ([S(f"{x}{par}", per) for par in range(2)] for x, per in (
        ("tn", OPS), ("txn", GC), ("tmul", GB), ("tadd", GB)))
    s_gbg, s_out = sem("tgbg"), sem("tout")
    acc_rows = m["acc_dram"][0:NT, :].rearrange("(c p) n -> p c n", p=P)
    out_rows = out.rearrange("b (c p) n -> p (b c) n", p=P)

    def chunk(i, par, c):
        return A[:, bass.ds((i * 2 + par) * GC + c, 1), :].rearrange("p c n -> p (c n)")

    with nc.Block() as block:
        @block.sync
        def _(sp):
            start(sp, s_in[0] + s_in[1])
            with sp.Fori(0, GROUPS // 2) as i:
                for par in range(2):
                    for q in range(GB):
                        row = sp.snap((i * 2 + par) * GC + q * TC)
                        s_n[par].wait(sp, i, -1)
                        s_in[par][q].done(sp.dma_start(A[:, bass.ds(row, TC), :], acc_rows[:, bass.ds(row, TC), :]))
            with sp.Fori(0, GROUPS // 2) as i:
                for par in range(2):
                    for q in range(GB):
                        row = sp.snap((i * 2 + par) * GC + q * TC)
                        s_add[par].wait(sp, i, q)
                        sp.dma_start(out_rows[:, bass.ds(row, TC), :], X1[:, bass.ds(row, TC), :]).then_inc(s_out, 16)
            sp.wait_ge(s_out, 16 * NB)

        @block.vector
        def _(dve):
            def stats(i, par):
                st, k = s_n[par], 0
                s_xn[par].wait(dve, i, -1)
                for q in range(GB):
                    s_in[par][q].wait(dve, i, 0)
                    st.done(dve.memset(GATE[:, par * GB + q:par * GB + q + 1], 0.0))
                    for c in range(q * TC, (q + 1) * TC):
                        st.done(dve.bn_stats(S6[:, par, c, :], chunk(i, par, c)))
                    k += TC + 1
                st.wait(dve, i, k - 1)
                st.done(dve.memset(GATE[:, 2 * GB + par:2 * GB + par + 1], 0.0))
                for c in range(GC):
                    st.done(dve.bn_aggr(MV[:, par, c, :], S6[:, par, c, :]))
                k += GC + 1
                for issue in rsqrt_and_shift(dve, MV[:, par, :, :], VAR[:, par, :], Y[:, par, :], TMP[:, par, :], NMR[:, par, :]):
                    st.wait(dve, i, k - 1)
                    st.done(issue())
                    k += 1
                assert k == OPS

            def scale(i, par):
                dve.wait_ge(s_gbg, 16)
                for q in range(GB):
                    s_xn[par].wait(dve, i, (q + 1) * TC - 1)
                    a = A[:, bass.ds((i * 2 + par) * GC + q * TC, TC), :]
                    g = GBG[:, bass.ds((i * 2 + par) * GB + q, 1), :].broadcast_to([P, TC, D])
                    s_mul[par].done(dve.tensor_tensor(a, a, g, ALU.mult))

            start(dve, s_n + s_mul)
            stats(0, 0)
            with dve.Fori(0, GROUPS // 2 - 1) as i:
                stats(i, 1)
                scale(i, 0)
                stats(i + 1, 0)
                scale(i, 1)
            stats(GROUPS // 2 - 1, 1)
            scale(GROUPS // 2 - 1, 0)
            scale(GROUPS // 2 - 1, 1)

        @block.scalar
        def _(act):
            start(act, s_xn)
            s_in[1][GB - 1].wait(act, 0, 0)
            act.dma_start(GBG[:, :, :], m["mod_dram"][:, 4, :].partition_broadcast(P)).then_inc(s_gbg, 16)
            with act.Fori(0, GROUPS // 2) as i:
                for par in range(2):
                    s_n[par].wait(act, i, OPS - 1)
                    for c in range(GC):
                        s_xn[par].done(act.activation(chunk(i, par, c), chunk(i, par, c), ACT.Identity, scale=Y[:, par, c:c + 1],
                                                      bias=NMR[:, par, c:c + 1]))

        @block.gpsimd
        def _(pool):
            start(pool, s_add)
            with pool.Fori(0, GROUPS // 2) as i:
                for par in range(2):
                    for q in range(GB):
                        row = pool.snap((i * 2 + par) * GC + q * TC)
                        s_mul[par].wait(pool, i, q)
                        x = X1[:, bass.ds(row, TC), :]
                        s_add[par].done(pool.tensor_tensor(x, x, A[:, bass.ds(row, TC), :], ALU.add))


def kernel(**inputs):
    import numpy as np
    import concourse.bacc as bacc
    from concourse.bass_utils import run_bass_kernel_spmd as run

    nc = bacc.Bacc("TRN2", target_bir_lowering=False, num_devices=1)
    arrays, aps = {}, {}
    for name, value in inputs.items():
        arrays[f"in_{name}"] = np.ascontiguousarray(value)
        aps[name] = nc.dram_tensor(f"in_{name}", arrays[f"in_{name}"].shape, mybir.dt.from_np(arrays[f"in_{name}"].dtype),
                                   kind="ExternalInput").ap()
    out = nc.dram_tensor("out_x", (NB, T, D), F32, kind="ExternalOutput").ap()
    build_program(nc, aps, out)
    return run(nc, [arrays], core_ids=[0]).results[0]["out_x"]
```
